# Optimizing a Trainium2 kernel written in Bass

```python
import numpy as np
import jax
import jax.numpy as jnp

def _softmax(x, axis=-1):
    return jax.nn.softmax(x, axis=axis)

def _gelu(x):
    return jax.nn.gelu(x, approximate=True)

def _silu(x):
    return jax.nn.silu(x)

def _sigmoid(x):
    return jax.nn.sigmoid(x)

def _layernorm(x, axis=-1, eps=1e-05):
    m = jnp.mean(x, axis=axis, keepdims=True)
    v = jnp.var(x, axis=axis, keepdims=True)
    return (x - m) / jnp.sqrt(v + eps)

def _scatter_add(tgt, idx, src, axis=0):
    return tgt.at[idx].add(src)

def _segment_sum(src, seg, n):
    return jax.ops.segment_sum(src, seg, n)
kernel_name = 'mk_prb_d1_jaxref_r4_aecf13'

def setup_inputs(seed: int=0):
    np.random.seed(seed)
    _w = jnp.asarray

    def _L0_attn_setup():
        import jax, jax.numpy as jnp
        import numpy as np
        import math
        B, L, D = (2, 512, 256)
        H, KV, HD = (16, 4, 64)
        GROUPS = H // KV
        ROPE_BASE = 10000.0

        def _alibi_slopes(n_heads):

            def pow2(n):
                start = 2.0 ** (-2.0 ** (-(math.log2(n) - 3)))
                return [start * start ** i for i in range(n)]
            if math.log2(n_heads).is_integer():
                return pow2(n_heads)
            c = 2 ** math.floor(math.log2(n_heads))
            return pow2(c) + _alibi_slopes(2 * c)[0::2][:n_heads - c]

        def _rope_cos_sin(seq_len, dim, dtype):
            inv_freq = 1.0 / ROPE_BASE ** (jnp.arange(0, dim, 2, dtype=jnp.float32) / dim)
            t = jnp.arange(seq_len, dtype=jnp.float32)
            freqs = t[:, None] * inv_freq[None, :]
            emb = jnp.concatenate([freqs, freqs], axis=-1)
            return (jnp.cos(emb).astype(dtype), jnp.sin(emb).astype(dtype))

        def _rotate_half(x):
            x1, x2 = (x[..., :x.shape[-1] // 2], x[..., x.shape[-1] // 2:])
            return jnp.concatenate([-x2, x1], axis=-1)
        key = jax.random.key(seed)
        ks = jax.random.split(key, 5)
        s = 0.02
        return {'x': jax.random.normal(ks[0], (B, L, D), jnp.float32), 'Wq': jax.random.normal(ks[1], (D, H * HD), jnp.float32) * s, 'Wk': jax.random.normal(ks[2], (D, KV * HD), jnp.float32) * s, 'Wv': jax.random.normal(ks[3], (D, KV * HD), jnp.float32) * s, 'Wo': jax.random.normal(ks[4], (H * HD, D), jnp.float32) * s}
    _L0_attn_in = _L0_attn_setup()

    def _L0_ffn_setup():
        import jax, jax.numpy as jnp
        import numpy as np
        D_MODEL = 256
        N_HEAD = 16
        HEAD_DIM = D_MODEL // N_HEAD
        D_FF = 1024
        N_EXPERTS = 4
        EPS = 1e-05

        def _layer_norm(x, gamma, beta):
            mu = jnp.mean(x, axis=-1, keepdims=True)
            var = jnp.mean((x - mu) ** 2, axis=-1, keepdims=True)
            return (x - mu) / jnp.sqrt(var + EPS) * gamma + beta
        key = jax.random.key(seed)
        ks = jax.random.split(key, 20)
        f32 = jnp.float32
        sc = 1.0 / np.sqrt(D_MODEL)
        scf = 1.0 / np.sqrt(D_FF)
        return {'src': jax.random.normal(ks[0], (4, 128, D_MODEL), f32), 'Wq': jax.random.normal(ks[1], (D_MODEL, D_MODEL), f32) * sc, 'bq': jnp.zeros((D_MODEL,), f32), 'Wk': jax.random.normal(ks[2], (D_MODEL, D_MODEL), f32) * sc, 'bk': jnp.zeros((D_MODEL,), f32), 'Wv': jax.random.normal(ks[3], (D_MODEL, D_MODEL), f32) * sc, 'bv': jnp.zeros((D_MODEL,), f32), 'Wo': jax.random.normal(ks[4], (D_MODEL, D_MODEL), f32) * sc, 'bo': jnp.zeros((D_MODEL,), f32), 'router_w': jax.random.normal(ks[5], (D_MODEL, 1), f32) * 0.05, 'router_b': jnp.zeros((1,), f32), 'W1': jax.random.normal(ks[6], (N_EXPERTS, D_MODEL, D_FF), f32) * sc, 'b1': jnp.zeros((N_EXPERTS, D_FF), f32), 'W2': jax.random.normal(ks[7], (N_EXPERTS, D_FF, D_MODEL), f32) * scf, 'b2': jnp.zeros((N_EXPERTS, D_MODEL), f32), 'ln1_g': jnp.ones((D_MODEL,), f32), 'ln1_b': jnp.zeros((D_MODEL,), f32), 'ln2_g': jnp.ones((D_MODEL,), f32), 'ln2_b': jnp.zeros((D_MODEL,), f32)}
    _L0_ffn_in = _L0_ffn_setup()
    _d = {'L0_attn_x': _L0_attn_in['x'], 'L0_attn_Wq': _L0_attn_in['Wq'], 'L0_attn_Wk': _L0_attn_in['Wk'], 'L0_attn_Wv': _L0_attn_in['Wv'], 'L0_attn_Wo': _L0_attn_in['Wo'], 'L0_ffn_Wq': _L0_ffn_in['Wq'], 'L0_ffn_bq': _L0_ffn_in['bq'], 'L0_ffn_Wk': _L0_ffn_in['Wk'], 'L0_ffn_bk': _L0_ffn_in['bk'], 'L0_ffn_Wv': _L0_ffn_in['Wv'], 'L0_ffn_bv': _L0_ffn_in['bv'], 'L0_ffn_Wo': _L0_ffn_in['Wo'], 'L0_ffn_bo': _L0_ffn_in['bo'], 'L0_ffn_router_w': _L0_ffn_in['router_w'], 'L0_ffn_router_b': _L0_ffn_in['router_b'], 'L0_ffn_W1': _L0_ffn_in['W1'], 'L0_ffn_b1': _L0_ffn_in['b1'], 'L0_ffn_W2': _L0_ffn_in['W2'], 'L0_ffn_b2': _L0_ffn_in['b2'], 'L0_ffn_ln1_g': _L0_ffn_in['ln1_g'], 'L0_ffn_ln1_b': _L0_ffn_in['ln1_b'], 'L0_ffn_ln2_g': _L0_ffn_in['ln2_g'], 'L0_ffn_ln2_b': _L0_ffn_in['ln2_b']}
    _x0 = _d['L0_attn_x']
    _d['L0_attn_x'] = jax.random.normal(jax.random.fold_in(jax.random.key(seed), 1), (8, 512, 256), dtype=_x0.dtype)
    del _x0
    return _d

def reference(L0_attn_x, L0_attn_Wq, L0_attn_Wk, L0_attn_Wv, L0_attn_Wo, L0_ffn_Wq, L0_ffn_bq, L0_ffn_Wk, L0_ffn_bk, L0_ffn_Wv, L0_ffn_bv, L0_ffn_Wo, L0_ffn_bo, L0_ffn_router_w, L0_ffn_router_b, L0_ffn_W1, L0_ffn_b1, L0_ffn_W2, L0_ffn_b2, L0_ffn_ln1_g, L0_ffn_ln1_b, L0_ffn_ln2_g, L0_ffn_ln2_b):

    def _L0_attn_ref(x, Wq, Wk, Wv, Wo):
        import jax, jax.numpy as jnp
        import numpy as np
        import math
        B, L, D = (2, 512, 256)
        H, KV, HD = (16, 4, 64)
        GROUPS = H // KV
        ROPE_BASE = 10000.0

        def _alibi_slopes(n_heads):

            def pow2(n):
                start = 2.0 ** (-2.0 ** (-(math.log2(n) - 3)))
                return [start * start ** i for i in range(n)]
            if math.log2(n_heads).is_integer():
                return pow2(n_heads)
            c = 2 ** math.floor(math.log2(n_heads))
            return pow2(c) + _alibi_slopes(2 * c)[0::2][:n_heads - c]

        def _rope_cos_sin(seq_len, dim, dtype):
            inv_freq = 1.0 / ROPE_BASE ** (jnp.arange(0, dim, 2, dtype=jnp.float32) / dim)
            t = jnp.arange(seq_len, dtype=jnp.float32)
            freqs = t[:, None] * inv_freq[None, :]
            emb = jnp.concatenate([freqs, freqs], axis=-1)
            return (jnp.cos(emb).astype(dtype), jnp.sin(emb).astype(dtype))

        def _rotate_half(x):
            x1, x2 = (x[..., :x.shape[-1] // 2], x[..., x.shape[-1] // 2:])
            return jnp.concatenate([-x2, x1], axis=-1)
        b, l, _ = x.shape
        q = (x @ Wq).reshape(b, l, H, HD).transpose(0, 2, 1, 3)
        k = (x @ Wk).reshape(b, l, KV, HD).transpose(0, 2, 1, 3)
        v = (x @ Wv).reshape(b, l, KV, HD).transpose(0, 2, 1, 3)
        k = jnp.repeat(k, GROUPS, axis=1)
        v = jnp.repeat(v, GROUPS, axis=1)
        cos, sin = _rope_cos_sin(l, HD, x.dtype)
        q = q * cos + _rotate_half(q) * sin
        k = k * cos + _rotate_half(k) * sin
        attn = jnp.einsum('bhqd,bhkd->bhqk', q, k) / math.sqrt(HD)
        pos = jnp.arange(l)
        rel = (pos[None, :] - pos[:, None]).astype(x.dtype)
        slopes = jnp.asarray(_alibi_slopes(H), dtype=x.dtype)
        attn = attn + slopes[None, :, None, None] * rel[None, None, :, :]
        attn = jax.nn.softmax(attn, axis=-1)
        out = jnp.einsum('bhqk,bhkd->bhqd', attn, v)
        out = out.transpose(0, 2, 1, 3).reshape(b, l, H * HD)
        return out @ Wo

    def _L0_ffn_ref(src, Wq, bq, Wk, bk, Wv, bv, Wo, bo, router_w, router_b, W1, b1, W2, b2, ln1_g, ln1_b, ln2_g, ln2_b):
        import jax, jax.numpy as jnp
        import numpy as np
        D_MODEL = 256
        N_HEAD = 16
        HEAD_DIM = D_MODEL // N_HEAD
        D_FF = 1024
        N_EXPERTS = 4
        EPS = 1e-05

        def _layer_norm(x, gamma, beta):
            mu = jnp.mean(x, axis=-1, keepdims=True)
            var = jnp.mean((x - mu) ** 2, axis=-1, keepdims=True)
            return (x - mu) / jnp.sqrt(var + EPS) * gamma + beta
        B, T, _ = src.shape
        q = (src @ Wq + bq).reshape(B, T, N_HEAD, HEAD_DIM)
        k = (src @ Wk + bk).reshape(B, T, N_HEAD, HEAD_DIM)
        v = (src @ Wv + bv).reshape(B, T, N_HEAD, HEAD_DIM)
        scale = HEAD_DIM ** (-0.5)
        scores = jnp.einsum('bqhd,bkhd->bhqk', q, k) * scale
        probs = jax.nn.softmax(scores, axis=-1)
        attn = jnp.einsum('bhqk,bkhd->bqhd', probs, v).reshape(B, T, D_MODEL)
        attn = attn @ Wo + bo
        x = _layer_norm(src + attn, ln1_g, ln1_b)
        keys = (x @ router_w + router_b)[..., 0]
        expert_idx = jnp.remainder(jnp.floor(keys).astype(jnp.int32), N_EXPERTS)
        ff_out = jnp.zeros_like(x)
        for e in range(N_EXPERTS):
            h = jax.nn.relu(x @ W1[e] + b1[e])
            y = h @ W2[e] + b2[e]
            ff_out = ff_out + jnp.where((expert_idx == e)[..., None], y, 0.0)
        return _layer_norm(x + ff_out, ln2_g, ln2_b)
    x = L0_attn_x
    xn = _layernorm(x, axis=-1)
    x = x + _L0_attn_ref(xn, L0_attn_Wq, L0_attn_Wk, L0_attn_Wv, L0_attn_Wo) + _L0_ffn_ref(xn, L0_ffn_Wq, L0_ffn_bq, L0_ffn_Wk, L0_ffn_bk, L0_ffn_Wv, L0_ffn_bv, L0_ffn_Wo, L0_ffn_bo, L0_ffn_router_w, L0_ffn_router_b, L0_ffn_W1, L0_ffn_b1, L0_ffn_W2, L0_ffn_b2, L0_ffn_ln1_g, L0_ffn_ln1_b, L0_ffn_ln2_g, L0_ffn_ln2_b)
    return x

_drawn_inputs = setup_inputs


def setup_inputs(seed=0):
    import zlib

    import numpy as np

    out = dict(_drawn_inputs(seed))
    spreads = {'L0_ffn_bq': (0.0, 0.277),
     'L0_ffn_bk': (0.0, 0.8),
     'L0_ffn_bv': (0.0, 0.1),
     'L0_ffn_bo': (0.0, 0.1),
     'L0_ffn_b1': (0.0, 0.277),
     'L0_ffn_b2': (0.0, 0.1),
     'L0_ffn_ln1_g': (1.0, 0.2),
     'L0_ffn_ln1_b': (0.0, 0.1),
     'L0_ffn_ln2_g': (1.0, 0.2),
     'L0_ffn_ln2_b': (0.0, 0.1)}
    factors = {'L0_attn_Wq': 8.0, 'L0_attn_Wk': 8.0}
    for name, (base, spread) in spreads.items():
        noise = np.random.default_rng([zlib.crc32(name.encode()), seed]).standard_normal(out[name].shape)
        drawn = base * np.exp(spread * noise) if base else spread * noise
        out[name] = jnp.asarray(drawn.astype(out[name].dtype))
    for name, factor in factors.items():
        out[name] = (out[name] * factor).astype(out[name].dtype)
    return out
```

```python
from contextlib import ExitStack

import concourse.bass as bass
from concourse import mybir

F32 = mybir.dt.float32
F32R = mybir.dt.float32r
BF16 = mybir.dt.bfloat16
I32 = mybir.dt.int32
ALU = mybir.AluOpType
ACT = mybir.ActivationFunctionType
AX = mybir.AxisListType

P = 128
B = 8
S = 512
D = 256
TT = S // P
KC = D // P
H = 16
EPS = 1e-5

HD = 64
KV = 4
GRP = H // KV
PAIRS = H // 2
XR = HD + 3
XRP = XR + 1

FH = D // H
FB = 64
FF = 1024
NE = 4
TOK = 256
TILES = (B * S - NE) // TOK + NE


class Signal:

    def __init__(self, ctx, nc, name, per, credit=0, step=1):
        self.sem = ctx.enter_context(nc.semaphore(name))
        self.per, self.credit, self.step = per, credit, step

    def at(self, b, n):
        return b * (self.per * self.step) + (self.credit + n + 1) * self.step

    def grant(self, eng):
        eng.sem_inc(self.sem, self.credit * self.step)


class LayerNorm:

    def __init__(self, nc, ctx, name):
        def sb(what, shape):
            return ctx.enter_context(nc.sbuf_tensor(f"{name}_{what}", shape, F32))

        self.nc = nc
        self.stats, self.aggr = sb("stats", [P, TT, 6]), sb("aggr", [P, TT, 2])
        self.var_eps, self.rstd, self.power = sb("var_eps", [P, TT]), sb("rstd", [P, TT]), sb("power", [P, TT])
        self.stats_done = Signal(ctx, nc, f"{name}_stats_done", TT)
        self.aggr_done = Signal(ctx, nc, f"{name}_aggr_done", TT)
        self.var_done = Signal(ctx, nc, f"{name}_var_done", 1)
        self.rstd_done = Signal(ctx, nc, f"{name}_rstd_done", 1)
        self.passed = ctx.enter_context(nc.semaphore(f"{name}_passed"))
        self.power_set = ctx.enter_context(nc.semaphore(f"{name}_power_set"))

    def set_power(self, pool):
        self.nc.gpsimd.memset(self.power[:, :], -0.5).then_inc(self.power_set, 1)
        pool.wait_ge(self.power_set, 1)

    def raise_variance(self, pool, b):
        pool.wait_ge(self.var_done.sem, self.var_done.at(b, 0))
        self.nc.gpsimd.tensor_tensor(self.rstd[:, :], self.var_eps[:, :], self.power[:, :],
                                     ALU.pow).then_inc(self.rstd_done.sem, 1)

    def statistics(self, dve, b, src):
        for t in range(TT):
            self.nc.vector.bn_stats(self.stats[:, t, :], src[:, t, :]).then_inc(self.stats_done.sem, 1)
        for t in range(TT):
            dve.wait_ge(self.stats_done.sem, self.stats_done.at(b, t))
            dve.sem_inc(self.passed, 1)
            self.nc.vector.bn_aggr(self.aggr[:, t, :], self.stats[:, t, :]).then_inc(self.aggr_done.sem, 1)
        dve.wait_ge(self.aggr_done.sem, self.aggr_done.at(b, TT - 1))
        self.nc.vector.tensor_scalar(self.var_eps[:, :], self.aggr[:, :, 1], EPS, None,
                                     ALU.add).then_inc(self.var_done.sem, 1)

    def apply(self, dve, b, src, dst, applied):
        dve.wait_ge(self.rstd_done.sem, self.rstd_done.at(b, 0))
        for t in range(TT):
            self.nc.vector.tensor_scalar(dst[:, t, :], src[:, t, :], self.aggr[:, t, 0:1], self.rstd[:, t:t + 1],
                                         ALU.subtract, ALU.mult).then_inc(applied.sem, 1)


def rotary_attention_phase(nc, x, Wq, Wk, Wv, Wo, rope, slopes, slope_parts, key_rows, ident, result):
    QB = H * HD // 512
    NB = TT * (QB + 1)
    MU = 2 * TT
    RG = 4
    with ExitStack() as ctx:
        def sb(name, shape, dt=F32):
            return ctx.enter_context(nc.sbuf_tensor("a_" + name, shape, dt))

        def ps(name, shape):
            return ctx.enter_context(nc.psum_tensor("a_" + name, shape, F32))

        def sig(name, per, credit=0, step=1):
            return Signal(ctx, nc, "a_" + name, per, credit, step)

        wq = sb("wq", [P, KC, H * HD])
        wkv = sb("wkv", [P, KC, 2 * KV * HD])
        wo = sb("wo", [P, PAIRS, D])
        rope_t = sb("rope_t", [P, 6, TT, HD // 2])
        alibi = sb("alibi", [P, H, S], BF16)
        idn = sb("idn", [P, P])
        ones = sb("ones", [P, HD])
        minus = sb("minus", [P, TT])
        xn = sb("xn", [P, TT, D])
        norm = LayerNorm(nc, ctx, "a_norm")
        xnT = sb("xnT", [P, KC, S])
        q_tok = sb("q_tok", [P, TT, H, HD + XRP])
        k_tok = sb("k_tok", [P, TT, KV, 3, HD])
        v = sb("v", [P, TT, KV * HD])
        kA = sb("kA", [P, KV, S], F32R)
        kB = sb("kB", [XR, KV, S], F32R)
        qA = sb("qA", [P, RG, S], F32R)
        qB = sb("qB", [XR, RG, S], F32R)
        probs = sb("probs", [P, 8, 2, S])
        rot_c = probs[:, 0:2, 0, :]
        rot_s = probs[:, 2:4, 0, :]
        rot = probs[:, 4:6, 0, :]
        maxes = sb("maxes", [P, H, TT])
        junk = sb("junk", [P, 2, S], BF16)
        rden = sb("rden", [P, S])
        oT = sb("oT", [P, PAIRS, S])
        acc = sb("acc", [P, TT, D])

        psS = ps("psS", [P, 4, S])
        psR = ps("psR", [P, 2, S])
        psO = ps("psO", [P, S])
        psD = ps("psD", [P, S])

        loads = ctx.enter_context(nc.semaphore("a_loads"))
        rows_made = ctx.enter_context(nc.semaphore("a_rows_made"))
        alibi_made = ctx.enter_context(nc.semaphore("a_alibi_made"))
        passed = ctx.enter_context(nc.semaphore("a_passed"))
        ones_made = ctx.enter_context(nc.semaphore("a_ones_made"))
        LOADS = (14 + TT) * 16
        x_in = sig("x_in", 1, step=16)
        xn_done = sig("xn_done", TT)
        xnT_ps = sig("xnT_ps", KC, credit=1)
        xnT_sb = sig("xnT_sb", KC)
        proj_ps = sig("proj_ps", NB)
        rot_mul = sig("rot_mul", NB)
        rot_half = sig("rot_half", NB)
        rot_sum = sig("rot_sum", NB, credit=2)
        hi_done = sig("hi_done", NB)
        lo_done = sig("lo_done", NB, credit=2)
        v_done = sig("v_done", TT)
        kT_ps = sig("kT_ps", 2 * KV)
        kA_done = sig("kA_done", KV)
        kB_done = sig("kB_done", KV)
        qAT_ps = sig("qAT_ps", H)
        qA_done = sig("qA_done", H)
        max_ps = sig("max_ps", PAIRS * MU)
        max_done = sig("max_done", PAIRS * MU, credit=2)
        neg_done = sig("neg_done", H)
        qBT_ps = sig("qBT_ps", H)
        qB_done = sig("qB_done", H)
        score_ps = sig("score_ps", 2 * H)
        exp_done = sig("exp_done", 2 * H, credit=2)
        pv_done = sig("pv_done", H, credit=4)
        rden_done = sig("rden_done", PAIRS)
        norm_done = sig("norm_done", PAIRS, credit=1)
        out_ps = sig("out_ps", 2)
        acc_done = sig("acc_done", 2, credit=1)
        res_in = sig("res_in", 1, step=16)
        stored = sig("stored", 1, credit=1, step=16)

        rows = x.rearrange("b (t p) d -> b p t d", p=P)
        out_rows = result.rearrange("b (t p) d -> b p t d", p=P)
        block = ctx.enter_context(nc.Block())

        @block.sync
        def _(sp):
            stored.grant(sp)
            sp.dma_start(idn[:, :], ident).then_inc(loads, 16)
            sp.dma_start(wq[:, :, :], Wq.rearrange("(c p) n -> p c n", p=P)).then_inc(loads, 16)
            sp.dma_start(wkv[:, :, 0:KV * HD], Wk.rearrange("(c p) n -> p c n", p=P)).then_inc(loads, 16)
            sp.dma_start(wkv[:, :, KV * HD:], Wv.rearrange("(c p) n -> p c n", p=P)).then_inc(loads, 16)
            sp.dma_start(wo[:, :, :], Wo.rearrange("(c p) n -> p c n", p=P)).then_inc(loads, 16)
            for k in range(6):
                sp.dma_start(rope_t[:, k, :, :], rope[k].rearrange("(t p) n -> p t n", p=P)).then_inc(loads, 16)
            for t in range(TT):
                sp.dma_start(q_tok[:, t, :, 2 * HD + 1:HD + XR], slope_parts.partition_broadcast(P)).then_inc(loads, 16)
            sp.dma_start(acc[:, 0, 0:H], slopes.partition_broadcast(P)).then_inc(loads, 16)
            sp.dma_start(probs[:, 0, 0, :], key_rows[1].partition_broadcast(P)).then_inc(loads, 16)
            sp.dma_start(probs[HD:XR, 1, 0, :], key_rows).then_inc(loads, 16)
            sp.wait_ge(alibi_made, H)
            with sp.Fori(0, B) as b:
                sp.wait_ge(xnT_ps.sem, xnT_ps.at(b, -1))
                sp.dma_start(xn[:, :, :], rows[b]).then_inc(x_in.sem, 16)
                sp.wait_ge(stored.sem, stored.at(b, -1))
                sp.dma_start(acc[:, :, :], rows[b]).then_inc(res_in.sem, 16)
                sp.wait_ge(acc_done.sem, acc_done.at(b, 1))
                sp.dma_start(out_rows[b], acc[:, :, :]).then_inc(stored.sem, 16)
            sp.wait_ge(stored.sem, stored.at(B - 1, 0))

        @block.gpsimd
        def _(pool):
            rot_sum.grant(pool)
            lo_done.grant(pool)
            nc.gpsimd.memset(ones[:, :], 1.0).then_inc(ones_made, 1)
            nc.gpsimd.memset(minus[:, :], -1.0).then_inc(ones_made, 1)
            pool.wait_ge(ones_made, 2)
            norm.set_power(pool)
            pool.wait_ge(loads, LOADS)
            with pool.Fori(0, B) as b:
                norm.raise_variance(pool, b)
                for n in range(NB):
                    t, i = divmod(n, QB + 1)
                    w = 512 if i < QB else KV * HD
                    pool.wait_ge(rot_half.sem, rot_half.at(b, n))
                    pool.wait_ge(lo_done.sem, lo_done.at(b, n - 2))
                    nc.gpsimd.tensor_tensor(rot[:, n % 2, 0:w], rot_c[:, n % 2, 0:w], rot_s[:, n % 2, 0:w],
                                            ALU.add).then_inc(rot_sum.sem, 1)
                    pool.wait_ge(hi_done.sem, hi_done.at(b, n))
                    src = rot[:, n % 2, 0:w].rearrange("p (h d) -> p h d", d=HD)
                    if i < QB:
                        hs = slice(i * 8, i * 8 + 8)
                        low, high = q_tok[:, t, hs, 0:HD], q_tok[:, t, hs, HD:2 * HD]
                    else:
                        low, high = k_tok[:, t, :, 0, :], k_tok[:, t, :, 1, :]
                    nc.gpsimd.tensor_tensor(low, src, high, ALU.subtract).then_inc(lo_done.sem, 1)
                for h in range(H):
                    pool.wait_ge(max_done.sem, max_done.at(b, TT * h + TT - 1))
                    nc.gpsimd.tensor_tensor(q_tok[:, :, h, 2 * HD], maxes[:, h, :], minus[:, :],
                                            ALU.mult).then_inc(neg_done.sem, 1)

        @block.scalar
        def _(act):
            exp_done.grant(act)
            act.wait_ge(loads, LOADS)
            for g in range(KV):
                nc.scalar.copy(kB[HD:XR, g, :], probs[HD:XR, 1, 0, :]).then_inc(rows_made, 1)
            act.wait_ge(rows_made, KV)
            act.wait_ge(alibi_made, H)
            with act.Fori(0, B) as b:
                for c in range(KC):
                    act.wait_ge(xnT_ps.sem, xnT_ps.at(b, c))
                    nc.scalar.copy(xnT[:, c, :], psR[:, c, :]).then_inc(xnT_sb.sem, 1)
                for n in range(NB):
                    t, i = divmod(n, QB + 1)
                    w = 512 if i < QB else KV * HD
                    if i == QB:
                        act.wait_ge(rot_half.sem, rot_half.at(b, n))
                        nc.scalar.copy(v[:, t, :], psS[:, n % 4, KV * HD:]).then_inc(v_done.sem, 1)
                    act.wait_ge(rot_sum.sem, rot_sum.at(b, n))
                    src = rot[:, n % 2, 0:w].rearrange("p (h d) -> p h d", d=HD)
                    if i < QB:
                        high = q_tok[:, t, i * 8:i * 8 + 8, HD:2 * HD]
                    else:
                        high = k_tok[:, t, :, 1:3, :]
                        src = src.unsqueeze(2).to_broadcast([P, KV, 2, HD])
                    nc.scalar.copy(high.bitcast(F32R), src).then_inc(hi_done.sem, 1)
                for g in range(KV):
                    act.wait_ge(kT_ps.sem, kT_ps.at(b, 2 * g))
                    nc.scalar.copy(kA[:, g, :], psR[:, 0, :]).then_inc(kA_done.sem, 1)

                def take_qA(p):
                    for h in (2 * p, 2 * p + 1):
                        act.wait_ge(qAT_ps.sem, qAT_ps.at(b, h))
                        nc.scalar.copy(qA[:, h % RG, :], psR[:, h % 2, :]).then_inc(qA_done.sem, 1)

                def take_qB(p):
                    for h in (2 * p, 2 * p + 1):
                        act.wait_ge(qBT_ps.sem, qBT_ps.at(b, h))
                        nc.scalar.copy(qB[:, h % RG, :], psR[0:XR, h % 2, :]).then_inc(qB_done.sem, 1)

                take_qA(0)
                take_qB(0)
                take_qA(1)
                for p in range(PAIRS):
                    for u in range(4):
                        i = 4 * p + u
                        act.wait_ge(score_ps.sem, score_ps.at(b, i))
                        act.wait_ge(pv_done.sem, pv_done.at(b, 2 * (p - 2) + u // 2))
                        nc.scalar.activation(probs[:, i % 8, :, :], psS[:, 2 * (u % 2):2 * (u % 2) + 2, :],
                                             ACT.Exp).then_inc(exp_done.sem, 1)
                    if p + 1 < PAIRS:
                        take_qB(p + 1)
                    if p + 2 < PAIRS:
                        take_qA(p + 2)

        @block.vector
        def _(dve):
            max_done.grant(dve)
            norm_done.grant(dve)
            acc_done.grant(dve)
            dve.wait_ge(loads, LOADS)
            for h in range(H):
                nc.vector.tensor_scalar(alibi[:, h, :], probs[:, 0, 0, :], acc[:, 0, h:h + 1], None,
                                        ALU.mult).then_inc(alibi_made, 1)
            dve.wait_ge(alibi_made, H)
            dve.wait_ge(rows_made, KV)
            with dve.Fori(0, B) as b:
                dve.wait_ge(x_in.sem, x_in.at(b, 0))
                norm.statistics(dve, b, xn)
                norm.apply(dve, b, xn, xn, xn_done)
                for n in range(NB):
                    t, i = divmod(n, QB + 1)
                    w, k = (512, 0) if i < QB else (KV * HD, 3)
                    hw = w // (HD // 2)
                    dve.wait_ge(proj_ps.sem, proj_ps.at(b, n))
                    dve.wait_ge(rot_sum.sem, rot_sum.at(b, n - 2))
                    halves = psS[:, n % 4, 0:w].rearrange("p (h d) -> p h d", d=HD // 2)
                    cos = rope_t[:, k, t, :].unsqueeze(1).to_broadcast([P, hw, HD // 2])
                    nc.vector.tensor_tensor(rot_c[:, n % 2, 0:w].rearrange("p (h d) -> p h d", d=HD // 2),
                                            halves, cos, ALU.mult).then_inc(rot_mul.sem, 1)
                    pairs = psS[:, n % 4, 0:w].rearrange("p (h a d) -> p h a d", a=2, d=HD // 2)
                    out = rot_s[:, n % 2, 0:w].rearrange("p (h a d) -> p h a d", a=2, d=HD // 2)
                    for a in range(2):
                        sin = rope_t[:, k + 1 + a, t, :].unsqueeze(1).to_broadcast([P, hw // 2, HD // 2])
                        last = nc.vector.tensor_tensor(out[:, :, a, :], pairs[:, :, 1 - a, :], sin, ALU.mult)
                    last.then_inc(rot_half.sem, 1)
                for g in range(KV):
                    dve.wait_ge(kT_ps.sem, kT_ps.at(b, 2 * g + 1))
                    nc.vector.tensor_copy(kB[0:HD, g, :], psR[0:HD, 1, :]).then_inc(kB_done.sem, 1)

                def take_max(m):
                    h, c = divmod(m, TT)
                    dve.wait_ge(max_ps.sem, max_ps.at(b, m))
                    dve.wait_ge(max_done.sem, max_done.at(b, m - 2))
                    dve.sem_inc(passed, 1)
                    nc.vector.tensor_tensor_reduce(
                        out=junk[:, m % 2, :], in0=psR[:, m % 2, :], in1=alibi[:, h, :], scale=1.0,
                        scalar=-3.0e38, op0=ALU.add, op1=ALU.max,
                        accum_out=maxes[:, h, c:c + 1]).then_inc(max_done.sem, 1)

                def normalize(p):
                    dve.wait_ge(pv_done.sem, pv_done.at(b, 2 * p + 1))
                    if p > 0:
                        dve.wait_ge(norm_done.sem, norm_done.at(b, p - 1))
                    nc.vector.reciprocal(rden[:, :], psD[:, :]).then_inc(rden_done.sem, 1)
                    dve.wait_ge(rden_done.sem, rden_done.at(b, p))
                    nc.vector.tensor_tensor(oT[:, p, :], psO[:, :], rden[:, :], ALU.mult).then_inc(norm_done.sem, 1)

                for m in range(MU):
                    take_max(m)
                for p in range(PAIRS):
                    for m in range(MU):
                        if m == 3 and p > 0:
                            normalize(p - 1)
                        if p + 1 < PAIRS:
                            take_max((p + 1) * MU + m)
                normalize(PAIRS - 1)
                dve.wait_ge(res_in.sem, res_in.at(b, 0))
                for k in range(2):
                    dve.wait_ge(out_ps.sem, out_ps.at(b, k))
                    nc.vector.tensor_tensor(acc[:, 2 * k:2 * k + 2, :], acc[:, 2 * k:2 * k + 2, :],
                                            psR[:, k, :].rearrange("p (t d) -> p t d", d=D),
                                            ALU.add).then_inc(acc_done.sem, 1)

        @block.tensor
        def _(pe):
            xnT_ps.grant(pe)
            pv_done.grant(pe)
            pe.wait_ge(loads, LOADS)
            pe.wait_ge(ones_made, 1)
            pe.wait_ge(rows_made, KV)
            with pe.Fori(0, B) as b:
                pe.wait_ge(acc_done.sem, acc_done.at(b, -1))
                for t in range(TT):
                    pe.wait_ge(xn_done.sem, xn_done.at(b, t))
                    for c in range(KC):
                        last = nc.tensor.transpose(psR[:, c, t * P:(t + 1) * P], xn[:, t, c * P:(c + 1) * P],
                                                   idn[:, :])
                        if t == TT - 1:
                            last.then_inc(xnT_ps.sem, 1)
                pe.wait_ge(xnT_sb.sem, xnT_sb.at(b, KC - 1))
                for n in range(NB):
                    t, i = divmod(n, QB + 1)
                    if n >= 4:
                        pe.wait_ge(rot_half.sem, rot_half.at(b, n - 4))
                        if (n - 4) % (QB + 1) == QB:
                            pe.wait_ge(v_done.sem, v_done.at(b, (n - 4) // (QB + 1)))
                    for c in range(KC):
                        w = wq[:, c, i * 512:(i + 1) * 512] if i < QB else wkv[:, c, :]
                        last = nc.tensor.matmul(psS[:, n % 4, :], xnT[:, c, t * P:(t + 1) * P], w,
                                                start=(c == 0), stop=(c == KC - 1))
                    last.then_inc(proj_ps.sem, 1)

                pe.wait_ge(lo_done.sem, lo_done.at(b, NB - 1))
                pe.wait_ge(v_done.sem, v_done.at(b, TT - 1))

                for g in range(KV):
                    for bank, first, taken in ((0, 1, kA_done), (1, 0, kB_done)):
                        if g > 0:
                            pe.wait_ge(taken.sem, taken.at(b, g - 1))
                        for t in range(TT):
                            src = k_tok[:, t, g, first:first + 2, :].rearrange("p a d -> p (a d)")
                            last = nc.tensor.transpose(psR[:, bank, t * P:(t + 1) * P], src, idn[:, :])
                        last.then_inc(kT_ps.sem, 1)
                pe.wait_ge(kA_done.sem, kA_done.at(b, KV - 1))
                pe.wait_ge(kB_done.sem, kB_done.at(b, KV - 1))

                def queries_parts(p):
                    for h in (2 * p, 2 * p + 1):
                        for t in range(TT):
                            last = nc.tensor.transpose(psR[:, h % 2, t * P:(t + 1) * P],
                                                       q_tok[:, t, h, 0:2 * HD], idn[:, :])
                        last.then_inc(qAT_ps.sem, 1)

                def scores_for_max(m):
                    h, c = divmod(m, TT)
                    if c == 0:
                        pe.wait_ge(qA_done.sem, qA_done.at(b, h))
                    if m % MU < 2:
                        pe.wait_ge(qA_done.sem, qA_done.at(b, h + m % MU))
                    else:
                        pe.wait_ge(max_done.sem, max_done.at(b, m - 2))
                    nc.tensor.matmul(psR[:, m % 2, :], qA[:, h % RG, c * P:(c + 1) * P], kA[:, h // GRP, :],
                                     start=True, stop=True).then_inc(max_ps.sem, 1)

                def queries_shifted(p):
                    for h in (2 * p, 2 * p + 1):
                        pe.wait_ge(max_done.sem, max_done.at(b, (p + 1) * MU - 2 + h % 2))
                        pe.wait_ge(neg_done.sem, neg_done.at(b, h))
                        for t in range(TT):
                            last = nc.tensor.transpose(psR[0:XR, h % 2, t * P:(t + 1) * P],
                                                       q_tok[:, t, h, HD:HD + XR], idn[:, :])
                        last.then_inc(qBT_ps.sem, 1)

                def scores(p, u):
                    h, half = 2 * p + u % 2, u // 2
                    pe.wait_ge(exp_done.sem, exp_done.at(b, 4 * p + u - 2))
                    pe.wait_ge(qB_done.sem, qB_done.at(b, h))
                    for a in range(2):
                        keys = slice((2 * half + a) * P, (2 * half + a + 1) * P)
                        bank = psS[:, 2 * (u % 2) + a, :]
                        nc.tensor.matmul(bank, kA[:, h // GRP, keys], qA[:, h % RG, :], start=True, stop=False)
                        last = nc.tensor.matmul(bank, kB[:, h // GRP, keys], qB[:, h % RG, :],
                                                start=False, stop=True)
                    last.then_inc(score_ps.sem, 1)

                def weigh_values(p, half):
                    pe.wait_ge(exp_done.sem, exp_done.at(b, 4 * p + 2 * half + 1))
                    if half == 0:
                        pe.wait_ge(norm_done.sem, norm_done.at(b, p - 1))
                    for a in range(2):
                        j = 2 * half + a
                        for src, dst in ((v, psO), (ones, psD)):
                            for e in range(2):
                                h = 2 * p + e
                                g = h // GRP
                                lhs = v[:, j, g * HD:(g + 1) * HD] if src is v else ones[:, :]
                                last = nc.tensor.matmul(dst[e * HD:(e + 1) * HD, :], lhs,
                                                        probs[:, (4 * p + 2 * half + e) % 8, a, :],
                                                        start=(j == 0), stop=(j == TT - 1))
                    last.then_inc(pv_done.sem, 1)

                queries_parts(0)
                for m in range(MU):
                    scores_for_max(m)
                queries_shifted(0)
                pe.wait_ge(qB_done.sem, qB_done.at(b, 1))
                queries_parts(1)
                for p in range(PAIRS):
                    nxt = p + 1 < PAIRS
                    for u in range(4):
                        scores(p, u)
                        if u == 1 and p > 0:
                            weigh_values(p - 1, 1)
                        if nxt:
                            for m in ((0, 1, 2), (3, 4, 5), (6, 7), ())[u]:
                                scores_for_max((p + 1) * MU + m)
                    if nxt:
                        queries_shifted(p + 1)
                    weigh_values(p, 0)
                    if p + 2 < PAIRS:
                        pe.wait_ge(qB_done.sem, qB_done.at(b, 2 * p + 3))
                        queries_parts(p + 2)
                weigh_values(PAIRS - 1, 1)
                pe.wait_ge(norm_done.sem, norm_done.at(b, PAIRS - 1))
                for t in range(TT):
                    for p in range(PAIRS):
                        last = nc.tensor.matmul(psR[:, t // 2, (t % 2) * D:(t % 2 + 1) * D],
                                                oT[:, p, t * P:(t + 1) * P], wo[:, p, :],
                                                start=(p == 0), stop=(p == PAIRS - 1))
                    if t % 2:
                        last.then_inc(out_ps.sem, 1)


def plain_attention_phase(nc, x, w, ident, expert, x1):
    NB = 2 * TT
    QUADS = H // 4
    MP = 2 * TT
    MQ = 2 * MP
    UQ = 8
    NEG = 3 * FH
    with ExitStack() as ctx:
        def sb(name, shape, dt=F32):
            return ctx.enter_context(nc.sbuf_tensor("f_" + name, shape, dt))

        def ps(name, shape):
            return ctx.enter_context(nc.psum_tensor("f_" + name, shape, F32))

        def sig(name, per, credit=0, step=1):
            return Signal(ctx, nc, "f_" + name, per, credit, step)

        wqk = sb("wqk", [P, KC, 2 * D])
        wv = sb("wv", [P, KC, D])
        wo = sb("wo", [P, QUADS, D])
        bqk = sb("bqk", [P, 2 * D])
        bv, bo, g1, b1, rw = (sb(n, [P, D]) for n in ("bv", "bo", "g1", "b1", "rw"))
        rb = sb("rb", [P, 1])
        idn = sb("idn", [P, P])
        norm0, norm1 = LayerNorm(nc, ctx, "f_norm0"), LayerNorm(nc, ctx, "f_norm1")
        xn = sb("xn", [P, TT, D])
        xnb = sb("xnb", [P, TT, D])
        xnT = sb("xnT", [P, KC, S])
        qk = sb("qk", [P, 2, 2 * D])
        q_tok = sb("q_tok", [P, TT, H, FB])
        k_tok = sb("k_tok", [P, TT, H, FB])
        v = sb("v", [P, TT, H, 2 * FH])
        kZ = sb("kZ", [P, 8, S], F32R)
        qM = sb("qM", [P, 2, S], F32R)
        qS = sb("qS", [P, 4, S], F32R)
        probs = sb("probs", [P, 8, 2, S])
        sums = sb("sums", [P, S])
        rsum = sb("rsum", [P, S])
        oT = sb("oT", [P, QUADS, S])
        r1 = sb("r1", [P, TT, D])
        keyj = sb("keyj", [P, TT, D])
        key = sb("key", [P, TT])
        keyb = sb("keyb", [P, TT])
        keyi = sb("keyi", [P, TT], I32)
        keyf = sb("keyf", [P, TT])
        above = sb("above", [P, TT])
        floor = sb("floor", [P, TT])
        floori = sb("floori", [P, TT], I32)
        modi = sb("modi", [P, TT], I32)

        psS = ps("psS", [P, 4, S])
        psR = ps("psR", [P, 2, S])
        psO = ps("psO", [P, S])

        loads = ctx.enter_context(nc.semaphore("f_loads"))
        zeroed = ctx.enter_context(nc.semaphore("f_zeroed"))
        passed = ctx.enter_context(nc.semaphore("f_passed"))
        scaled = ctx.enter_context(nc.semaphore("f_scaled"))
        key_step = sig("key_step", 8)
        LOADS = 16 * 16
        ZEROED = 7
        x_in = sig("x_in", 1, step=16)
        xn_done = sig("xn_done", TT)
        xnb_done = sig("xnb_done", 1, credit=1)
        xnT_ps = sig("xnT_ps", KC, credit=1)
        xnT_sb = sig("xnT_sb", KC)
        proj_ps = sig("proj_ps", NB)
        bias_done = sig("bias_done", NB)
        hi_done = sig("hi_done", TT)
        lo_done = sig("lo_done", TT, credit=2)
        neg_reset = sig("neg_reset", 1)
        kT_ps = sig("kT_ps", 2 * QUADS)
        k_even = sig("k_even", 2 * QUADS)
        k_odd = sig("k_odd", 2 * QUADS)
        qM_ps = sig("qM_ps", 2 * QUADS)
        qM_done = sig("qM_done", 2 * QUADS)
        max_ps = sig("max_ps", QUADS * MQ)
        max_done = sig("max_done", QUADS * MQ)
        qS_ps = sig("qS_ps", 2 * QUADS, credit=1)
        qS_done = sig("qS_done", 2 * QUADS)
        score_ps = sig("score_ps", QUADS * UQ)
        exp_done = sig("exp_done", QUADS * UQ, credit=2)
        pv_done = sig("pv_done", 2 * QUADS, credit=2)
        sum_done = sig("sum_done", QUADS)
        rsum_done = sig("rsum_done", QUADS)
        norm_done = sig("norm_done", QUADS, credit=1)
        out_ps = sig("out_ps", 2)
        r1_done = sig("r1_done", 2, credit=1)
        n1_done = sig("n1_done", TT)
        gain_done = sig("gain_done", 1)
        x1_done = sig("x1_done", 1, credit=1)
        key_done = sig("key_done", 1)

        rows = x.rearrange("b (t p) d -> b p t d", p=P)
        def max_use(m):
            quad, m = divmod(m, MQ)
            return 22 * quad + 4 + m + (m >= MP)

        def shifted_use(p):
            quad, e = divmod(p, 2)
            return 22 * quad + (12, 21)[e]

        block = ctx.enter_context(nc.Block())

        @block.sync
        def _(sp):
            sp.dma_start(idn[:, :], ident).then_inc(loads, 16)
            sp.dma_start(wqk[:, :, 0:D], w["Wq"].rearrange("(c p) n -> p c n", p=P)).then_inc(loads, 16)
            sp.dma_start(wqk[:, :, D:], w["Wk"].rearrange("(c p) n -> p c n", p=P)).then_inc(loads, 16)
            sp.dma_start(wv[:, :, :], w["Wv"].rearrange("(c p) n -> p c n", p=P)).then_inc(loads, 16)
            sp.dma_start(bqk[:, 0:D], w["bq"].partition_broadcast(P)).then_inc(loads, 16)
            sp.dma_start(bqk[:, D:], w["bk"].partition_broadcast(P)).then_inc(loads, 16)
            for tile, name in ((bv, "bv"), (bo, "bo"), (g1, "ln1_g"), (b1, "ln1_b")):
                sp.dma_start(tile[:, :], w[name].partition_broadcast(P)).then_inc(loads, 16)
            sp.dma_start(rw[:, :], w["router_w"].rearrange("d a -> (d a)").partition_broadcast(P)).then_inc(loads, 16)
            sp.dma_start(rb[:, :], w["router_b"].partition_broadcast(P)).then_inc(loads, 16)
            sp.wait_ge(zeroed, ZEROED)
            heads = w["Wo"].rearrange("(q i d) n -> i d q n", i=4, d=FH)
            for i in range(4):
                sp.dma_start(wo[32 * i:32 * i + FH, :, :], heads[i]).then_inc(loads, 16)
            with sp.Fori(0, B) as b:
                sp.wait_ge(xnT_ps.sem, xnT_ps.at(b, -1))
                sp.sem_inc(passed, 1)
                sp.wait_ge(xnb_done.sem, xnb_done.at(b, -1))
                sp.dma_start(xn[:, :, :], rows[b]).then_inc(x_in.sem, 16)

        @block.gpsimd
        def _(pool):
            lo_done.grant(pool)
            xnb_done.grant(pool)
            x1_done.grant(pool)
            norm0.set_power(pool)
            norm1.set_power(pool)
            for tile in (q_tok, k_tok, v, wo):
                nc.gpsimd.memset(tile[:, :, :] if len(tile.shape) == 3 else tile[:, :, :, :], 0.0).then_inc(zeroed, 1)
            nc.gpsimd.memset(kZ[:, :, :].bitcast(F32), 0.0).then_inc(zeroed, 1)
            pool.wait_ge(zeroed, 5)
            nc.gpsimd.memset(k_tok[:, :, :, NEG], 1.0).then_inc(zeroed, 1)
            nc.gpsimd.memset(v[:, :, :, FH:], 1.0).then_inc(zeroed, 1)
            pool.wait_ge(zeroed, ZEROED)
            pool.wait_ge(loads, LOADS)
            with pool.Fori(0, B) as b:
                norm0.raise_variance(pool, b)
                pool.wait_ge(qS_ps.sem, qS_ps.at(b, -1))
                pool.sem_inc(passed, 1)
                nc.gpsimd.memset(q_tok[:, :, :, NEG], 0.0).then_inc(neg_reset.sem, 1)
                for t in range(TT):
                    pool.wait_ge(hi_done.sem, hi_done.at(b, t))
                    src = qk[:, t % 2, :].rearrange("p (a h d) -> p a h d", a=2, d=FH)
                    nc.gpsimd.tensor_tensor(q_tok[:, t, :, FH:2 * FH], src[:, 0], q_tok[:, t, :, 0:FH], ALU.subtract)
                    nc.gpsimd.tensor_tensor(k_tok[:, t, :, 2 * FH:NEG], src[:, 1], k_tok[:, t, :, 0:FH],
                                            ALU.subtract).then_inc(lo_done.sem, 1)
                pool.wait_ge(r1_done.sem, r1_done.at(b, -1))
                bias = bo[:, :].unsqueeze(1).to_broadcast([P, TT, D])
                nc.gpsimd.tensor_tensor(xnb[:, :, :], xn[:, :, :], bias, ALU.add).then_inc(xnb_done.sem, 1)
                norm1.raise_variance(pool, b)
                pool.wait_ge(n1_done.sem, n1_done.at(b, TT - 1))
                x1_b = x1[:, bass.ds(b * TT, TT), :]
                gain, offset = (g[:, :].unsqueeze(1).to_broadcast([P, TT, D]) for g in (g1, b1))
                pool.sem_inc(passed, 1)
                nc.gpsimd.tensor_tensor(x1_b, r1[:, :, :], gain, ALU.mult).then_inc(gain_done.sem, 1)
                pool.wait_ge(gain_done.sem, gain_done.at(b, 0))
                pool.sem_inc(passed, 1)
                nc.gpsimd.tensor_tensor(x1_b, x1_b, offset, ALU.add).then_inc(x1_done.sem, 1)

        @block.scalar
        def _(act):
            exp_done.grant(act)
            act.wait_ge(loads, LOADS)
            nc.scalar.mul(wqk[:, :, 0:D], wqk[:, :, 0:D], FH ** -0.5).then_inc(scaled, 1)
            nc.scalar.mul(bqk[:, 0:D], bqk[:, 0:D], FH ** -0.5).then_inc(scaled, 1)
            with act.Fori(0, B) as b:
                for c in range(KC):
                    act.wait_ge(xnT_ps.sem, xnT_ps.at(b, c))
                    nc.scalar.copy(xnT[:, c, :], psR[:, c, :]).then_inc(xnT_sb.sem, 1)
                for t in range(TT):
                    act.wait_ge(bias_done.sem, bias_done.at(b, 2 * t))
                    src = qk[:, t % 2, :].rearrange("p (a h d) -> p a h d", a=2, d=FH)
                    q_high = q_tok[:, t, :, :].rearrange("p h (a c) -> p h a c", a=2)[:, :, :, 0:FH]
                    k_high = k_tok[:, t, :, 0:2 * FH].rearrange("p h (a c) -> p h a c", a=2)
                    nc.scalar.copy(q_high.bitcast(F32R), src[:, 0].unsqueeze(2).to_broadcast([P, H, 2, FH]))
                    nc.scalar.copy(k_high.bitcast(F32R),
                                   src[:, 1].unsqueeze(2).to_broadcast([P, H, 2, FH])).then_inc(hi_done.sem, 1)

                def take_keys_and_queries(quad):
                    for p in (2 * quad, 2 * quad + 1):
                        act.wait_ge(kT_ps.sem, kT_ps.at(b, p))
                        nc.scalar.copy(kZ[FB:, (2 * p + 1) % 8, :],
                                       psR[FB:, p % 2, :]).then_inc(k_odd.sem, 1)
                    for p in (2 * quad, 2 * quad + 1):
                        act.wait_ge(qM_ps.sem, qM_ps.at(b, p))
                        nc.scalar.copy(qM[:, p % 2, :], psR[:, p % 2, :]).then_inc(qM_done.sem, 1)

                def take_shifted(p):
                    act.wait_ge(qS_ps.sem, qS_ps.at(b, p))
                    nc.scalar.copy(qS[:, p % 4, :], psR[:, shifted_use(p) % 2, :]).then_inc(qS_done.sem, 1)

                take_keys_and_queries(0)
                take_shifted(0)
                take_shifted(1)
                take_keys_and_queries(1)
                for quad in range(QUADS):
                    for u in range(UQ):
                        i = UQ * quad + u
                        act.wait_ge(score_ps.sem, score_ps.at(b, i))
                        act.wait_ge(pv_done.sem, pv_done.at(b, 2 * (quad - 1) + u // 4))
                        nc.scalar.activation(probs[:, u, :, :], psS[:, 2 * (u % 2):2 * (u % 2) + 2, :],
                                             ACT.Exp).then_inc(exp_done.sem, 1)
                        if u == 4 and quad + 1 < QUADS:
                            take_shifted(2 * quad + 2)
                    if quad + 1 < QUADS:
                        take_shifted(2 * quad + 3)
                    if quad + 2 < QUADS:
                        take_keys_and_queries(quad + 2)

        @block.vector
        def _(dve):
            norm_done.grant(dve)
            r1_done.grant(dve)
            dve.wait_ge(loads, LOADS)
            dve.wait_ge(scaled, 2)
            dve.wait_ge(zeroed, ZEROED)
            with dve.Fori(0, B) as b:
                dve.wait_ge(x_in.sem, x_in.at(b, 0))
                norm0.statistics(dve, b, xn)
                norm0.apply(dve, b, xn, xn, xn_done)
                for t in range(TT):
                    dve.wait_ge(lo_done.sem, lo_done.at(b, t - 2))
                    dve.wait_ge(proj_ps.sem, proj_ps.at(b, 2 * t))
                    nc.vector.tensor_tensor(qk[:, t % 2, :], psS[:, 2 * t % 4, :], bqk[:, :],
                                            ALU.add).then_inc(bias_done.sem, 1)
                    dve.wait_ge(proj_ps.sem, proj_ps.at(b, 2 * t + 1))
                    nc.vector.tensor_tensor(v[:, t, :, 0:FH],
                                            psS[:, (2 * t + 1) % 4, 0:D].rearrange("p (h d) -> p h d", d=FH),
                                            bv[:, :].rearrange("p (h d) -> p h d", d=FH),
                                            ALU.add).then_inc(bias_done.sem, 1)

                def take_keys(quad):
                    for p in (2 * quad, 2 * quad + 1):
                        dve.wait_ge(kT_ps.sem, kT_ps.at(b, p))
                        nc.vector.tensor_copy(kZ[0:FB, 2 * p % 8, :], psR[0:FB, p % 2, :]).then_inc(k_even.sem, 1)

                def take_max(m):
                    h, c = divmod(m, TT)
                    dve.wait_ge(max_ps.sem, max_ps.at(b, m))
                    nc.vector.tensor_reduce(q_tok[:, c, h, NEG:NEG + 1], psR[:, max_use(m) % 2, :], AX.X, ALU.max,
                                            negate=True).then_inc(max_done.sem, 1)

                def normalize(quad):
                    dve.wait_ge(pv_done.sem, pv_done.at(b, 2 * quad + 1))
                    if quad:
                        dve.wait_ge(norm_done.sem, norm_done.at(b, quad - 1))
                    dve.sem_inc(passed, 1)
                    nc.vector.stream_shuffle(sums[:, :], psO[:, :], [FH + i % FH for i in range(32)])\
                        .then_inc(sum_done.sem, 1)
                    dve.wait_ge(sum_done.sem, sum_done.at(b, quad))
                    nc.vector.reciprocal(rsum[:, :], sums[:, :]).then_inc(rsum_done.sem, 1)
                    dve.wait_ge(rsum_done.sem, rsum_done.at(b, quad))
                    nc.vector.tensor_tensor(oT[:, quad, :], psO[:, :], rsum[:, :], ALU.mult).then_inc(norm_done.sem, 1)

                take_keys(0)
                for m in range(MQ):
                    take_max(m)
                take_keys(1)
                for quad in range(QUADS):
                    for m in range(MQ):
                        if m == 10 and quad:
                            normalize(quad - 1)
                        if quad + 1 < QUADS:
                            take_max((quad + 1) * MQ + m)
                    if quad + 2 < QUADS:
                        take_keys(quad + 2)
                normalize(QUADS - 1)
                dve.wait_ge(xnb_done.sem, xnb_done.at(b, 0))
                dve.wait_ge(x1_done.sem, x1_done.at(b, -1))
                for k in range(2):
                    dve.wait_ge(out_ps.sem, out_ps.at(b, k))
                    nc.vector.tensor_tensor(r1[:, 2 * k:2 * k + 2, :], xnb[:, 2 * k:2 * k + 2, :],
                                            psR[:, k, :].rearrange("p (t d) -> p t d", d=D),
                                            ALU.add).then_inc(r1_done.sem, 1)
                dve.wait_ge(r1_done.sem, r1_done.at(b, 1))
                norm1.statistics(dve, b, r1)
                norm1.apply(dve, b, r1, r1, n1_done)
                dve.wait_ge(x1_done.sem, x1_done.at(b, 0))
                nc.vector.tensor_tensor(keyj[:, :, :], x1[:, bass.ds(b * TT, TT), :],
                                        rw[:, :].unsqueeze(1).to_broadcast([P, TT, D]),
                                        ALU.mult).then_inc(key_done.sem, 1)
                dve.wait_ge(key_done.sem, key_done.at(b, 0))

                def step(k):
                    dve.wait_ge(key_step.sem, key_step.at(b, k))

                nc.vector.tensor_reduce(key[:, :], keyj[:, :, :], AX.X, ALU.add).then_inc(key_step.sem, 1)
                step(0)
                nc.vector.tensor_scalar(keyb[:, :], key[:, :], rb[:, 0:1], None, ALU.add).then_inc(key_step.sem, 1)
                step(1)
                nc.vector.tensor_copy(keyi[:, :], keyb[:, :]).then_inc(key_step.sem, 1)
                step(2)
                nc.vector.tensor_copy(keyf[:, :], keyi[:, :]).then_inc(key_step.sem, 1)
                step(3)
                nc.vector.tensor_tensor(above[:, :], keyf[:, :], keyb[:, :], ALU.is_gt).then_inc(key_step.sem, 1)
                step(4)
                nc.vector.tensor_tensor(floori[:, :], keyf[:, :], above[:, :], ALU.subtract).then_inc(key_step.sem, 1)
                step(5)
                nc.vector.tensor_scalar(modi[:, :], floori[:, :], NE - 1, None, ALU.bitwise_and)\
                    .then_inc(key_step.sem, 1)
                step(6)
                nc.vector.tensor_copy(expert[:, bass.ds(b * TT, TT)], modi[:, :]).then_inc(key_step.sem, 1)

        @block.tensor
        def _(pe):
            xnT_ps.grant(pe)
            qS_ps.grant(pe)
            pv_done.grant(pe)
            pe.wait_ge(loads, LOADS)
            pe.wait_ge(scaled, 2)
            pe.wait_ge(zeroed, ZEROED)
            with pe.Fori(0, B) as b:
                pe.wait_ge(r1_done.sem, r1_done.at(b, -1))
                for t in range(TT):
                    pe.wait_ge(xn_done.sem, xn_done.at(b, t))
                    for c in range(KC):
                        last = nc.tensor.transpose(psR[:, c, t * P:(t + 1) * P], xn[:, t, c * P:(c + 1) * P],
                                                   idn[:, :])
                        if t == TT - 1:
                            last.then_inc(xnT_ps.sem, 1)
                pe.wait_ge(xnT_sb.sem, xnT_sb.at(b, KC - 1))
                for n in range(NB):
                    t, i = divmod(n, 2)
                    if n >= 4:
                        pe.wait_ge(bias_done.sem, bias_done.at(b, n - 4))
                    for c in range(KC):
                        rhs, wide = ((wqk[:, c, :], 2 * D), (wv[:, c, :], D))[i]
                        last = nc.tensor.matmul(psS[:, n % 4, 0:wide], xnT[:, c, t * P:(t + 1) * P], rhs,
                                                start=(c == 0), stop=(c == KC - 1))
                    last.then_inc(proj_ps.sem, 1)
                pe.wait_ge(lo_done.sem, lo_done.at(b, TT - 1))
                pe.wait_ge(neg_reset.sem, neg_reset.at(b, 0))
                pe.wait_ge(bias_done.sem, bias_done.at(b, NB - 1))

                def transpose_pair(bank, src, p):
                    for t in range(TT):
                        heads = src[:, t, 2 * p:2 * p + 2, :].rearrange("p h d -> p (h d)")
                        last = nc.tensor.transpose(psR[:, bank, t * P:(t + 1) * P], heads, idn[:, :])
                    return last

                def keys_and_queries(quad):
                    for p in (2 * quad, 2 * quad + 1):
                        transpose_pair(p % 2, k_tok, p).then_inc(kT_ps.sem, 1)
                    for p in (2 * quad, 2 * quad + 1):
                        pe.wait_ge(k_even.sem, k_even.at(b, p))
                        pe.wait_ge(k_odd.sem, k_odd.at(b, p))
                        transpose_pair(p % 2, q_tok, p).then_inc(qM_ps.sem, 1)

                def scores_for_max(m):
                    h, c = divmod(m, TT)
                    quad, k = divmod(m, MQ)
                    if k < 2:
                        pe.wait_ge(qM_done.sem, qM_done.at(b, 2 * quad + k))
                        pe.wait_ge(qM_done.sem, qM_done.at(b, 2 * quad))
                    elif k == MP or k == MP + 1:
                        if k == MP:
                            pe.wait_ge(max_done.sem, max_done.at(b, m - 1))
                        else:
                            pe.wait_ge(qS_done.sem, qS_done.at(b, 2 * quad))
                    else:
                        pe.wait_ge(max_done.sem, max_done.at(b, m - 2))
                    nc.tensor.matmul(psR[:, max_use(m) % 2, :], qM[:, h // 2 % 2, c * P:(c + 1) * P], kZ[:, h % 8, :],
                                     start=True, stop=True).then_inc(max_ps.sem, 1)

                def shifted(p):
                    quad, e = divmod(p, 2)
                    pe.wait_ge(max_done.sem, max_done.at(b, quad * MQ + (e + 1) * MP - 1))
                    transpose_pair(shifted_use(p) % 2, q_tok, p).then_inc(qS_ps.sem, 1)

                def scores(quad, u):
                    h, half = 4 * quad + u % 4, u // 4
                    pe.wait_ge(exp_done.sem, exp_done.at(b, UQ * quad + u - 2))
                    pe.wait_ge(qS_done.sem, qS_done.at(b, h // 2))
                    for a in range(2):
                        j = 2 * half + a
                        last = nc.tensor.matmul(psS[:, 2 * (u % 2) + a, :], kZ[:, h % 8, j * P:(j + 1) * P],
                                                qS[:, h // 2 % 4, :], start=True, stop=True)
                    last.then_inc(score_ps.sem, 1)

                def weigh_values(quad, half):
                    pe.wait_ge(exp_done.sem, exp_done.at(b, UQ * quad + 4 * half + 3))
                    if half == 0:
                        pe.wait_ge(norm_done.sem, norm_done.at(b, quad - 1))
                    for a in range(2):
                        j = 2 * half + a
                        for e in range(4):
                            last = nc.tensor.matmul(psO[32 * e:32 * e + 32, :], v[:, j, 4 * quad + e, :],
                                                    probs[:, 4 * half + e, a, :],
                                                    start=(j == 0), stop=(j == TT - 1), tile_position=(0, 32 * e))
                    last.then_inc(pv_done.sem, 1)

                keys_and_queries(0)
                for m in range(MP):
                    scores_for_max(m)
                shifted(0)
                for m in range(MP, MQ):
                    scores_for_max(m)
                shifted(1)
                pe.wait_ge(qS_done.sem, qS_done.at(b, 1))
                keys_and_queries(1)
                for quad in range(QUADS):
                    nxt = quad + 1 < QUADS
                    for u in range(UQ):
                        scores(quad, u)
                        if u == 5:
                            weigh_values(quad, 0)
                        if u == 1 and quad:
                            weigh_values(quad - 1, 1)
                        if nxt:
                            if u == 4:
                                shifted(2 * quad + 2)
                            for m in ((0, 1), (2, 3), (4, 5), (6, 7), (8, 9), (10, 11), (12, 13), (14, 15))[u]:
                                scores_for_max((quad + 1) * MQ + m)
                    if nxt:
                        shifted(2 * quad + 3)
                    if quad + 2 < QUADS:
                        pe.wait_ge(qS_done.sem, qS_done.at(b, 2 * quad + 3))
                        keys_and_queries(quad + 2)
                weigh_values(QUADS - 1, 1)
                pe.wait_ge(norm_done.sem, norm_done.at(b, QUADS - 1))
                for t in range(TT):
                    for quad in range(QUADS):
                        last = nc.tensor.matmul(psR[:, t // 2, (t % 2) * D:(t % 2 + 1) * D],
                                                oT[:, quad, t * P:(t + 1) * P], wo[:, quad, :],
                                                start=(quad == 0), stop=(quad == QUADS - 1))
                    if t % 2:
                        last.then_inc(out_ps.sem, 1)


def routing_phase(nc, expert, x1, before, tile_starts, place, tile_expert, sorted_x):
    CT = B * TT
    with ExitStack() as ctx:
        def sb(name, shape, dt=F32):
            return ctx.enter_context(nc.sbuf_tensor("r_" + name, shape, dt))

        tri = sb("tri", [P, P])
        starts = sb("starts", [P, TILES])
        ones = sb("ones", [P, P])
        zeros = sb("zeros", [P, D])
        hot = sb("hot", [P, NE, CT])
        total = sb("total", [P, NE * CT])
        upto = sb("upto", [P, NE * CT])
        ahead = sb("ahead", [P, NE * CT])
        count = sb("count", [P, NE])
        count_i = sb("count_i", [P, NE], I32)
        padded_i = sb("padded_i", [P, NE], I32)
        padded = sb("padded", [P, NE])
        end = sb("end", [P, NE])
        shift = sb("shift", [P, NE])
        row = sb("row", [P, NE, CT])
        row_f = sb("row_f", [P, CT])
        tile_f = sb("tile_f", [P, 2, TILES])
        psP = ctx.enter_context(nc.psum_tensor("r_psP", [P, NE * CT], F32))
        psT = ctx.enter_context(nc.psum_tensor("r_psT", [P, 512], F32))

        loads, consts, cleared, hot_done, sums_ps, chain, placed, scattered = (
            ctx.enter_context(nc.semaphore("r_" + n)) for n in
            ("loads", "consts", "cleared", "hot_done", "sums_ps", "chain", "placed", "scattered"))
        block = ctx.enter_context(nc.Block())

        @block.sync
        def _(sp):
            sp.dma_start(tri[:, :], before).then_inc(loads, 16)
            sp.dma_start(starts[:, :], tile_starts.partition_broadcast(P)).then_inc(loads, 16)
            sp.wait_ge(consts, 3)
            sp.dma_start(sorted_x.rearrange("(n p) d -> p n d", p=P),
                         zeros[:, :].unsqueeze(1).to_broadcast([P, TILES * TOK // P, D])).then_inc(cleared, 16)
            sp.wait_ge(cleared, 16)

        @block.gpsimd
        def _(pool):
            nc.gpsimd.memset(ones[:, :], 1.0).then_inc(consts, 1)
            nc.gpsimd.memset(zeros[:, :], 0.0).then_inc(consts, 1)
            nc.gpsimd.memset(shift[:, :], 0.0).then_inc(consts, 1)
            pool.wait_ge(cleared, 16)
            pool.wait_ge(placed, 1)
            for c in range(CT):
                nc.gpsimd.indirect_dma_start(
                    out=sorted_x, out_offset=bass.IndirectOffsetOnAxis(ap=place[:, c:c + 1], axis=0),
                    in_=x1[:, c, :], in_offset=None).then_inc(scattered, 16)
            pool.wait_ge(scattered, 16 * CT)

        @block.tensor
        def _(pe):
            pe.wait_ge(loads, 32)
            pe.wait_ge(consts, 3)
            pe.wait_ge(hot_done, NE)
            tokens = hot[:, :, :].rearrange("p e c -> p (e c)")
            nc.tensor.matmul(psP[:, :], tri[:, :], tokens, start=True, stop=True)
            nc.tensor.matmul(psT[:, 0:NE * CT], ones[:, :], tokens, start=True, stop=True).then_inc(sums_ps, 1)

        @block.vector
        def _(dve):
            steps = [0]

            def link(instruction):
                steps[0] += 1
                instruction.then_inc(chain, 1)
                dve.wait_ge(chain, steps[0])

            for e in range(NE):
                nc.vector.tensor_scalar(hot[:, e, :], expert[:, :], float(e), None, ALU.is_equal).then_inc(hot_done, 1)
            dve.wait_ge(sums_ps, 1)
            dve.wait_ge(consts, 3)
            dve.wait_ge(loads, 32)
            link(nc.vector.tensor_copy(total[:, :], psT[:, 0:NE * CT]))
            link(nc.vector.tensor_tensor_scan(upto[:, :], ones[:, :], total[:, :], 0.0, ALU.mult, ALU.add))
            link(nc.vector.tensor_tensor(ahead[:, :], upto[:, :], total[:, :], ALU.subtract))
            ends = upto[:, :].rearrange("p (e c) -> p e c", c=CT)[:, :, CT - 1]
            link(nc.vector.tensor_copy(count[:, 0:1], ends[:, 0:1]))
            link(nc.vector.tensor_tensor(count[:, 1:NE], ends[:, 1:NE], ends[:, 0:NE - 1], ALU.subtract))
            link(nc.vector.tensor_scalar(count_i[:, :], count[:, :], float(TOK - 1), None, ALU.add))
            bits = TOK.bit_length() - 1
            link(nc.vector.tensor_scalar(padded_i[:, :], count_i[:, :], bits, bits,
                                         ALU.logical_shift_right, ALU.logical_shift_left))
            link(nc.vector.tensor_copy(padded[:, :], padded_i[:, :]))
            link(nc.vector.tensor_tensor_scan(end[:, :], ones[:, 0:NE], padded[:, :], 0.0, ALU.mult, ALU.add))
            link(nc.vector.tensor_tensor(shift[:, 1:NE], end[:, 0:NE - 1], ends[:, 0:NE - 1], ALU.subtract))
            flat = row[:, :, :].rearrange("p e c -> p (e c)")
            link(nc.vector.tensor_tensor(flat, psP[:, :], ahead[:, :], ALU.add))
            link(nc.vector.tensor_tensor(row[:, :, :], row[:, :, :],
                                         shift[:, :].unsqueeze(2).to_broadcast([P, NE, CT]), ALU.add))
            link(nc.vector.tensor_tensor(row[:, :, :], row[:, :, :], hot[:, :, :], ALU.mult))
            link(nc.vector.tensor_reduce(row_f[:, :], row[:, :, :].rearrange("p e c -> p c e"), AX.X, ALU.add))
            link(nc.vector.tensor_copy(place[:, :], row_f[:, :]))
            link(nc.vector.tensor_scalar(tile_f[:, 0, :], starts[:, :], end[:, 0:1], None, ALU.is_ge))
            link(nc.vector.scalar_tensor_tensor(tile_f[:, 1, :], starts[:, :], end[:, 1:2], tile_f[:, 0, :],
                                                ALU.is_ge, ALU.add))
            link(nc.vector.scalar_tensor_tensor(tile_f[:, 0, :], starts[:, :], end[:, 2:3], tile_f[:, 1, :],
                                                ALU.is_ge, ALU.add))
            nc.vector.tensor_copy(tile_expert[:, :], tile_f[:, 0, :]).then_inc(placed, 1)


def experts_phase(nc, W1, b1, W2, b2, ident, tile_expert, sorted_x, sorted_y):
    MC = FF // P
    TC = TOK // P
    LOOPED = (TILES - 3) // 2
    with ExitStack() as ctx:
        def sb(name, shape, dt=F32):
            return ctx.enter_context(nc.sbuf_tensor("e_" + name, shape, dt))

        def sig(name, per, credit=0, step=1):
            return Signal(ctx, nc, "e_" + name, per, credit, step)

        idn = sb("idn", [P, P])
        w1 = sb("w1", [P, 2, KC, FF])
        w2 = sb("w2", [P, 2, MC, D])
        o1_rows = sb("o1_rows", [MC, 2, P])
        o1 = sb("o1", [P, 2, MC])
        o2 = sb("o2", [P, 2, D])
        xs = sb("xs", [P, 2, TC, D])
        xT = sb("xT", [P, 2, KC, TOK])
        hT = sb("hT", [P, 2, MC, TOK])
        y = sb("y", [P, 2, TC, D])
        psX = ctx.enter_context(nc.psum_tensor("e_psX", [P, 2, 512], F32))
        psH = ctx.enter_context(nc.psum_tensor("e_psH", [P, 4, 512], F32))
        psY = ctx.enter_context(nc.psum_tensor("e_psY", [P, 2, 512], F32))

        passed = ctx.enter_context(nc.semaphore("e_passed"))
        ident_in = ctx.enter_context(nc.semaphore("e_ident_in"))
        x_in = [sig(f"x_in{k}", 1, step=16) for k in range(2)]
        w_in = [sig(f"w_in{k}", 1, step=64) for k in range(2)]
        xT_ps = sig("xT_ps", 2)
        xT_sb = sig("xT_sb", 2)
        o1_ps = sig("o1_ps", 2)
        o1_sb = sig("o1_sb", 2)
        h_ps = sig("h_ps", MC)
        h_sb = sig("h_sb", MC, credit=4)
        y_ps = sig("y_ps", 2)
        y_sb = sig("y_sb", 2, credit=2)
        stored = [sig(f"stored{k}", 1, credit=1, step=16) for k in range(2)]
        x_tiles = sorted_x.rearrange("(i c p) d -> i p c d", p=P, c=TC)
        y_tiles = sorted_y.rearrange("(i c p) d -> i p c d", p=P, c=TC)
        block = ctx.enter_context(nc.Block())

        def tiles(engine, step):
            with engine.Fori(0, LOOPED) as i:
                for k in range(2):
                    step(i, k, True)
            for t in range(2 * LOOPED, TILES):
                step(t // 2, t % 2, t + 2 < TILES)

        @block.sync
        def _(sp):
            for s in stored:
                s.grant(sp)
            sp.dma_start(idn[:, :], ident).then_inc(ident_in, 16)

            def load(i, k):
                e = sp.value_load(tile_expert[0:1, bass.ds(2 * i + k, 1)], min_val=0, max_val=NE - 1)
                sp.dma_start(xs[:, k, :, :], x_tiles[2 * i + k]).then_inc(x_in[k].sem, 16)
                sp.dma_start(w1[:, k, :, :], W1[e].rearrange("(c p) n -> p c n", p=P)).then_inc(w_in[k].sem, 16)
                sp.dma_start(w2[:, k, :, :], W2[e].rearrange("(m p) n -> p m n", p=P)).then_inc(w_in[k].sem, 16)
                sp.dma_start(o1_rows[:, k, :], b1[e].rearrange("(m p) -> m p", p=P)).then_inc(w_in[k].sem, 16)
                sp.dma_start(o2[:, k, :], b2[e].partition_broadcast(P)).then_inc(w_in[k].sem, 16)

            def step(i, k, more):
                sp.wait_ge(y_sb.sem, y_sb.at(i, k))
                sp.dma_start(y_tiles[2 * i + k], y[:, k, :, :]).then_inc(stored[k].sem, 16)
                if more:
                    load(i + 1, k)

            load(0, 0)
            load(0, 1)
            tiles(sp, step)
            last = divmod(TILES - 1, 2)
            sp.wait_ge(stored[last[1]].sem, stored[last[1]].at(last[0], 0))
            sp.wait_ge(stored[1 - last[1]].sem, stored[1 - last[1]].at((TILES - 2) // 2, 0))

        @block.scalar
        def _(act):
            h_sb.grant(act)

            def step(i, k, more):
                act.wait_ge(o1_ps.sem, o1_ps.at(i, k))
                nc.scalar.copy(o1[:, k, :], psY[:, k, 0:MC]).then_inc(o1_sb.sem, 1)
                act.wait_ge(o1_sb.sem, o1_sb.at(i, k))
                for m in range(MC):
                    if m % 2 == 0:
                        act.wait_ge(h_ps.sem, h_ps.at(i, 4 * k + m // 2))
                    last = nc.scalar.activation(hT[:, k, m, :], psH[:, m // 2, m % 2 * TOK:(m % 2 + 1) * TOK],
                                                ACT.Relu, bias=o1[:, k, m:m + 1])
                    if m % 2:
                        last.then_inc(h_sb.sem, 1)

            tiles(act, step)

        @block.vector
        def _(dve):
            y_sb.grant(dve)

            def step(i, k, more):
                dve.wait_ge(xT_ps.sem, xT_ps.at(i, k))
                nc.vector.tensor_copy(xT[:, k, :, :].rearrange("p c n -> p (c n)"), psX[:, k, :])\
                    .then_inc(xT_sb.sem, 1)
                dve.wait_ge(y_ps.sem, y_ps.at(i, k))
                dve.wait_ge(stored[k].sem, stored[k].at(i, -1))
                offset = o2[:, k, :].unsqueeze(1).to_broadcast([P, TC, D])
                nc.vector.tensor_tensor(y[:, k, :, :], psY[:, k, :].rearrange("p (c n) -> p c n", c=TC), offset,
                                        ALU.add).then_inc(y_sb.sem, 1)

            tiles(dve, step)

        @block.tensor
        def _(pe):
            pe.wait_ge(ident_in, 16)

            def step(i, k, more):
                pe.wait_ge(x_in[k].sem, x_in[k].at(i, 0))
                for c in range(KC):
                    for t in range(TC):
                        last = nc.tensor.transpose(psX[:, k, c * TOK + t * P:c * TOK + (t + 1) * P],
                                                   xs[:, k, t, c * P:(c + 1) * P], idn[:, :])
                last.then_inc(xT_ps.sem, 1)
                pe.wait_ge(w_in[k].sem, w_in[k].at(i, 0))
                pe.wait_ge(y_sb.sem, y_sb.at(i, k - 2))
                pe.sem_inc(passed, 1)
                nc.tensor.transpose(psY[:, k, 0:MC], o1_rows[:, k, :], idn[0:MC, 0:MC]).then_inc(o1_ps.sem, 1)
                pe.wait_ge(xT_sb.sem, xT_sb.at(i, k))
                for m in range(MC):
                    if m % 2 == 0:
                        pe.wait_ge(h_sb.sem, h_sb.at(i, 4 * k + m // 2 - 4))
                    for c in range(KC):
                        last = nc.tensor.matmul(psH[:, m // 2, m % 2 * TOK:(m % 2 + 1) * TOK],
                                                w1[:, k, c, m * P:(m + 1) * P], xT[:, k, c, :],
                                                start=(c == 0), stop=(c == KC - 1))
                    if m % 2:
                        last.then_inc(h_ps.sem, 1)
                pe.wait_ge(h_sb.sem, h_sb.at(i, 4 * k + 3))
                for t in range(TC):
                    for m in range(MC):
                        last = nc.tensor.matmul(psY[:, k, t * D:(t + 1) * D], hT[:, k, m, t * P:(t + 1) * P],
                                                w2[:, k, m, :], start=(m == 0), stop=(m == MC - 1))
                last.then_inc(y_ps.sem, 1)

            tiles(pe, step)


def combine_phase(nc, x1, place, sorted_y, attended, gain, offset, out):
    CT = B * TT
    with ExitStack() as ctx:
        def sb(name, shape, dt=F32):
            return ctx.enter_context(nc.sbuf_tensor("c_" + name, shape, dt))

        def sig(name, per, credit=0, step=1):
            return Signal(ctx, nc, "c_" + name, per, credit, step)

        g2, b2 = sb("g2", [P, D]), sb("b2", [P, D])
        y = sb("y", [P, CT, D])
        r2 = sb("r2", [P, TT, D])
        scaled = sb("scaled", [P, TT, D])
        att = sb("att", [P, TT, D])
        res = sb("res", [P, TT, D])
        norm = LayerNorm(nc, ctx, "c_norm")
        loads = ctx.enter_context(nc.semaphore("c_loads"))
        gathered = ctx.enter_context(nc.semaphore("c_gathered"))
        att_in = sig("att_in", 1, step=16)
        r2_done = sig("r2_done", 1)
        n2_done = sig("n2_done", TT)
        gain_done = sig("gain_done", 1, credit=1)
        offset_done = sig("offset_done", 1)
        out_done = sig("out_done", 1, credit=1)
        stored = sig("stored", 1, credit=1, step=16)
        att_rows = attended.rearrange("b (t p) d -> b p t d", p=P)
        out_rows = out.rearrange("b (t p) d -> b p t d", p=P)
        block = ctx.enter_context(nc.Block())

        @block.sync
        def _(sp):
            stored.grant(sp)
            sp.dma_start(g2[:, :], gain.partition_broadcast(P)).then_inc(loads, 16)
            sp.dma_start(b2[:, :], offset.partition_broadcast(P)).then_inc(loads, 16)
            with sp.Fori(0, B) as b:
                sp.wait_ge(out_done.sem, out_done.at(b, -1))
                sp.dma_start(att[:, :, :], att_rows[b]).then_inc(att_in.sem, 16)
                sp.wait_ge(out_done.sem, out_done.at(b, 0))
                sp.dma_start(out_rows[b], res[:, :, :]).then_inc(stored.sem, 16)
            sp.wait_ge(stored.sem, stored.at(B - 1, 0))

        @block.gpsimd
        def _(pool):
            gain_done.grant(pool)
            norm.set_power(pool)
            pool.wait_ge(loads, 32)
            for c in range(CT):
                nc.gpsimd.indirect_dma_start(
                    out=y[:, c, :], out_offset=None, in_=sorted_y,
                    in_offset=bass.IndirectOffsetOnAxis(ap=place[:, c:c + 1], axis=0)).then_inc(gathered, 16)
            wide = [P, TT, D]
            with pool.Fori(0, B) as b:
                norm.raise_variance(pool, b)
                pool.wait_ge(n2_done.sem, n2_done.at(b, TT - 1))
                pool.wait_ge(out_done.sem, out_done.at(b, -1))
                nc.gpsimd.tensor_tensor(scaled[:, :, :], r2[:, :, :], g2[:, :].unsqueeze(1).to_broadcast(wide),
                                        ALU.mult).then_inc(gain_done.sem, 1)
                pool.wait_ge(gain_done.sem, gain_done.at(b, 0))
                nc.gpsimd.tensor_tensor(scaled[:, :, :], scaled[:, :, :], b2[:, :].unsqueeze(1).to_broadcast(wide),
                                        ALU.add).then_inc(offset_done.sem, 1)

        @block.vector
        def _(dve):
            out_done.grant(dve)
            dve.wait_ge(gathered, 16 * CT)
            with dve.Fori(0, B) as b:
                tiles = bass.ds(b * TT, TT)
                dve.wait_ge(gain_done.sem, gain_done.at(b, -1))
                nc.vector.tensor_tensor(r2[:, :, :], x1[:, tiles, :], y[:, tiles, :], ALU.add).then_inc(r2_done.sem, 1)
                dve.wait_ge(r2_done.sem, r2_done.at(b, 0))
                norm.statistics(dve, b, r2)
                norm.apply(dve, b, r2, r2, n2_done)
                dve.wait_ge(offset_done.sem, offset_done.at(b, 0))
                dve.wait_ge(att_in.sem, att_in.at(b, 0))
                dve.wait_ge(stored.sem, stored.at(b, -1))
                nc.vector.tensor_tensor(res[:, :, :], scaled[:, :, :], att[:, :, :], ALU.add).then_inc(out_done.sem, 1)


def shape_constants():
    import numpy as np

    inv_freq = 1.0 / np.float32(10000.0) ** (np.arange(0, HD, 2, dtype=np.float32) / np.float32(HD))
    angle = (np.arange(S, dtype=np.float32)[:, None] * inv_freq.astype(np.float32)[None, :]).astype(np.float32)
    cos, sin = np.cos(angle).astype(np.float32), np.sin(angle).astype(np.float32)
    scale = np.float32(HD ** -0.5)
    start = 2.0 ** (-2.0 ** (-(np.log2(H) - 3)))
    slopes = np.array([start * start ** i for i in range(H)], np.float32)
    high = (slopes.view(np.uint32) & np.uint32(0xFFFFF000)).view(np.float32)
    pos = np.arange(S, dtype=np.float32)
    return {
        "rope": np.stack([cos * scale, -sin * scale, sin * scale, cos, -sin, sin]),
        "slopes": slopes,
        "slope_parts": np.stack([high, slopes - high], 1),
        "key_rows": np.stack([np.ones_like(pos), pos, pos]),
        "before": np.triu(np.ones((P, P), np.float32), 1),
        "tile_starts": np.arange(TILES, dtype=np.float32) * TOK,
        "ident": np.eye(P, dtype=np.float32),
    }


_INS = ["L0_attn_x", "L0_attn_Wq", "L0_attn_Wk", "L0_attn_Wv", "L0_attn_Wo", "L0_ffn_Wq", "L0_ffn_bq", "L0_ffn_Wk",
        "L0_ffn_bk", "L0_ffn_Wv", "L0_ffn_bv", "L0_ffn_Wo", "L0_ffn_bo", "L0_ffn_router_w", "L0_ffn_router_b",
        "L0_ffn_W1", "L0_ffn_b1", "L0_ffn_W2", "L0_ffn_b2", "L0_ffn_ln1_g", "L0_ffn_ln1_b", "L0_ffn_ln2_g",
        "L0_ffn_ln2_b"]


def block_program(nc, ins, consts, out):
    x = ins["L0_attn_x"]
    w = {n[len("L0_ffn_"):]: ap for n, ap in ins.items() if n.startswith("L0_ffn_")}
    attended = nc.dram_tensor("attended", (B, S, D), F32, kind="Internal").ap()
    sorted_x = nc.dram_tensor("sorted_x", (TILES * TOK, D), F32, kind="Internal").ap()
    sorted_y = nc.dram_tensor("sorted_y", (TILES * TOK, D), F32, kind="Internal").ap()
    rotary_attention_phase(nc, x, *(ins["L0_attn_" + n] for n in ("Wq", "Wk", "Wv", "Wo")), consts["rope"],
                           consts["slopes"], consts["slope_parts"], consts["key_rows"], consts["ident"], attended)
    with ExitStack() as ctx:
        def sb(name, shape, dt):
            return ctx.enter_context(nc.sbuf_tensor(name, shape, dt))

        x1 = sb("x1", [P, B * TT, D], F32)
        expert = sb("expert", [P, B * TT], F32)
        place = sb("place", [P, B * TT], I32)
        tile_expert = sb("tile_expert", [P, TILES], I32)
        plain_attention_phase(nc, x, w, consts["ident"], expert, x1)
        routing_phase(nc, expert, x1, consts["before"], consts["tile_starts"], place, tile_expert, sorted_x)
        experts_phase(nc, w["W1"], w["b1"], w["W2"], w["b2"], consts["ident"], tile_expert, sorted_x, sorted_y)
        combine_phase(nc, x1, place, sorted_y, attended, w["ln2_g"], w["ln2_b"], out)


def kernel(**inputs):
    import numpy as np
    import concourse.bacc as bacc
    from concourse.bass_utils import run_bass_kernel_spmd

    nc = bacc.Bacc("TRN2", target_bir_lowering=False, num_devices=1)
    arrays = {}

    def argument(name, a):
        a = np.ascontiguousarray(a)
        arrays[f"in_{name}"] = a
        return nc.dram_tensor(f"in_{name}", a.shape, mybir.dt.from_np(a.dtype), kind="ExternalInput").ap()

    ins = {name: argument(name, inputs[name]) for name in _INS}
    consts = {name: argument(name, a) for name, a in shape_constants().items()}
    out = nc.dram_tensor("out_0", (B, S, D), F32, kind="ExternalOutput").ap()
    block_program(nc, ins, consts, out)
    result = run_bass_kernel_spmd(nc, [arrays], core_ids=[0])
    return np.array(result.results[0]["out_0"])
```

```python
from contextlib import ExitStack

import concourse.bass as bass
from concourse import mybir

F32 = mybir.dt.float32
F32R = mybir.dt.float32r
BF16 = mybir.dt.bfloat16
I32 = mybir.dt.int32
ALU = mybir.AluOpType
ACT = mybir.ActivationFunctionType
AX = mybir.AxisListType

P = 128
B = 8
S = 512
D = 256
TT = S // P
KC = D // P
H = 16
EPS = 1e-5

HD = 64
KV = 4
GRP = H // KV
PAIRS = H // 2
XR = HD + 3
XRP = XR + 1

FH = D // H
FB = 64
FF = 1024
NE = 4
TOK = 256
TILES = (B * S - NE) // TOK + NE


class Signal:

    def __init__(self, ctx, nc, name, per, credit=0, step=1):
        self.sem = ctx.enter_context(nc.semaphore(name))
        self.per, self.credit, self.step = per, credit, step

    def at(self, b, n):
        return b * (self.per * self.step) + (self.credit + n + 1) * self.step

    def grant(self, eng):
        eng.sem_inc(self.sem, self.credit * self.step)


class LayerNorm:

    def __init__(self, nc, ctx, name, count=TT, turns=1):
        def sb(what, shape):
            return ctx.enter_context(nc.sbuf_tensor(f"{name}_{what}", shape, F32))

        self.nc, self.count = nc, count
        self.stats, self.aggr = sb("stats", [P, count, 6]), sb("aggr", [P, count, 2])
        self.var_eps, self.rstd, self.power = (sb(what, [P, count]) for what in ("var_eps", "rstd", "power"))
        self.stats_done = Signal(ctx, nc, f"{name}_stats_done", count * turns)
        self.aggr_done = Signal(ctx, nc, f"{name}_aggr_done", count * turns)
        self.var_done = Signal(ctx, nc, f"{name}_var_done", turns)
        self.rstd_done = Signal(ctx, nc, f"{name}_rstd_done", turns)
        self.passed = ctx.enter_context(nc.semaphore(f"{name}_passed"))
        self.power_set = ctx.enter_context(nc.semaphore(f"{name}_power_set"))

    def set_power(self, pool):
        self.nc.gpsimd.memset(self.power[:, :], -0.5).then_inc(self.power_set, 1)
        pool.wait_ge(self.power_set, 1)

    def raise_variance(self, pool, b, turn=0):
        pool.wait_ge(self.var_done.sem, self.var_done.at(b, turn))
        self.nc.gpsimd.tensor_tensor(self.rstd[:, :], self.var_eps[:, :], self.power[:, :],
                                     ALU.pow).then_inc(self.rstd_done.sem, 1)

    def statistics(self, dve, b, src, turn=0):
        for t in range(self.count):
            self.nc.vector.bn_stats(self.stats[:, t, :], src[:, t, :]).then_inc(self.stats_done.sem, 1)
        for t in range(self.count):
            dve.wait_ge(self.stats_done.sem, self.stats_done.at(b, self.count * turn + t))
            dve.sem_inc(self.passed, 1)
            self.nc.vector.bn_aggr(self.aggr[:, t, :], self.stats[:, t, :]).then_inc(self.aggr_done.sem, 1)
        dve.wait_ge(self.aggr_done.sem, self.aggr_done.at(b, self.count * turn + self.count - 1))
        self.nc.vector.tensor_scalar(self.var_eps[:, :], self.aggr[:, :, 1], EPS, None,
                                     ALU.add).then_inc(self.var_done.sem, 1)

    def apply(self, dve, b, src, dst, applied, turn=0):
        dve.wait_ge(self.rstd_done.sem, self.rstd_done.at(b, turn))
        for t in range(self.count):
            self.nc.vector.tensor_scalar(dst[:, t, :], src[:, t, :], self.aggr[:, t, 0:1], self.rstd[:, t:t + 1],
                                         ALU.subtract, ALU.mult).then_inc(applied.sem, 1)


def rotary_attention_phase(nc, x, Wq, Wk, Wv, Wo, rope, slopes, slope_parts, key_rows, ident, place, sorted_z,
                           result):
    QB = H * HD // 512
    NB = TT * (QB + 1)
    MU = 2 * TT
    RG = 4
    AHEAD = 3
    KEYS_AFTER = (5, 6, 7, 8)
    FIRST_AFTER = 9
    MAXES_AFTER = (10, 11)
    NORM_AT = 5
    with ExitStack() as ctx:
        def sb(name, shape, dt=F32):
            return ctx.enter_context(nc.sbuf_tensor("a_" + name, shape, dt))

        def ps(name, shape):
            return ctx.enter_context(nc.psum_tensor("a_" + name, shape, F32))

        def sig(name, per, credit=0, step=1):
            return Signal(ctx, nc, "a_" + name, per, credit, step)

        wq = sb("wq", [P, KC, H * HD])
        wkv = sb("wkv", [P, KC, 2 * KV * HD])
        wo = sb("wo", [P, PAIRS, D])
        rope_t = sb("rope_t", [P, 6, TT, HD // 2])
        alibi = sb("alibi", [P, H, S], BF16)
        idn = sb("idn", [P, P])
        ones = sb("ones", [P, HD])
        minus = sb("minus", [P, TT])
        xn = sb("xn", [P, TT, D])
        norm = LayerNorm(nc, ctx, "a_norm")
        xnT = sb("xnT", [P, KC, S])
        q_tok = sb("q_tok", [P, TT, H, HD + XRP])
        k_tok = sb("k_tok", [P, TT, KV, 3, HD])
        v = sb("v", [P, TT, KV * HD])
        kA = sb("kA", [P, KV, S], F32R)
        kB = sb("kB", [XR, KV, S], F32R)
        qA = sb("qA", [P, RG, S], F32R)
        qB = sb("qB", [XR, RG, S], F32R)
        probs = sb("probs", [P, 8, 2, S])
        rot_c = probs[:, 0:2, 0, :]
        rot_s = probs[:, 2:4, 0, :]
        rot = probs[:, 4:6, 0, :]
        maxes = sb("maxes", [P, H, TT])
        junk = sb("junk", [P, 2, S], BF16)
        den = sb("den", [P, S])
        rden = sb("rden", [P, S])
        oT = sb("oT", [P, PAIRS, S])
        acc = sb("acc", [P, TT, D])
        fed = sb("fed", [P, TT, D])
        rows_of = sb("rows_of", [P, TT], I32)

        psS = ps("psS", [P, 4, S])
        psR = ps("psR", [P, 2, S])
        psO = ps("psO", [P, S])
        psD = ps("psD", [P, S])

        loads = ctx.enter_context(nc.semaphore("a_loads"))
        rows_made = ctx.enter_context(nc.semaphore("a_rows_made"))
        alibi_made = ctx.enter_context(nc.semaphore("a_alibi_made"))
        passed = ctx.enter_context(nc.semaphore("a_passed"))
        ones_made = ctx.enter_context(nc.semaphore("a_ones_made"))
        LOADS = (14 + TT) * 16
        x_in = sig("x_in", 1, step=16)
        xn_done = sig("xn_done", TT)
        xnT_ps = sig("xnT_ps", KC, credit=1)
        xnT_sb = sig("xnT_sb", KC)
        proj_ps = sig("proj_ps", NB)
        rot_mul = sig("rot_mul", NB)
        rot_half = sig("rot_half", NB)
        rot_sum = sig("rot_sum", NB, credit=2)
        hi_done = sig("hi_done", NB)
        lo_done = sig("lo_done", NB, credit=2)
        v_done = sig("v_done", TT)
        kT_ps = sig("kT_ps", 2 * KV)
        kA_done = sig("kA_done", KV)
        kB_done = sig("kB_done", KV)
        qAT_ps = sig("qAT_ps", H)
        qA_done = sig("qA_done", H)
        max_ps = sig("max_ps", PAIRS * MU)
        max_done = sig("max_done", PAIRS * MU, credit=2)
        neg_done = sig("neg_done", H)
        qBT_ps = sig("qBT_ps", H)
        qB_done = sig("qB_done", H)
        score_ps = sig("score_ps", 2 * H)
        exp_done = sig("exp_done", 2 * H, credit=2)
        pv_done = sig("pv_done", H, credit=4)
        o_taken = sig("o_taken", PAIRS, credit=1)
        rden_done = sig("rden_done", PAIRS, credit=1)
        norm_done = sig("norm_done", PAIRS, credit=1)
        out_ps = sig("out_ps", 2)
        acc_done = sig("acc_done", 2, credit=1)
        res_in = sig("res_in", 1, step=16)
        rows_known = sig("rows_known", 1)
        fed_in = sig("fed_in", TT, step=16)
        fed_added = sig("fed_added", 1, credit=1)
        stored = sig("stored", 1, credit=1, step=16)

        def bank_of(n):
            return (n, None, KV * HD) if n < TT else (n % TT, n // TT - 1, 512)

        rows = x.rearrange("b (t p) d -> b p t d", p=P)
        out_rows = result.rearrange("b (t p) d -> b p t d", p=P)
        block = ctx.enter_context(nc.Block())

        @block.sync
        def _(sp):
            stored.grant(sp)
            sp.dma_start(idn[:, :], ident).then_inc(loads, 16)
            sp.dma_start(wq[:, :, :], Wq.rearrange("(c p) n -> p c n", p=P)).then_inc(loads, 16)
            sp.dma_start(wkv[:, :, 0:KV * HD], Wk.rearrange("(c p) n -> p c n", p=P)).then_inc(loads, 16)
            sp.dma_start(wkv[:, :, KV * HD:], Wv.rearrange("(c p) n -> p c n", p=P)).then_inc(loads, 16)
            sp.dma_start(wo[:, :, :], Wo.rearrange("(c p) n -> p c n", p=P)).then_inc(loads, 16)
            for k in range(6):
                sp.dma_start(rope_t[:, k, :, :], rope[k].rearrange("(t p) n -> p t n", p=P)).then_inc(loads, 16)
            for t in range(TT):
                sp.dma_start(q_tok[:, t, :, 2 * HD + 1:HD + XR], slope_parts.partition_broadcast(P)).then_inc(loads, 16)
            sp.dma_start(acc[:, 0, 0:H], slopes.partition_broadcast(P)).then_inc(loads, 16)
            sp.dma_start(probs[:, 0, 0, :], key_rows[1].partition_broadcast(P)).then_inc(loads, 16)
            sp.dma_start(probs[HD:XR, 1, 0, :], key_rows).then_inc(loads, 16)
            sp.wait_ge(alibi_made, H)
            sp.dma_start(xn[:, :, :], rows[0]).then_inc(x_in.sem, 16)

            def batch(b, following):
                sp.wait_ge(xnT_ps.sem, xnT_ps.at(b, KC - 1))
                sp.dma_start(xn[:, :, :], rows[following]).then_inc(x_in.sem, 16)
                sp.wait_ge(stored.sem, stored.at(b, -1))
                sp.dma_start(acc[:, :, :], rows[b]).then_inc(res_in.sem, 16)
                sp.wait_ge(acc_done.sem, acc_done.at(b, 1))
                sp.dma_start(out_rows[b], acc[:, :, :]).then_inc(stored.sem, 16)

            with sp.Fori(0, B - 1) as b:
                batch(b, b + 1)
            batch(B - 1, B - 1)
            sp.wait_ge(stored.sem, stored.at(B - 1, 0))

        @block.gpsimd
        def _(pool):
            rot_sum.grant(pool)
            lo_done.grant(pool)
            norm_done.grant(pool)
            fed_added.grant(pool)
            nc.gpsimd.memset(ones[:, :], 1.0).then_inc(ones_made, 1)
            nc.gpsimd.memset(minus[:, :], -1.0).then_inc(ones_made, 1)
            pool.wait_ge(ones_made, 2)
            norm.set_power(pool)
            pool.wait_ge(loads, LOADS)
            def rotate(b, n):
                t, i, w = bank_of(n)
                pool.wait_ge(rot_half.sem, rot_half.at(b, n))
                pool.wait_ge(lo_done.sem, lo_done.at(b, n - 2))
                nc.gpsimd.tensor_tensor(rot[:, n % 2, 0:w], rot_c[:, n % 2, 0:w], rot_s[:, n % 2, 0:w],
                                        ALU.add).then_inc(rot_sum.sem, 1)
                pool.wait_ge(hi_done.sem, hi_done.at(b, n))
                src = rot[:, n % 2, 0:w].rearrange("p (h d) -> p h d", d=HD)
                if i is None:
                    low, high = k_tok[:, t, :, 0, :], k_tok[:, t, :, 1, :]
                else:
                    hs = slice(i * 8, i * 8 + 8)
                    low, high = q_tok[:, t, hs, 0:HD], q_tok[:, t, hs, HD:2 * HD]
                nc.gpsimd.tensor_tensor(low, src, high, ALU.subtract).then_inc(lo_done.sem, 1)

            def gather_fed(b):
                pool.wait_ge(fed_added.sem, fed_added.at(b, -1))
                pool.sem_inc(passed, 1)
                nc.gpsimd.tensor_copy(rows_of[:, :], place[:, bass.ds(b * TT, TT)]).then_inc(rows_known.sem, 1)
                pool.wait_ge(rows_known.sem, rows_known.at(b, 0))
                pool.sem_inc(passed, 1)
                for t in range(TT):
                    nc.gpsimd.indirect_dma_start(
                        out=fed[:, t, :], out_offset=None, in_=sorted_z,
                        in_offset=bass.IndirectOffsetOnAxis(ap=rows_of[:, t:t + 1], axis=0))\
                        .then_inc(fed_in.sem, 16)

            def add_fed(b):
                pool.wait_ge(fed_in.sem, fed_in.at(b, TT - 1))
                pool.wait_ge(res_in.sem, res_in.at(b, 0))
                nc.gpsimd.tensor_tensor(acc[:, :, :], acc[:, :, :], fed[:, :, :], ALU.add).then_inc(fed_added.sem, 1)

            def negate(b, p):
                for h in (2 * p, 2 * p + 1):
                    pool.wait_ge(max_done.sem, max_done.at(b, TT * h + TT - 1))
                    nc.gpsimd.tensor_tensor(q_tok[:, :, h, 2 * HD], maxes[:, h, :], minus[:, :],
                                            ALU.mult).then_inc(neg_done.sem, 1)

            def normalize(b, p):
                pool.wait_ge(rden_done.sem, rden_done.at(b, p))
                nc.gpsimd.tensor_tensor(oT[:, p, :], oT[:, p, :], rden[:, :], ALU.mult).then_inc(norm_done.sem, 1)

            norm.raise_variance(pool, 0)
            for n in range(AHEAD):
                rotate(0, n)
            with pool.Fori(0, B) as b:
                for n in range(AHEAD, NB):
                    rotate(b, n)
                negate(b, 0)
                for p in range(PAIRS):
                    if p + 1 < PAIRS:
                        negate(b, p + 1)
                    if p > 0:
                        normalize(b, p - 1)
                    if p == 0:
                        gather_fed(b)
                    if p == NORM_AT:
                        norm.raise_variance(pool, b + 1)
                        add_fed(b)
                for n in range(AHEAD):
                    if n == 1:
                        normalize(b, PAIRS - 1)
                    rotate(b + 1, n)

        @block.scalar
        def _(act):
            exp_done.grant(act)
            o_taken.grant(act)
            act.wait_ge(loads, LOADS)
            for g in range(KV):
                nc.scalar.copy(kB[HD:XR, g, :], probs[HD:XR, 1, 0, :]).then_inc(rows_made, 1)
            act.wait_ge(rows_made, KV)
            act.wait_ge(alibi_made, H)
            def take_xnT(b):
                for c in range(KC):
                    act.wait_ge(xnT_ps.sem, xnT_ps.at(b, c))
                    nc.scalar.copy(xnT[:, c, :], psR[:, c, :]).then_inc(xnT_sb.sem, 1)

            def high_part(b, n):
                t, i, w = bank_of(n)
                if i is None:
                    act.wait_ge(rot_half.sem, rot_half.at(b, n))
                    nc.scalar.copy(v[:, t, :], psS[:, n % 4, KV * HD:]).then_inc(v_done.sem, 1)
                act.wait_ge(rot_sum.sem, rot_sum.at(b, n))
                src = rot[:, n % 2, 0:w].rearrange("p (h d) -> p h d", d=HD)
                if i is None:
                    high = k_tok[:, t, :, 1:3, :]
                    src = src.unsqueeze(2).to_broadcast([P, KV, 2, HD])
                else:
                    high = q_tok[:, t, i * 8:i * 8 + 8, HD:2 * HD]
                nc.scalar.copy(high.bitcast(F32R), src).then_inc(hi_done.sem, 1)

            def take_kA(b, g):
                act.wait_ge(kT_ps.sem, kT_ps.at(b, 2 * g))
                nc.scalar.copy(kA[:, g, :], psR[:, 0, :]).then_inc(kA_done.sem, 1)

            def take_qA(b, p):
                for h in (2 * p, 2 * p + 1):
                    act.wait_ge(qAT_ps.sem, qAT_ps.at(b, h))
                    nc.scalar.copy(qA[:, h % RG, :], psR[:, h % 2, :]).then_inc(qA_done.sem, 1)

            def take_qB(b, p):
                for h in (2 * p, 2 * p + 1):
                    act.wait_ge(qBT_ps.sem, qBT_ps.at(b, h))
                    nc.scalar.copy(qB[:, h % RG, :], psR[0:XR, h % 2, :]).then_inc(qB_done.sem, 1)

            def take_output(b, p):
                act.wait_ge(pv_done.sem, pv_done.at(b, 2 * p + 1))
                nc.scalar.copy(oT[:, p, :], psO[:, :])
                act.wait_ge(rden_done.sem, rden_done.at(b, p - 1))
                nc.scalar.copy(den[:, :], psD[:, :]).then_inc(o_taken.sem, 1)

            take_xnT(0)
            for n in range(AHEAD):
                high_part(0, n)
            with act.Fori(0, B) as b:
                for n in range(AHEAD, NB):
                    high_part(b, n)
                    if n in KEYS_AFTER:
                        take_kA(b, KEYS_AFTER.index(n))
                    if n == FIRST_AFTER:
                        take_qA(b, 0)
                take_qB(b, 0)
                take_qA(b, 1)
                for p in range(PAIRS):
                    for u in range(4):
                        i = 4 * p + u
                        act.wait_ge(score_ps.sem, score_ps.at(b, i))
                        act.wait_ge(pv_done.sem, pv_done.at(b, 2 * (p - 2) + u // 2))
                        nc.scalar.activation(probs[:, i % 8, :, :], psS[:, 2 * (u % 2):2 * (u % 2) + 2, :],
                                             ACT.Exp).then_inc(exp_done.sem, 1)
                        if u == 1 and p > 0:
                            take_output(b, p - 1)
                    if p + 1 < PAIRS:
                        take_qB(b, p + 1)
                    if p + 2 < PAIRS:
                        take_qA(b, p + 2)
                take_output(b, PAIRS - 1)
                take_xnT(b + 1)
                for n in range(AHEAD):
                    high_part(b + 1, n)

        @block.vector
        def _(dve):
            max_done.grant(dve)
            rden_done.grant(dve)
            acc_done.grant(dve)
            dve.wait_ge(loads, LOADS)
            for h in range(H):
                nc.vector.tensor_scalar(alibi[:, h, :], probs[:, 0, 0, :], acc[:, 0, h:h + 1], None,
                                        ALU.mult).then_inc(alibi_made, 1)
            dve.wait_ge(alibi_made, H)
            dve.wait_ge(rows_made, KV)
            def rotate(b, n):
                t, i, w = bank_of(n)
                k, hw = (3 if i is None else 0), w // (HD // 2)
                dve.wait_ge(proj_ps.sem, proj_ps.at(b, n))
                dve.wait_ge(rot_sum.sem, rot_sum.at(b, n - 2))
                halves = psS[:, n % 4, 0:w].rearrange("p (h d) -> p h d", d=HD // 2)
                cos = rope_t[:, k, t, :].unsqueeze(1).to_broadcast([P, hw, HD // 2])
                nc.vector.tensor_tensor(rot_c[:, n % 2, 0:w].rearrange("p (h d) -> p h d", d=HD // 2),
                                        halves, cos, ALU.mult).then_inc(rot_mul.sem, 1)
                pairs = psS[:, n % 4, 0:w].rearrange("p (h a d) -> p h a d", a=2, d=HD // 2)
                out = rot_s[:, n % 2, 0:w].rearrange("p (h a d) -> p h a d", a=2, d=HD // 2)
                for a in range(2):
                    sin = rope_t[:, k + 1 + a, t, :].unsqueeze(1).to_broadcast([P, hw // 2, HD // 2])
                    last = nc.vector.tensor_tensor(out[:, :, a, :], pairs[:, :, 1 - a, :], sin, ALU.mult)
                last.then_inc(rot_half.sem, 1)

            def take_kB(b, g):
                dve.wait_ge(kT_ps.sem, kT_ps.at(b, 2 * g + 1))
                nc.vector.tensor_copy(kB[0:HD, g, :], psR[0:HD, 1, :]).then_inc(kB_done.sem, 1)

            def take_max(b, m):
                h, c = divmod(m, TT)
                dve.wait_ge(max_ps.sem, max_ps.at(b, m))
                dve.wait_ge(max_done.sem, max_done.at(b, m - 2))
                dve.sem_inc(passed, 1)
                nc.vector.tensor_tensor_reduce(
                    out=junk[:, m % 2, :], in0=psR[:, m % 2, :], in1=alibi[:, h, :], scale=1.0,
                    scalar=-3.0e38, op0=ALU.add, op1=ALU.max,
                    accum_out=maxes[:, h, c:c + 1]).then_inc(max_done.sem, 1)

            def invert_sums(b, p):
                dve.wait_ge(o_taken.sem, o_taken.at(b, p))
                dve.wait_ge(norm_done.sem, norm_done.at(b, p - 1))
                nc.vector.reciprocal(rden[:, :], den[:, :]).then_inc(rden_done.sem, 1)

            dve.wait_ge(x_in.sem, x_in.at(0, 0))
            norm.statistics(dve, 0, xn)
            norm.apply(dve, 0, xn, xn, xn_done)
            for n in range(AHEAD):
                rotate(0, n)
            with dve.Fori(0, B) as b:
                for n in range(AHEAD, NB):
                    rotate(b, n)
                    if n in KEYS_AFTER:
                        take_kB(b, KEYS_AFTER.index(n))
                    if n in MAXES_AFTER:
                        for m in range(4):
                            take_max(b, 4 * MAXES_AFTER.index(n) + m)
                for p in range(PAIRS):
                    if p + 1 < PAIRS:
                        for m in range(MU):
                            take_max(b, (p + 1) * MU + m)
                    if p > 0:
                        invert_sums(b, p - 1)
                    if p == NORM_AT:
                        dve.wait_ge(x_in.sem, x_in.at(b + 1, 0))
                        norm.statistics(dve, b + 1, xn)
                        norm.apply(dve, b + 1, xn, xn, xn_done)
                invert_sums(b, PAIRS - 1)
                for n in range(AHEAD):
                    rotate(b + 1, n)
                dve.wait_ge(fed_added.sem, fed_added.at(b, 0))
                for k, bank in enumerate((psO, psD)):
                    dve.wait_ge(out_ps.sem, out_ps.at(b, k))
                    nc.vector.tensor_tensor(acc[:, 2 * k:2 * k + 2, :], acc[:, 2 * k:2 * k + 2, :],
                                            bank[:, :].rearrange("p (t d) -> p t d", d=D),
                                            ALU.add).then_inc(acc_done.sem, 1)

        @block.tensor
        def _(pe):
            xnT_ps.grant(pe)
            pv_done.grant(pe)
            pe.wait_ge(loads, LOADS)
            pe.wait_ge(ones_made, 1)
            pe.wait_ge(rows_made, KV)
            def transpose_rows(b):
                for t in range(TT):
                    pe.wait_ge(xn_done.sem, xn_done.at(b, t))
                    for c in range(KC):
                        last = nc.tensor.transpose(psR[:, c, t * P:(t + 1) * P], xn[:, t, c * P:(c + 1) * P],
                                                   idn[:, :])
                        if t == TT - 1:
                            last.then_inc(xnT_ps.sem, 1)

            def project(b, n):
                t, i, w = bank_of(n)
                if n == 0:
                    pe.wait_ge(xnT_sb.sem, xnT_sb.at(b, KC - 1))
                if n >= 4:
                    pe.wait_ge(rot_half.sem, rot_half.at(b, n - 4))
                    if n - 4 < TT:
                        pe.wait_ge(v_done.sem, v_done.at(b, n - 4))
                for c in range(KC):
                    rhs = wkv[:, c, :] if i is None else wq[:, c, i * 512:(i + 1) * 512]
                    last = nc.tensor.matmul(psS[:, n % 4, :], xnT[:, c, t * P:(t + 1) * P], rhs,
                                            start=(c == 0), stop=(c == KC - 1))
                last.then_inc(proj_ps.sem, 1)

            def transpose_keys(b, g):
                if g == 0:
                    pe.wait_ge(lo_done.sem, lo_done.at(b, TT - 1))
                for bank, first, taken in ((0, 1, kA_done), (1, 0, kB_done)):
                    if g > 0:
                        pe.wait_ge(taken.sem, taken.at(b, g - 1))
                    for t in range(TT):
                        src = k_tok[:, t, g, first:first + 2, :].rearrange("p a d -> p (a d)")
                        last = nc.tensor.transpose(psR[:, bank, t * P:(t + 1) * P], src, idn[:, :])
                    last.then_inc(kT_ps.sem, 1)

            def transpose_queries(b, h):
                for t in range(TT):
                    last = nc.tensor.transpose(psR[:, h % 2, t * P:(t + 1) * P],
                                               q_tok[:, t, h, 0:2 * HD], idn[:, :])
                last.then_inc(qAT_ps.sem, 1)

            def transpose_shifted(b, h):
                pe.wait_ge(max_done.sem, max_done.at(b, (h // 2 + 1) * MU - 2 + h % 2))
                pe.wait_ge(neg_done.sem, neg_done.at(b, h))
                for t in range(TT):
                    last = nc.tensor.transpose(psR[0:XR, h % 2, t * P:(t + 1) * P],
                                               q_tok[:, t, h, HD:HD + XR], idn[:, :])
                last.then_inc(qBT_ps.sem, 1)

            def scores_for_max(b, m):
                h, c = divmod(m, TT)
                if c == 0:
                    pe.wait_ge(qA_done.sem, qA_done.at(b, h))
                if m % MU < 2:
                    pe.wait_ge(qA_done.sem, qA_done.at(b, h + m % MU))
                else:
                    pe.wait_ge(max_done.sem, max_done.at(b, m - 2))
                nc.tensor.matmul(psR[:, m % 2, :], qA[:, h % RG, c * P:(c + 1) * P], kA[:, h // GRP, :],
                                 start=True, stop=True).then_inc(max_ps.sem, 1)

            def scores(b, p, u):
                h, half = 2 * p + u % 2, u // 2
                pe.wait_ge(exp_done.sem, exp_done.at(b, 4 * p + u - 2))
                pe.wait_ge(qB_done.sem, qB_done.at(b, h))
                for a in range(2):
                    keys = slice((2 * half + a) * P, (2 * half + a + 1) * P)
                    bank = psS[:, 2 * (u % 2) + a, :]
                    nc.tensor.matmul(bank, kA[:, h // GRP, keys], qA[:, h % RG, :], start=True, stop=False)
                    last = nc.tensor.matmul(bank, kB[:, h // GRP, keys], qB[:, h % RG, :],
                                            start=False, stop=True)
                last.then_inc(score_ps.sem, 1)

            def weigh(b, p, j, summed):
                half = j // 2
                if j % 2 == 0 and not summed:
                    pe.wait_ge(exp_done.sem, exp_done.at(b, 4 * p + 2 * half + 1))
                    if half == 0:
                        pe.wait_ge(o_taken.sem, o_taken.at(b, p - 1))
                        if p == 0:
                            pe.wait_ge(acc_done.sem, acc_done.at(b, -1))
                for e in range(2):
                    g = (2 * p + e) // GRP
                    out, lhs = (psD, ones[:, :]) if summed else (psO, v[:, j, g * HD:(g + 1) * HD])
                    last = nc.tensor.matmul(out[e * HD:(e + 1) * HD, :], lhs,
                                            probs[:, (4 * p + 2 * half + e) % 8, j % 2, :],
                                            start=(j == 0), stop=(j == TT - 1))
                if j % 2 and summed:
                    last.then_inc(pv_done.sem, 1)

            transpose_rows(0)
            for n in range(AHEAD):
                project(0, n)
            with pe.Fori(0, B) as b:
                for n in range(AHEAD, NB):
                    project(b, n)
                    if n in KEYS_AFTER:
                        transpose_keys(b, KEYS_AFTER.index(n))
                    if n == FIRST_AFTER:
                        pe.wait_ge(kA_done.sem, kA_done.at(b, KV - 1))
                        pe.wait_ge(kB_done.sem, kB_done.at(b, KV - 1))
                        pe.wait_ge(lo_done.sem, lo_done.at(b, 2 * TT - 1))
                        transpose_queries(b, 0)
                        transpose_queries(b, 1)
                    if n in MAXES_AFTER:
                        for m in range(4):
                            scores_for_max(b, 4 * MAXES_AFTER.index(n) + m)
                transpose_shifted(b, 0)
                transpose_shifted(b, 1)
                pe.wait_ge(lo_done.sem, lo_done.at(b, NB - 1))
                pe.wait_ge(qB_done.sem, qB_done.at(b, 1))
                transpose_queries(b, 2)
                transpose_queries(b, 3)
                for p in range(PAIRS):
                    nxt, before = p + 1 < PAIRS, p > 0

                    def maximum(m):
                        if nxt:
                            scores_for_max(b, (p + 1) * MU + m)

                    scores(b, p, 0)
                    if before:
                        weigh(b, p - 1, 2, False)
                    maximum(0)
                    if before:
                        weigh(b, p - 1, 2, True)
                    maximum(1)
                    scores(b, p, 1)
                    maximum(2)
                    if before:
                        weigh(b, p - 1, 3, False)
                    maximum(3)
                    if before:
                        weigh(b, p - 1, 3, True)
                    maximum(4)
                    scores(b, p, 2)
                    maximum(5)
                    scores(b, p, 3)
                    maximum(6)
                    weigh(b, p, 0, False)
                    maximum(7)
                    weigh(b, p, 0, True)
                    weigh(b, p, 1, False)
                    if nxt:
                        transpose_shifted(b, 2 * p + 2)
                        transpose_shifted(b, 2 * p + 3)
                    weigh(b, p, 1, True)
                    if p + 2 < PAIRS:
                        for h in (2 * p + 4, 2 * p + 5):
                            pe.wait_ge(qB_done.sem, qB_done.at(b, h - 2))
                            transpose_queries(b, h)
                for j in (2, 3):
                    weigh(b, PAIRS - 1, j, False)
                    weigh(b, PAIRS - 1, j, True)
                transpose_rows(b + 1)
                for n in range(AHEAD):
                    project(b + 1, n)
                pe.wait_ge(norm_done.sem, norm_done.at(b, PAIRS - 1))
                for t in range(TT):
                    bank = (psO, psD)[t // 2]
                    for p in range(PAIRS):
                        last = nc.tensor.matmul(bank[:, (t % 2) * D:(t % 2 + 1) * D],
                                                oT[:, p, t * P:(t + 1) * P], wo[:, p, :],
                                                start=(p == 0), stop=(p == PAIRS - 1))
                    if t % 2:
                        last.then_inc(out_ps.sem, 1)


def plain_attention_phase(nc, x, w, ident, x1, sorted_x):
    NB = 2 * TT
    QUADS = H // 4
    MP = 2 * TT
    MQ = 2 * MP
    UQ = 8
    NEG = 3 * FH
    RING = 3
    AHEAD = 8
    NORM_AT = 1
    with ExitStack() as ctx:
        def sb(name, shape, dt=F32):
            return ctx.enter_context(nc.sbuf_tensor("f_" + name, shape, dt))

        def ps(name, shape):
            return ctx.enter_context(nc.psum_tensor("f_" + name, shape, F32))

        def sig(name, per, credit=0, step=1):
            return Signal(ctx, nc, "f_" + name, per, credit, step)

        wqk = sb("wqk", [P, KC, 2 * D])
        wv = sb("wv", [P, KC, D])
        wo = sb("wo", [P, QUADS, D])
        bqk = sb("bqk", [P, 2 * D])
        bv, bo, g1, b1 = (sb(n, [P, D]) for n in ("bv", "bo", "g1", "b1"))
        idn = sb("idn", [P, P])
        zeros = sb("zeros", [P, D])
        norm0, norm1 = LayerNorm(nc, ctx, "f_norm0"), LayerNorm(nc, ctx, "f_norm1")
        xn = sb("xn", [P, TT, D])
        xnb = sb("xnb", [P, TT, D])
        xnT = sb("xnT", [P, KC, S])
        qk = sb("qk", [P, 2, 2 * D])
        q_tok = sb("q_tok", [P, TT, H, FB])
        k_tok = sb("k_tok", [P, TT, H, FB])
        v = sb("v", [P, TT, H, 2 * FH])
        kZ = sb("kZ", [P, 8, S], F32R)
        qM = sb("qM", [P, 2, S], F32R)
        qS = sb("qS", [P, 4, S], F32R)
        probs = sb("probs", [P, 8, 2, S])
        sums = sb("sums", [P, S])
        rsum = sb("rsum", [P, S])
        oT = sb("oT", [P, QUADS, S])
        r1 = sb("r1", [P, TT, D])

        psS = ps("psS", [P, 4, S])
        psR = ps("psR", [P, RING, S])
        psO = ps("psO", [P, S])

        loads = ctx.enter_context(nc.semaphore("f_loads"))
        zeroed = ctx.enter_context(nc.semaphore("f_zeroed"))
        cleared = ctx.enter_context(nc.semaphore("f_cleared"))
        passed = ctx.enter_context(nc.semaphore("f_passed"))
        scaled = ctx.enter_context(nc.semaphore("f_scaled"))
        LOADS = 14 * 16
        ZEROED = 8
        x_in = sig("x_in", 1, step=16)
        xn_done = sig("xn_done", TT)
        xnb_done = sig("xnb_done", 1, credit=1)
        xnT_ps = sig("xnT_ps", KC, credit=1)
        xnT_sb = sig("xnT_sb", KC)
        proj_ps = sig("proj_ps", NB)
        bias_done = sig("bias_done", NB)
        hi_done = sig("hi_done", TT)
        lo_done = sig("lo_done", TT, credit=2)
        neg_reset = sig("neg_reset", 1)
        kT_ps = sig("kT_ps", 2 * QUADS)
        kZ_done = sig("kZ_done", 2 * QUADS)
        qM_ps = sig("qM_ps", 2 * QUADS)
        qM_done = sig("qM_done", 2 * QUADS)
        max_ps = sig("max_ps", QUADS * MQ)
        max_done = sig("max_done", QUADS * MQ)
        qS_ps = sig("qS_ps", 2 * QUADS, credit=1)
        qS_done = sig("qS_done", 2 * QUADS)
        score_ps = sig("score_ps", QUADS * UQ)
        exp_done = sig("exp_done", QUADS * UQ, credit=2)
        pv_done = sig("pv_done", 2 * QUADS, credit=2)
        o_taken = sig("o_taken", QUADS, credit=1)
        sum_done = sig("sum_done", QUADS)
        rsum_done = sig("rsum_done", QUADS)
        norm_done = sig("norm_done", QUADS, credit=1)
        out_ps = sig("out_ps", 2)
        r1_done = sig("r1_done", 2, credit=1)
        n1_done = sig("n1_done", TT)
        gain_done = sig("gain_done", 1)
        x1_done = sig("x1_done", 1, credit=1)

        rows = x.rearrange("b (t p) d -> b p t d", p=P)
        USES = MQ + 6

        def key_use(p):
            return USES * (p // 2) + p % 2

        def query_use(p):
            return USES * (p // 2) + 2 + p % 2

        def max_use(m):
            quad, m = divmod(m, MQ)
            return USES * quad + 4 + m + (m >= MP)

        def shifted_use(p):
            return USES * (p // 2) + (4 + MP, 5 + MQ)[p % 2]

        block = ctx.enter_context(nc.Block())

        @block.sync
        def _(sp):
            sp.dma_start(xn[:, :, :], rows[0]).then_inc(x_in.sem, 16)
            sp.dma_start(idn[:, :], ident).then_inc(loads, 16)
            sp.dma_start(wqk[:, :, 0:D], w["Wq"].rearrange("(c p) n -> p c n", p=P)).then_inc(loads, 16)
            sp.dma_start(wqk[:, :, D:], w["Wk"].rearrange("(c p) n -> p c n", p=P)).then_inc(loads, 16)
            sp.dma_start(wv[:, :, :], w["Wv"].rearrange("(c p) n -> p c n", p=P)).then_inc(loads, 16)
            sp.dma_start(bqk[:, 0:D], w["bq"].partition_broadcast(P)).then_inc(loads, 16)
            sp.dma_start(bqk[:, D:], w["bk"].partition_broadcast(P)).then_inc(loads, 16)
            for tile, name in ((bv, "bv"), (bo, "bo"), (g1, "ln1_g"), (b1, "ln1_b")):
                sp.dma_start(tile[:, :], w[name].partition_broadcast(P)).then_inc(loads, 16)
            sp.wait_ge(zeroed, ZEROED)
            heads = w["Wo"].rearrange("(q i d) n -> i d q n", i=4, d=FH)
            for i in range(4):
                sp.dma_start(wo[32 * i:32 * i + FH, :, :], heads[i]).then_inc(loads, 16)
            sp.dma_start(sorted_x.rearrange("(n p) d -> p n d", p=P),
                         zeros[:, :].unsqueeze(1).to_broadcast([P, TILES * TOK // P, D])).then_inc(cleared, 16)

            def load(b, following):
                sp.wait_ge(xnT_ps.sem, xnT_ps.at(b, KC - 1))
                sp.sem_inc(passed, 1)
                sp.wait_ge(xnb_done.sem, xnb_done.at(b, 0))
                sp.dma_start(xn[:, :, :], rows[following]).then_inc(x_in.sem, 16)

            with sp.Fori(0, B - 1) as b:
                load(b, b + 1)
            load(B - 1, B - 1)
            sp.wait_ge(cleared, 16)

        @block.gpsimd
        def _(pool):
            lo_done.grant(pool)
            norm_done.grant(pool)
            xnb_done.grant(pool)
            x1_done.grant(pool)
            norm0.set_power(pool)
            norm1.set_power(pool)
            for tile in (q_tok, k_tok, v, wo):
                nc.gpsimd.memset(tile[:, :, :] if len(tile.shape) == 3 else tile[:, :, :, :], 0.0).then_inc(zeroed, 1)
            nc.gpsimd.memset(kZ[:, :, :].bitcast(F32), 0.0).then_inc(zeroed, 1)
            nc.gpsimd.memset(zeros[:, :], 0.0).then_inc(zeroed, 1)
            pool.wait_ge(zeroed, 6)
            nc.gpsimd.memset(k_tok[:, :, :, NEG], 1.0).then_inc(zeroed, 1)
            nc.gpsimd.memset(v[:, :, :, FH:], 1.0).then_inc(zeroed, 1)
            pool.wait_ge(zeroed, ZEROED)
            pool.wait_ge(loads, LOADS)

            def xnb_sum(b):
                pool.wait_ge(r1_done.sem, r1_done.at(b, -1))
                pool.wait_ge(xn_done.sem, xn_done.at(b, TT - 1))
                bias = bo[:, :].unsqueeze(1).to_broadcast([P, TT, D])
                nc.gpsimd.tensor_tensor(xnb[:, :, :], xn[:, :, :], bias, ALU.add).then_inc(xnb_done.sem, 1)

            def low_parts(b, t):
                pool.wait_ge(hi_done.sem, hi_done.at(b, t))
                src = qk[:, t % 2, :].rearrange("p (a h d) -> p a h d", a=2, d=FH)
                nc.gpsimd.tensor_tensor(q_tok[:, t, :, FH:2 * FH], src[:, 0], q_tok[:, t, :, 0:FH], ALU.subtract)
                nc.gpsimd.tensor_tensor(k_tok[:, t, :, 2 * FH:NEG], src[:, 1], k_tok[:, t, :, 0:FH],
                                        ALU.subtract).then_inc(lo_done.sem, 1)

            def normalize(b, quad):
                pool.wait_ge(rsum_done.sem, rsum_done.at(b, quad))
                nc.gpsimd.tensor_tensor(oT[:, quad, :], oT[:, quad, :], rsum[:, :], ALU.mult)\
                    .then_inc(norm_done.sem, 1)

            def reset_maxima(b):
                pool.wait_ge(qS_ps.sem, qS_ps.at(b, -1))
                pool.sem_inc(passed, 1)
                nc.gpsimd.memset(q_tok[:, :, :, NEG], 0.0).then_inc(neg_reset.sem, 1)

            norm0.raise_variance(pool, 0)
            reset_maxima(0)
            xnb_sum(0)
            for t in range(AHEAD // 2):
                low_parts(0, t)
            with pool.Fori(0, B) as b:
                for t in range(AHEAD // 2, TT):
                    low_parts(b, t)
                for quad in range(1, QUADS):
                    normalize(b, quad - 1)
                norm0.raise_variance(pool, b + 1)
                reset_maxima(b + 1)
                for t in range(AHEAD // 2):
                    low_parts(b + 1, t)
                    if t == 0:
                        normalize(b, QUADS - 1)
                norm1.raise_variance(pool, b)
                xnb_sum(b + 1)
                pool.wait_ge(n1_done.sem, n1_done.at(b, TT - 1))
                x1_b = x1[:, bass.ds(b * TT, TT), :]
                gain, offset = (g[:, :].unsqueeze(1).to_broadcast([P, TT, D]) for g in (g1, b1))
                pool.sem_inc(passed, 1)
                nc.gpsimd.tensor_tensor(x1_b, r1[:, :, :], gain, ALU.mult).then_inc(gain_done.sem, 1)
                pool.wait_ge(gain_done.sem, gain_done.at(b, 0))
                pool.sem_inc(passed, 1)
                nc.gpsimd.tensor_tensor(x1_b, x1_b, offset, ALU.add).then_inc(x1_done.sem, 1)

        @block.scalar
        def _(act):
            exp_done.grant(act)
            o_taken.grant(act)
            act.wait_ge(loads, LOADS)
            nc.scalar.mul(wqk[:, :, 0:D], wqk[:, :, 0:D], FH ** -0.5).then_inc(scaled, 1)
            nc.scalar.mul(bqk[:, 0:D], bqk[:, 0:D], FH ** -0.5).then_inc(scaled, 1)

            def take_xnT(b):
                for c in range(KC):
                    act.wait_ge(xnT_ps.sem, xnT_ps.at(b, c))
                    nc.scalar.copy(xnT[:, c, :], psR[:, c, :]).then_inc(xnT_sb.sem, 1)

            def high_parts(b, t):
                act.wait_ge(bias_done.sem, bias_done.at(b, 2 * t))
                src = qk[:, t % 2, :].rearrange("p (a h d) -> p a h d", a=2, d=FH)
                q_high = q_tok[:, t, :, :].rearrange("p h (a c) -> p h a c", a=2)[:, :, :, 0:FH]
                k_high = k_tok[:, t, :, 0:2 * FH].rearrange("p h (a c) -> p h a c", a=2)
                nc.scalar.copy(q_high.bitcast(F32R), src[:, 0].unsqueeze(2).to_broadcast([P, H, 2, FH]))
                nc.scalar.copy(k_high.bitcast(F32R),
                               src[:, 1].unsqueeze(2).to_broadcast([P, H, 2, FH])).then_inc(hi_done.sem, 1)

            def take_keys(b, p):
                act.wait_ge(kT_ps.sem, kT_ps.at(b, p))
                nc.scalar.copy(kZ[0:FB, 2 * p % 8, :], psR[0:FB, key_use(p) % RING, :])
                nc.scalar.copy(kZ[FB:, (2 * p + 1) % 8, :], psR[FB:, key_use(p) % RING, :]).then_inc(kZ_done.sem, 1)

            def take_queries(b, p):
                act.wait_ge(qM_ps.sem, qM_ps.at(b, p))
                nc.scalar.copy(qM[:, p % 2, :], psR[:, query_use(p) % RING, :]).then_inc(qM_done.sem, 1)

            def take_shifted(b, p):
                act.wait_ge(qS_ps.sem, qS_ps.at(b, p))
                nc.scalar.copy(qS[:, p % 4, :], psR[:, shifted_use(p) % RING, :]).then_inc(qS_done.sem, 1)

            def take_output(b, quad):
                act.wait_ge(pv_done.sem, pv_done.at(b, 2 * quad + 1))
                nc.scalar.copy(oT[:, quad, :], psO[:, :]).then_inc(o_taken.sem, 1)

            take_xnT(0)
            for t in range(AHEAD // 2):
                high_parts(0, t)
            with act.Fori(0, B) as b:
                for t in range(AHEAD // 2, TT):
                    high_parts(b, t)
                for quad in (0, 1):
                    for p in (2 * quad, 2 * quad + 1):
                        take_keys(b, p)
                    for p in (2 * quad, 2 * quad + 1):
                        take_queries(b, p)
                    if quad == 0:
                        take_shifted(b, 0)
                        take_shifted(b, 1)
                for quad in range(QUADS):
                    nxt = quad + 1 < QUADS
                    for u in range(UQ):
                        i = UQ * quad + u
                        act.wait_ge(score_ps.sem, score_ps.at(b, i))
                        act.wait_ge(pv_done.sem, pv_done.at(b, 2 * (quad - 1) + u // 4))
                        nc.scalar.activation(probs[:, u, :, :], psS[:, 2 * (u % 2):2 * (u % 2) + 2, :],
                                             ACT.Exp).then_inc(exp_done.sem, 1)
                        if u == 3 and quad:
                            take_output(b, quad - 1)
                        if u == 4 and nxt:
                            take_shifted(b, 2 * quad + 2)
                    if nxt:
                        take_shifted(b, 2 * quad + 3)
                    if quad + 2 < QUADS:
                        for p in (2 * quad + 4, 2 * quad + 5):
                            take_keys(b, p)
                        for p in (2 * quad + 4, 2 * quad + 5):
                            take_queries(b, p)
                take_output(b, QUADS - 1)
                take_xnT(b + 1)
                for t in range(AHEAD // 2):
                    high_parts(b + 1, t)

        @block.vector
        def _(dve):
            r1_done.grant(dve)
            dve.wait_ge(loads, LOADS)
            dve.wait_ge(scaled, 2)
            dve.wait_ge(zeroed, ZEROED)

            def add_bias(b, t):
                dve.wait_ge(lo_done.sem, lo_done.at(b, t - 2))
                dve.wait_ge(proj_ps.sem, proj_ps.at(b, 2 * t))
                nc.vector.tensor_tensor(qk[:, t % 2, :], psS[:, 2 * t % 4, :], bqk[:, :],
                                        ALU.add).then_inc(bias_done.sem, 1)
                dve.wait_ge(proj_ps.sem, proj_ps.at(b, 2 * t + 1))
                nc.vector.tensor_tensor(v[:, t, :, 0:FH],
                                        psS[:, (2 * t + 1) % 4, 0:D].rearrange("p (h d) -> p h d", d=FH),
                                        bv[:, :].rearrange("p (h d) -> p h d", d=FH),
                                        ALU.add).then_inc(bias_done.sem, 1)

            def take_max(b, m):
                h, c = divmod(m, TT)
                dve.wait_ge(max_ps.sem, max_ps.at(b, m))
                nc.vector.tensor_reduce(q_tok[:, c, h, NEG:NEG + 1], psR[:, max_use(m) % RING, :], AX.X, ALU.max,
                                        negate=True).then_inc(max_done.sem, 1)

            def invert_sums(b, quad):
                dve.wait_ge(o_taken.sem, o_taken.at(b, quad))
                dve.wait_ge(norm_done.sem, norm_done.at(b, quad - 1))
                dve.sem_inc(passed, 1)
                nc.vector.stream_shuffle(sums[:, :], oT[:, quad, :], [FH + i % FH for i in range(32)])\
                    .then_inc(sum_done.sem, 1)
                dve.wait_ge(sum_done.sem, sum_done.at(b, quad))
                nc.vector.reciprocal(rsum[:, :], sums[:, :]).then_inc(rsum_done.sem, 1)

            dve.wait_ge(x_in.sem, x_in.at(0, 0))
            norm0.statistics(dve, 0, xn)
            norm0.apply(dve, 0, xn, xn, xn_done)
            for t in range(AHEAD // 2):
                add_bias(0, t)
            with dve.Fori(0, B) as b:
                for t in range(AHEAD // 2, TT):
                    add_bias(b, t)
                for m in range(MQ):
                    take_max(b, m)
                for quad in range(QUADS):
                    nxt = quad + 1 < QUADS
                    if nxt:
                        for m in range(MQ):
                            take_max(b, (quad + 1) * MQ + m)
                    if quad:
                        invert_sums(b, quad - 1)
                dve.wait_ge(x_in.sem, x_in.at(b + 1, 0))
                norm0.statistics(dve, b + 1, xn)
                norm0.apply(dve, b + 1, xn, xn, xn_done)
                invert_sums(b, QUADS - 1)
                for t in range(AHEAD // 2):
                    add_bias(b + 1, t)
                dve.wait_ge(xnb_done.sem, xnb_done.at(b, 0))
                dve.wait_ge(x1_done.sem, x1_done.at(b, -1))
                for k in range(2):
                    dve.wait_ge(out_ps.sem, out_ps.at(b, k))
                    nc.vector.tensor_tensor(r1[:, 2 * k:2 * k + 2, :], xnb[:, 2 * k:2 * k + 2, :],
                                            (psO[:, :], psR[:, 2, :])[k].rearrange("p (t d) -> p t d", d=D),
                                            ALU.add).then_inc(r1_done.sem, 1)
                dve.wait_ge(r1_done.sem, r1_done.at(b, 1))
                norm1.statistics(dve, b, r1)
                norm1.apply(dve, b, r1, r1, n1_done)

        @block.tensor
        def _(pe):
            xnT_ps.grant(pe)
            qS_ps.grant(pe)
            pv_done.grant(pe)
            pe.wait_ge(loads, LOADS)
            pe.wait_ge(scaled, 2)
            pe.wait_ge(zeroed, ZEROED)

            def transpose_rows(b):
                for t in range(TT):
                    pe.wait_ge(xn_done.sem, xn_done.at(b, t))
                    for c in range(KC):
                        last = nc.tensor.transpose(psR[:, c, t * P:(t + 1) * P], xn[:, t, c * P:(c + 1) * P],
                                                   idn[:, :])
                        if t == TT - 1:
                            last.then_inc(xnT_ps.sem, 1)

            def project(b, n):
                t, i = divmod(n, 2)
                if n == 0:
                    pe.wait_ge(xnT_sb.sem, xnT_sb.at(b, KC - 1))
                if n >= 4:
                    pe.wait_ge(bias_done.sem, bias_done.at(b, n - 4))
                for c in range(KC):
                    rhs, wide = ((wqk[:, c, :], 2 * D), (wv[:, c, :], D))[i]
                    last = nc.tensor.matmul(psS[:, n % 4, 0:wide], xnT[:, c, t * P:(t + 1) * P], rhs,
                                            start=(c == 0), stop=(c == KC - 1))
                last.then_inc(proj_ps.sem, 1)

            def transpose_pair(bank, src, p):
                for t in range(TT):
                    heads = src[:, t, 2 * p:2 * p + 2, :].rearrange("p h d -> p (h d)")
                    last = nc.tensor.transpose(psR[:, bank, t * P:(t + 1) * P], heads, idn[:, :])
                return last

            def bank_read(b, use):
                if use < RING:
                    pe.wait_ge(r1_done.sem, r1_done.at(b, -1))
                    return
                quad, k = divmod(use - RING, USES)
                if k < 2:
                    pe.wait_ge(kZ_done.sem, kZ_done.at(b, 2 * quad + k))
                elif k < 4:
                    pe.wait_ge(qM_done.sem, qM_done.at(b, 2 * quad + k - 2))
                elif k == 4 + MP or k == 5 + MQ:
                    pe.wait_ge(qS_done.sem, qS_done.at(b, 2 * quad + (k == 5 + MQ)))
                else:
                    pe.wait_ge(max_done.sem, max_done.at(b, MQ * quad + k - 4 - (k > 4 + MP)))

            def keys(b, p):
                bank_read(b, key_use(p))
                transpose_pair(key_use(p) % RING, k_tok, p).then_inc(kT_ps.sem, 1)

            def queries(b, p):
                bank_read(b, query_use(p))
                transpose_pair(query_use(p) % RING, q_tok, p).then_inc(qM_ps.sem, 1)

            def scores_for_max(b, m):
                h, c = divmod(m, TT)
                if c == 0:
                    pe.wait_ge(qM_done.sem, qM_done.at(b, h // 2))
                bank_read(b, max_use(m))
                nc.tensor.matmul(psR[:, max_use(m) % RING, :], qM[:, h // 2 % 2, c * P:(c + 1) * P],
                                 kZ[:, h % 8, :], start=True, stop=True).then_inc(max_ps.sem, 1)

            def shifted(b, p):
                bank_read(b, shifted_use(p))
                pe.wait_ge(max_done.sem, max_done.at(b, (p + 1) * MP - 1))
                transpose_pair(shifted_use(p) % RING, q_tok, p).then_inc(qS_ps.sem, 1)

            def scores(b, quad, u):
                h, half = 4 * quad + u % 4, u // 4
                pe.wait_ge(exp_done.sem, exp_done.at(b, UQ * quad + u - 2))
                pe.wait_ge(qS_done.sem, qS_done.at(b, h // 2))
                for a in range(2):
                    j = 2 * half + a
                    last = nc.tensor.matmul(psS[:, 2 * (u % 2) + a, :], kZ[:, h % 8, j * P:(j + 1) * P],
                                            qS[:, h // 2 % 4, :], start=True, stop=True)
                last.then_inc(score_ps.sem, 1)

            def weigh(b, quad, j):
                if j % 2 == 0:
                    pe.wait_ge(exp_done.sem, exp_done.at(b, UQ * quad + 2 * j + 3))
                if j == 0:
                    pe.wait_ge(o_taken.sem, o_taken.at(b, quad - 1))
                    if quad == 0:
                        pe.wait_ge(r1_done.sem, r1_done.at(b, -1))
                for e in range(4):
                    last = nc.tensor.matmul(psO[32 * e:32 * e + 32, :], v[:, j, 4 * quad + e, :],
                                            probs[:, 4 * (j // 2) + e, j % 2, :],
                                            start=(j == 0), stop=(j == TT - 1), tile_position=(0, 32 * e))
                if j % 2:
                    last.then_inc(pv_done.sem, 1)

            transpose_rows(0)
            for n in range(AHEAD):
                project(0, n)
            with pe.Fori(0, B) as b:
                for n in range(AHEAD, NB):
                    project(b, n)
                pe.wait_ge(neg_reset.sem, neg_reset.at(b, 0))
                pe.wait_ge(lo_done.sem, lo_done.at(b, TT - 1))
                pe.wait_ge(bias_done.sem, bias_done.at(b, NB - 1))
                for p in (0, 1):
                    keys(b, p)
                for p in (0, 1):
                    queries(b, p)
                for m in range(MP):
                    scores_for_max(b, m)
                shifted(b, 0)
                for m in range(MP, MQ):
                    scores_for_max(b, m)
                shifted(b, 1)
                for p in (2, 3):
                    keys(b, p)
                for p in (2, 3):
                    queries(b, p)
                for quad in range(QUADS):
                    nxt = quad + 1 < QUADS
                    for u in range(UQ):
                        scores(b, quad, u)
                        if nxt:
                            scores_for_max(b, (quad + 1) * MQ + 2 * u)
                        if u in (1, 2) and quad:
                            weigh(b, quad - 1, u + 1)
                        if u in (5, 6):
                            weigh(b, quad, u - 5)
                        if nxt:
                            scores_for_max(b, (quad + 1) * MQ + 2 * u + 1)
                            if u == 3:
                                shifted(b, 2 * quad + 2)
                    if nxt:
                        shifted(b, 2 * quad + 3)
                    if quad + 2 < QUADS:
                        for p in (2 * quad + 4, 2 * quad + 5):
                            keys(b, p)
                        for p in (2 * quad + 4, 2 * quad + 5):
                            queries(b, p)
                for j in (2, 3):
                    weigh(b, QUADS - 1, j)
                transpose_rows(b + 1)
                for n in range(AHEAD):
                    project(b + 1, n)
                pe.wait_ge(norm_done.sem, norm_done.at(b, QUADS - 1))
                for t in range(TT):
                    bank = (psO[:, :], psR[:, 2, :])[t // 2]
                    for quad in range(QUADS):
                        last = nc.tensor.matmul(bank[:, (t % 2) * D:(t % 2 + 1) * D],
                                                oT[:, quad, t * P:(t + 1) * P], wo[:, quad, :],
                                                start=(quad == 0), stop=(quad == QUADS - 1))
                    if t % 2:
                        last.then_inc(out_ps.sem, 1)


def routing_phase(nc, x1, router_w, router_b, before, tile_starts, place, tile_expert, sorted_x):
    CT = B * TT
    with ExitStack() as ctx:
        def sb(name, shape, dt=F32):
            return ctx.enter_context(nc.sbuf_tensor("r_" + name, shape, dt))

        tri = sb("tri", [P, P])
        starts = sb("starts", [P, TILES])
        ones = sb("ones", [P, P])
        rw = sb("rw", [P, D])
        rb = sb("rb", [P, 1])
        weighed = sb("weighed", [P, 2, D])
        dots = sb("dots", [P, CT])
        key = sb("key", [P, CT])
        nearest_i = sb("nearest_i", [P, CT], I32)
        nearest = sb("nearest", [P, CT])
        above = sb("above", [P, CT])
        floor_i = sb("floor_i", [P, CT], I32)
        expert_i = sb("expert_i", [P, CT], I32)
        expert = sb("expert", [P, CT])
        hot = sb("hot", [P, NE, CT])
        total = sb("total", [P, NE * CT])
        upto = sb("upto", [P, NE * CT])
        ahead = sb("ahead", [P, NE * CT])
        count = sb("count", [P, NE])
        count_i = sb("count_i", [P, NE], I32)
        padded_i = sb("padded_i", [P, NE], I32)
        padded = sb("padded", [P, NE])
        end = sb("end", [P, NE])
        shift = sb("shift", [P, NE])
        row = sb("row", [P, NE, CT])
        row_f = sb("row_f", [P, CT])
        tile_f = sb("tile_f", [P, 2, TILES])
        psP = ctx.enter_context(nc.psum_tensor("r_psP", [P, NE * CT], F32))
        psT = ctx.enter_context(nc.psum_tensor("r_psT", [P, 512], F32))

        loads, consts, dot_done, hot_done, sums_ps, chain, placed, scattered = (
            ctx.enter_context(nc.semaphore("r_" + n)) for n in
            ("loads", "consts", "dot_done", "hot_done", "sums_ps", "chain", "placed", "scattered"))
        block = ctx.enter_context(nc.Block())

        @block.sync
        def _(sp):
            sp.dma_start(tri[:, :], before).then_inc(loads, 16)
            sp.dma_start(starts[:, :], tile_starts.partition_broadcast(P)).then_inc(loads, 16)
            sp.dma_start(rw[:, :], router_w.rearrange("d a -> (d a)").partition_broadcast(P)).then_inc(loads, 16)
            sp.dma_start(rb[:, :], router_b.partition_broadcast(P)).then_inc(loads, 16)

        @block.gpsimd
        def _(pool):
            nc.gpsimd.memset(ones[:, :], 1.0).then_inc(consts, 1)
            nc.gpsimd.memset(shift[:, :], 0.0).then_inc(consts, 1)
            pool.wait_ge(placed, 1)
            for c in range(CT):
                nc.gpsimd.indirect_dma_start(
                    out=sorted_x, out_offset=bass.IndirectOffsetOnAxis(ap=place[:, c:c + 1], axis=0),
                    in_=x1[:, c, :], in_offset=None).then_inc(scattered, 16)
            pool.wait_ge(scattered, 16 * CT)

        @block.tensor
        def _(pe):
            pe.wait_ge(loads, 64)
            pe.wait_ge(consts, 2)
            pe.wait_ge(hot_done, NE)
            tokens = hot[:, :, :].rearrange("p e c -> p (e c)")
            nc.tensor.matmul(psP[:, :], tri[:, :], tokens, start=True, stop=True)
            nc.tensor.matmul(psT[:, 0:NE * CT], ones[:, :], tokens, start=True, stop=True).then_inc(sums_ps, 1)

        @block.vector
        def _(dve):
            steps = [0]

            def link(instruction):
                steps[0] += 1
                instruction.then_inc(chain, 1)
                dve.wait_ge(chain, steps[0])

            dve.wait_ge(loads, 64)
            for c in range(CT):
                if c >= 2:
                    dve.wait_ge(dot_done, c - 1)
                nc.vector.tensor_tensor_reduce(out=weighed[:, c % 2, :], in0=x1[:, c, :], in1=rw[:, :], scale=1.0,
                                               scalar=0.0, op0=ALU.mult, op1=ALU.add,
                                               accum_out=dots[:, c:c + 1]).then_inc(dot_done, 1)
            dve.wait_ge(dot_done, CT)
            link(nc.vector.tensor_scalar(key[:, :], dots[:, :], rb[:, 0:1], None, ALU.add))
            link(nc.vector.tensor_copy(nearest_i[:, :], key[:, :]))
            link(nc.vector.tensor_copy(nearest[:, :], nearest_i[:, :]))
            link(nc.vector.tensor_tensor(above[:, :], nearest[:, :], key[:, :], ALU.is_gt))
            link(nc.vector.tensor_tensor(floor_i[:, :], nearest[:, :], above[:, :], ALU.subtract))
            link(nc.vector.tensor_scalar(expert_i[:, :], floor_i[:, :], NE - 1, None, ALU.bitwise_and))
            link(nc.vector.tensor_copy(expert[:, :], expert_i[:, :]))
            for e in range(NE):
                nc.vector.tensor_scalar(hot[:, e, :], expert[:, :], float(e), None, ALU.is_equal).then_inc(hot_done, 1)
            dve.wait_ge(sums_ps, 1)
            dve.wait_ge(consts, 2)
            link(nc.vector.tensor_copy(total[:, :], psT[:, 0:NE * CT]))
            link(nc.vector.tensor_tensor_scan(upto[:, :], ones[:, :], total[:, :], 0.0, ALU.mult, ALU.add))
            link(nc.vector.tensor_tensor(ahead[:, :], upto[:, :], total[:, :], ALU.subtract))
            ends = upto[:, :].rearrange("p (e c) -> p e c", c=CT)[:, :, CT - 1]
            link(nc.vector.tensor_copy(count[:, 0:1], ends[:, 0:1]))
            link(nc.vector.tensor_tensor(count[:, 1:NE], ends[:, 1:NE], ends[:, 0:NE - 1], ALU.subtract))
            link(nc.vector.tensor_scalar(count_i[:, :], count[:, :], float(TOK - 1), None, ALU.add))
            bits = TOK.bit_length() - 1
            link(nc.vector.tensor_scalar(padded_i[:, :], count_i[:, :], bits, bits,
                                         ALU.logical_shift_right, ALU.logical_shift_left))
            link(nc.vector.tensor_copy(padded[:, :], padded_i[:, :]))
            link(nc.vector.tensor_tensor_scan(end[:, :], ones[:, 0:NE], padded[:, :], 0.0, ALU.mult, ALU.add))
            link(nc.vector.tensor_tensor(shift[:, 1:NE], end[:, 0:NE - 1], ends[:, 0:NE - 1], ALU.subtract))
            flat = row[:, :, :].rearrange("p e c -> p (e c)")
            link(nc.vector.tensor_tensor(flat, psP[:, :], ahead[:, :], ALU.add))
            link(nc.vector.tensor_tensor(row[:, :, :], row[:, :, :],
                                         shift[:, :].unsqueeze(2).to_broadcast([P, NE, CT]), ALU.add))
            link(nc.vector.tensor_tensor(row[:, :, :], row[:, :, :], hot[:, :, :], ALU.mult))
            link(nc.vector.tensor_reduce(row_f[:, :], row[:, :, :].rearrange("p e c -> p c e"), AX.X, ALU.add))
            link(nc.vector.tensor_copy(place[:, :], row_f[:, :]))
            link(nc.vector.tensor_scalar(tile_f[:, 0, :], starts[:, :], end[:, 0:1], None, ALU.is_ge))
            link(nc.vector.scalar_tensor_tensor(tile_f[:, 1, :], starts[:, :], end[:, 1:2], tile_f[:, 0, :],
                                                ALU.is_ge, ALU.add))
            link(nc.vector.scalar_tensor_tensor(tile_f[:, 0, :], starts[:, :], end[:, 2:3], tile_f[:, 1, :],
                                                ALU.is_ge, ALU.add))
            nc.vector.tensor_copy(tile_expert[:, :], tile_f[:, 0, :]).then_inc(placed, 1)


def experts_phase(nc, W1, b1, W2, b2, gain, offset, ident, tile_expert, sorted_x, sorted_z):
    MC = FF // P
    TC = TOK // P
    LOOPED = (TILES - 3) // 2
    with ExitStack() as ctx:
        def sb(name, shape, dt=F32):
            return ctx.enter_context(nc.sbuf_tensor("e_" + name, shape, dt))

        def sig(name, per, credit=0, step=1):
            return Signal(ctx, nc, "e_" + name, per, credit, step)

        idn = sb("idn", [P, P])
        w1 = sb("w1", [P, 2, KC, FF])
        w2 = sb("w2", [P, 2, MC, D])
        o1_rows = sb("o1_rows", [MC, 2, P])
        o1 = sb("o1", [P, 2, MC])
        o2 = sb("o2", [P, 2, D])
        xs = sb("xs", [P, 2, TC, D])
        xT = sb("xT", [P, 2, KC, TOK])
        hT = sb("hT", [P, 2, MC, TOK])
        xo = sb("xo", [P, 2, TC, D])
        r2 = sb("r2", [P, 2, TC, D])
        z = sb("z", [P, 2, TC, D])
        g2, b2_norm = sb("g2", [P, D]), sb("b2_norm", [P, D])
        norm = LayerNorm(nc, ctx, "e_norm", TC, turns=2)
        psX = ctx.enter_context(nc.psum_tensor("e_psX", [P, 2, 512], F32))
        psH = ctx.enter_context(nc.psum_tensor("e_psH", [P, 4, 512], F32))
        psY = ctx.enter_context(nc.psum_tensor("e_psY", [P, 2, 512], F32))

        passed = ctx.enter_context(nc.semaphore("e_passed"))
        passed_sp = ctx.enter_context(nc.semaphore("e_passed_sp"))
        consts_in = ctx.enter_context(nc.semaphore("e_consts_in"))
        x_in = [sig(f"x_in{k}", 1, step=16) for k in range(2)]
        w_in = [sig(f"w_in{k}", 1, step=64) for k in range(2)]
        xT_ps = sig("xT_ps", 2)
        xT_sb = sig("xT_sb", 2)
        o1_ps = sig("o1_ps", 2)
        o1_sb = sig("o1_sb", 2)
        h_ps = sig("h_ps", MC)
        h_sb = sig("h_sb", MC, credit=4)
        y_ps = sig("y_ps", 2)
        xo_done = sig("xo_done", 2)
        r2_done = sig("r2_done", 2, credit=2)
        normed = sig("normed", 2 * TC)
        gain_done = sig("gain_done", 2, credit=2)
        z_done = sig("z_done", 2)
        stored = [sig(f"stored{k}", 1, credit=1, step=16) for k in range(2)]
        x_tiles = sorted_x.rearrange("(i c p) d -> i p c d", p=P, c=TC)
        z_tiles = sorted_z.rearrange("(i c p) d -> i p c d", p=P, c=TC)
        block = ctx.enter_context(nc.Block())

        def tiles(engine, step):
            with engine.Fori(0, LOOPED) as i:
                for k in range(2):
                    step(i, k, 2)
            for t in range(2 * LOOPED, TILES):
                step(t // 2, t % 2, min(2, TILES - 1 - t))

        @block.sync
        def _(sp):
            for s in stored:
                s.grant(sp)
            sp.dma_start(idn[:, :], ident).then_inc(consts_in, 16)
            sp.dma_start(g2[:, :], gain.partition_broadcast(P)).then_inc(consts_in, 16)
            sp.dma_start(b2_norm[:, :], offset.partition_broadcast(P)).then_inc(consts_in, 16)

            def load(i, k):
                e = sp.value_load(tile_expert[0:1, bass.ds(2 * i + k, 1)], min_val=0, max_val=NE - 1)
                sp.dma_start(xs[:, k, :, :], x_tiles[2 * i + k]).then_inc(x_in[k].sem, 16)
                sp.dma_start(w1[:, k, :, :], W1[e].rearrange("(c p) n -> p c n", p=P)).then_inc(w_in[k].sem, 16)
                sp.dma_start(w2[:, k, :, :], W2[e].rearrange("(m p) n -> p m n", p=P)).then_inc(w_in[k].sem, 16)
                sp.dma_start(o1_rows[:, k, :], b1[e].rearrange("(m p) -> m p", p=P)).then_inc(w_in[k].sem, 16)
                sp.dma_start(o2[:, k, :], b2[e].partition_broadcast(P)).then_inc(w_in[k].sem, 16)

            def step(i, k, follow):
                if follow == 2:
                    sp.wait_ge(r2_done.sem, r2_done.at(i, k))
                    sp.sem_inc(passed_sp, 1)
                    load(i + 1, k)
                sp.wait_ge(z_done.sem, z_done.at(i, k))
                sp.dma_start(z_tiles[2 * i + k], z[:, k, :, :]).then_inc(stored[k].sem, 16)

            load(0, 0)
            load(0, 1)
            tiles(sp, step)
            last = divmod(TILES - 1, 2)
            sp.wait_ge(stored[last[1]].sem, stored[last[1]].at(last[0], 0))
            sp.wait_ge(stored[1 - last[1]].sem, stored[1 - last[1]].at((TILES - 2) // 2, 0))

        @block.scalar
        def _(act):
            h_sb.grant(act)

            def step(i, k, follow):
                act.wait_ge(o1_ps.sem, o1_ps.at(i, k))
                nc.scalar.copy(o1[:, k, :], psY[:, k, 0:MC]).then_inc(o1_sb.sem, 1)
                act.wait_ge(o1_sb.sem, o1_sb.at(i, k))
                for m in range(MC):
                    if m % 2 == 0:
                        act.wait_ge(h_ps.sem, h_ps.at(i, 4 * k + m // 2))
                    last = nc.scalar.activation(hT[:, k, m, :], psH[:, m // 2, m % 2 * TOK:(m % 2 + 1) * TOK],
                                                ACT.Relu, bias=o1[:, k, m:m + 1])
                    if m % 2:
                        last.then_inc(h_sb.sem, 1)

            tiles(act, step)

        @block.gpsimd
        def _(pool):
            gain_done.grant(pool)
            norm.set_power(pool)
            pool.wait_ge(consts_in, 48)
            wide = [P, TC, D]

            def residual(i, k):
                pool.wait_ge(x_in[k].sem, x_in[k].at(i, 0))
                pool.wait_ge(w_in[k].sem, w_in[k].at(i, 0))
                pool.wait_ge(r2_done.sem, r2_done.at(i, k - 2))
                nc.gpsimd.tensor_tensor(xo[:, k, :, :], xs[:, k, :, :], o2[:, k, :].unsqueeze(1).to_broadcast(wide),
                                        ALU.add).then_inc(xo_done.sem, 1)

            def step(i, k, follow):
                residual(i, k)
                norm.raise_variance(pool, i, k)
                pool.wait_ge(normed.sem, normed.at(i, TC * k + TC - 1))
                pool.wait_ge(stored[k].sem, stored[k].at(i, -1))
                nc.gpsimd.tensor_tensor(z[:, k, :, :], r2[:, k, :, :], g2[:, :].unsqueeze(1).to_broadcast(wide),
                                        ALU.mult).then_inc(gain_done.sem, 1)
                pool.wait_ge(gain_done.sem, gain_done.at(i, k))
                nc.gpsimd.tensor_tensor(z[:, k, :, :], z[:, k, :, :], b2_norm[:, :].unsqueeze(1).to_broadcast(wide),
                                        ALU.add).then_inc(z_done.sem, 1)

            tiles(pool, step)

        @block.vector
        def _(dve):
            r2_done.grant(dve)

            def take_rows(i, k):
                dve.wait_ge(xT_ps.sem, xT_ps.at(i, k))
                nc.vector.tensor_copy(xT[:, k % 2, :, :].rearrange("p c n -> p (c n)"), psX[:, k % 2, :])\
                    .then_inc(xT_sb.sem, 1)

            def step(i, k, follow):
                if follow:
                    take_rows(i, k + 1)
                dve.wait_ge(y_ps.sem, y_ps.at(i, k))
                dve.wait_ge(xo_done.sem, xo_done.at(i, k))
                dve.wait_ge(gain_done.sem, gain_done.at(i, k - 2))
                nc.vector.tensor_tensor(r2[:, k, :, :], psY[:, k, :].rearrange("p (c n) -> p c n", c=TC),
                                        xo[:, k, :, :], ALU.add).then_inc(r2_done.sem, 1)
                dve.wait_ge(r2_done.sem, r2_done.at(i, k))
                norm.statistics(dve, i, r2[:, k, :, :], k)
                norm.apply(dve, i, r2[:, k, :, :], r2[:, k, :, :], normed, k)

            take_rows(0, 0)
            tiles(dve, step)

        @block.tensor
        def _(pe):
            pe.wait_ge(consts_in, 48)

            def transpose_tile(i, k):
                i, place = (i, k) if k < 2 else (i + 1, 0)
                pe.wait_ge(x_in[place].sem, x_in[place].at(i, 0))
                for c in range(KC):
                    for t in range(TC):
                        last = nc.tensor.transpose(psX[:, place, c * TOK + t * P:c * TOK + (t + 1) * P],
                                                   xs[:, place, t, c * P:(c + 1) * P], idn[:, :])
                last.then_inc(xT_ps.sem, 1)

            def transpose_offsets(i, k):
                i, place = (i, k) if k < 2 else (i + 1, 0)
                pe.wait_ge(w_in[place].sem, w_in[place].at(i, 0))
                pe.wait_ge(r2_done.sem, r2_done.at(i, place - 2))
                pe.sem_inc(passed, 1)
                nc.tensor.transpose(psY[:, place, 0:MC], o1_rows[:, place, :], idn[0:MC, 0:MC]).then_inc(o1_ps.sem, 1)

            def step(i, k, follow):
                pe.wait_ge(xT_sb.sem, xT_sb.at(i, k))
                for m in range(MC):
                    if m % 2 == 0:
                        pe.wait_ge(h_sb.sem, h_sb.at(i, 4 * k + m // 2 - 4))
                    for c in range(KC):
                        last = nc.tensor.matmul(psH[:, m // 2, m % 2 * TOK:(m % 2 + 1) * TOK],
                                                w1[:, k, c, m * P:(m + 1) * P], xT[:, k, c, :],
                                                start=(c == 0), stop=(c == KC - 1))
                    if m % 2:
                        last.then_inc(h_ps.sem, 1)
                if follow:
                    transpose_tile(i, k + 1)
                pe.wait_ge(h_sb.sem, h_sb.at(i, 4 * k + 3))
                for t in range(TC):
                    for m in range(MC):
                        last = nc.tensor.matmul(psY[:, k, t * D:(t + 1) * D], hT[:, k, m, t * P:(t + 1) * P],
                                                w2[:, k, m, :], start=(m == 0), stop=(m == MC - 1))
                last.then_inc(y_ps.sem, 1)
                if follow:
                    transpose_offsets(i, k + 1)

            transpose_tile(0, 0)
            transpose_offsets(0, 0)
            tiles(pe, step)
def shape_constants():
    import numpy as np

    inv_freq = 1.0 / np.float32(10000.0) ** (np.arange(0, HD, 2, dtype=np.float32) / np.float32(HD))
    angle = (np.arange(S, dtype=np.float32)[:, None] * inv_freq.astype(np.float32)[None, :]).astype(np.float32)
    cos, sin = np.cos(angle).astype(np.float32), np.sin(angle).astype(np.float32)
    scale = np.float32(HD ** -0.5)
    start = 2.0 ** (-2.0 ** (-(np.log2(H) - 3)))
    slopes = np.array([start * start ** i for i in range(H)], np.float32)
    high = (slopes.view(np.uint32) & np.uint32(0xFFFFF000)).view(np.float32)
    pos = np.arange(S, dtype=np.float32)
    return {
        "rope": np.stack([cos * scale, -sin * scale, sin * scale, cos, -sin, sin]),
        "slopes": slopes,
        "slope_parts": np.stack([high, slopes - high], 1),
        "key_rows": np.stack([np.ones_like(pos), pos, pos]),
        "before": np.triu(np.ones((P, P), np.float32), 1),
        "tile_starts": np.arange(TILES, dtype=np.float32) * TOK,
        "ident": np.eye(P, dtype=np.float32),
    }


_INS = ["L0_attn_x", "L0_attn_Wq", "L0_attn_Wk", "L0_attn_Wv", "L0_attn_Wo", "L0_ffn_Wq", "L0_ffn_bq", "L0_ffn_Wk",
        "L0_ffn_bk", "L0_ffn_Wv", "L0_ffn_bv", "L0_ffn_Wo", "L0_ffn_bo", "L0_ffn_router_w", "L0_ffn_router_b",
        "L0_ffn_W1", "L0_ffn_b1", "L0_ffn_W2", "L0_ffn_b2", "L0_ffn_ln1_g", "L0_ffn_ln1_b", "L0_ffn_ln2_g",
        "L0_ffn_ln2_b"]


def block_program(nc, ins, consts, out):
    x = ins["L0_attn_x"]
    w = {n[len("L0_ffn_"):]: ap for n, ap in ins.items() if n.startswith("L0_ffn_")}
    sorted_x = nc.dram_tensor("sorted_x", (TILES * TOK, D), F32, kind="Internal").ap()
    sorted_z = nc.dram_tensor("sorted_z", (TILES * TOK, D), F32, kind="Internal").ap()
    with ExitStack() as ctx:
        place = ctx.enter_context(nc.sbuf_tensor("place", [P, B * TT], I32))
        tile_expert = ctx.enter_context(nc.sbuf_tensor("tile_expert", [P, TILES], I32))
        with nc.sbuf_tensor("x1", [P, B * TT, D], F32) as x1:
            plain_attention_phase(nc, x, w, consts["ident"], x1, sorted_x)
            routing_phase(nc, x1, w["router_w"], w["router_b"], consts["before"], consts["tile_starts"], place,
                          tile_expert, sorted_x)
        experts_phase(nc, w["W1"], w["b1"], w["W2"], w["b2"], w["ln2_g"], w["ln2_b"], consts["ident"],
                      tile_expert, sorted_x, sorted_z)
        rotary_attention_phase(nc, x, *(ins["L0_attn_" + n] for n in ("Wq", "Wk", "Wv", "Wo")), consts["rope"],
                               consts["slopes"], consts["slope_parts"], consts["key_rows"], consts["ident"],
                               place, sorted_z, out)


def kernel(**inputs):
    import numpy as np
    import concourse.bacc as bacc
    from concourse.bass_utils import run_bass_kernel_spmd

    nc = bacc.Bacc("TRN2", target_bir_lowering=False, num_devices=1)
    arrays = {}

    def argument(name, a):
        a = np.ascontiguousarray(a)
        arrays[f"in_{name}"] = a
        return nc.dram_tensor(f"in_{name}", a.shape, mybir.dt.from_np(a.dtype), kind="ExternalInput").ap()

    ins = {name: argument(name, inputs[name]) for name in _INS}
    consts = {name: argument(name, a) for name, a in shape_constants().items()}
    out = nc.dram_tensor("out_0", (B, S, D), F32, kind="ExternalOutput").ap()
    block_program(nc, ins, consts, out)
    result = run_bass_kernel_spmd(nc, [arrays], core_ids=[0])
    return np.array(result.results[0]["out_0"])
```

```python
from contextlib import ExitStack

import concourse.bass as bass
from concourse import mybir

F32 = mybir.dt.float32
F32R = mybir.dt.float32r
BF16 = mybir.dt.bfloat16
I32 = mybir.dt.int32
ALU = mybir.AluOpType
ACT = mybir.ActivationFunctionType
AX = mybir.AxisListType

P = 128
B = 8
S = 512
D = 256
TT = S // P
KC = D // P
H = 16
EPS = 1e-5

HD = 64
KV = 4
GRP = H // KV
XR = HD + 3
XRP = XR + 1

FH = D // H
FB = 64
FF = 1024
NE = 4
TOK = 256
TILES = (B * S - NE) // TOK + NE


class Signal:

    def __init__(self, ctx, nc, name, per, credit=0, step=1):
        self.sem = ctx.enter_context(nc.semaphore(name))
        self.per, self.credit, self.step = per, credit, step

    def at(self, b, n):
        return b * (self.per * self.step) + (self.credit + n + 1) * self.step

    def grant(self, eng):
        eng.sem_inc(self.sem, self.credit * self.step)


class LayerNorm:

    def __init__(self, nc, ctx, name, count=TT, turns=1):
        def sb(what, shape):
            return ctx.enter_context(nc.sbuf_tensor(f"{name}_{what}", shape, F32))

        self.nc, self.count = nc, count
        self.stats, self.aggr = sb("stats", [P, count, 6]), sb("aggr", [P, count, 2])
        self.var_eps, self.rstd, self.power = (sb(what, [P, count]) for what in ("var_eps", "rstd", "power"))
        self.stats_done = Signal(ctx, nc, f"{name}_stats_done", count * turns)
        self.aggr_done = Signal(ctx, nc, f"{name}_aggr_done", count * turns)
        self.var_done = Signal(ctx, nc, f"{name}_var_done", turns)
        self.rstd_done = Signal(ctx, nc, f"{name}_rstd_done", turns)
        self.passed = ctx.enter_context(nc.semaphore(f"{name}_passed"))
        self.power_set = ctx.enter_context(nc.semaphore(f"{name}_power_set"))

    def set_power(self, pool):
        self.nc.gpsimd.memset(self.power[:, :], -0.5).then_inc(self.power_set, 1)
        pool.wait_ge(self.power_set, 1)

    def raise_variance(self, pool, b, turn=0):
        pool.wait_ge(self.var_done.sem, self.var_done.at(b, turn))
        self.nc.gpsimd.tensor_tensor(self.rstd[:, :], self.var_eps[:, :], self.power[:, :],
                                     ALU.pow).then_inc(self.rstd_done.sem, 1)

    def statistics(self, dve, b, src, turn=0):
        for t in range(self.count):
            self.nc.vector.bn_stats(self.stats[:, t, :], src[:, t, :]).then_inc(self.stats_done.sem, 1)
        for t in range(self.count):
            dve.wait_ge(self.stats_done.sem, self.stats_done.at(b, self.count * turn + t))
            dve.sem_inc(self.passed, 1)
            self.nc.vector.bn_aggr(self.aggr[:, t, :], self.stats[:, t, :]).then_inc(self.aggr_done.sem, 1)
        dve.wait_ge(self.aggr_done.sem, self.aggr_done.at(b, self.count * turn + self.count - 1))
        self.nc.vector.tensor_scalar(self.var_eps[:, :], self.aggr[:, :, 1], EPS, None,
                                     ALU.add).then_inc(self.var_done.sem, 1)

    def apply(self, dve, b, src, dst, applied, turn=0):
        dve.wait_ge(self.rstd_done.sem, self.rstd_done.at(b, turn))
        for t in range(self.count):
            self.nc.vector.tensor_scalar(dst[:, t, :], src[:, t, :], self.aggr[:, t, 0:1], self.rstd[:, t:t + 1],
                                         ALU.subtract, ALU.mult).then_inc(applied.sem, 1)


def rotary_attention_phase(nc, x, Wq, Wk, Wv, Wo, rope, slopes, slope_parts, key_rows, ident, place, sorted_z,
                           result):
    QB = H * HD // 512
    NB = TT * (QB + 1)
    QUADS = KV
    UQ = TT * GRP
    MQ = GRP * TT
    RG = 2 * GRP
    HALF = HD // 2

    ADDED = QUADS - 1
    SUM_AT = 10
    NORM_AT = 3

    def units(h):
        return [("max", TT * h + c) for c in range(TT)]

    SIDE_AFTER = {7: [("K", 0), ("L", 0)], 8: [("K", 1)], 9: [("L", 1)],
                  10: [("A", 0), ("A", 1)] + units(0)[:2],
                  11: units(0)[2:] + [("A", 2)] + units(1)[:2]}
    SIDE_BEFORE = [("B", 0)] + units(1)[2:] + [("A", 3)] + units(2) + [("B", 1)] + units(3) + [("A", 4)]

    def side(quad, slot):
        first, items = GRP * (quad + 1), []
        if quad == 0 and slot in (0, 2):
            items.append(("B", 2 + slot // 2))
        if first < H:
            k, third = divmod(slot, 3)
            if k < GRP:
                items += units(first + k)[(0, 2, 3)[third]:(2, 3, 4)[third]]
            if third == 1 and k + 1 < GRP:
                items.append(("A", first + k + 1))
            if third == 1 and k >= 1:
                items.append(("B", first + k - 1))
            if quad + 2 < KV and slot in (12, 15):
                items.append(("KL"[slot == 15], quad + 2))
            if slot == 14 and first + GRP < H:
                items.append(("A", first + GRP))
        return items

    ring = [i for n in sorted(SIDE_AFTER) for i in SIDE_AFTER[n]] + SIDE_BEFORE
    ring += [i for quad in range(QUADS) for slot in range(UQ) for i in side(quad, slot)]

    def bank_of(kind, n):
        return ring.index((kind, n)) % 2

    with ExitStack() as ctx:
        def sb(name, shape, dt=F32):
            return ctx.enter_context(nc.sbuf_tensor("a_" + name, shape, dt))

        def ps(name, shape):
            return ctx.enter_context(nc.psum_tensor("a_" + name, shape, F32))

        def sig(name, per, credit=0, step=1):
            return Signal(ctx, nc, "a_" + name, per, credit, step)

        wq = sb("wq", [P, KC, H * HD])
        wkv = sb("wkv", [P, KC, 2 * KV * HD])
        wo = sb("wo", [P, QUADS, 2, D])
        rope_t = sb("rope_t", [P, 6, TT, HD // 2])
        alibi = sb("alibi", [P, H, S], BF16)
        idn = sb("idn", [P, P])
        ones = sb("ones", [P, HALF])
        minus = sb("minus", [P, TT])
        xn = sb("xn", [P, TT, D])
        norm = LayerNorm(nc, ctx, "a_norm")
        xnT = sb("xnT", [P, KC, S])
        q_tok = sb("q_tok", [P, TT, H, HD + XRP])
        k_tok = sb("k_tok", [P, TT, KV, 3, HD])
        v = sb("v", [P, TT, KV * HD])
        kA = sb("kA", [P, KV, S], F32R)
        kB = sb("kB", [XR, KV, S], F32R)
        qA = sb("qA", [P, RG, S], F32R)
        qB = sb("qB", [XR, RG, S], F32R)
        probs = sb("probs", [P, UQ, S])
        rot_c = probs[:, 0:2, :]
        rot_s = probs[:, 2:4, :]
        rot = probs[:, 4:6, :]
        maxes = sb("maxes", [P, H, TT])
        junk = sb("junk", [P, 2, S], BF16)
        den = sb("den", [P, S])
        rden = sb("rden", [P, S])
        oT = sb("oT", [P, QUADS, 2, S])
        positions, slope_cols = oT[:, 0, 0, :], oT[:, 0, 1, 0:H]
        part_cols = oT[:, 1, 0, 0:2 * H].rearrange("p (h a) -> p h a", a=2)
        const_rows = oT[HD:XR, 1, 1, :]
        acc = sb("acc", [P, TT, D])
        fed = sb("fed", [P, TT, D])
        rows_of = sb("rows_of", [P, TT], I32)

        psS = ps("psS", [P, 3, S])
        psR = ps("psR", [P, 2, S])
        psO = ps("psO", [P, 2, S])
        psD = ps("psD", [P, S])

        staged = ctx.enter_context(nc.semaphore("a_staged"))
        loads = ctx.enter_context(nc.semaphore("a_loads"))
        wo_in = ctx.enter_context(nc.semaphore("a_wo_in"))
        slopes_set = ctx.enter_context(nc.semaphore("a_slopes_set"))
        rows_made = ctx.enter_context(nc.semaphore("a_rows_made"))
        alibi_made = ctx.enter_context(nc.semaphore("a_alibi_made"))
        passed = ctx.enter_context(nc.semaphore("a_passed"))
        ones_made = ctx.enter_context(nc.semaphore("a_ones_made"))
        STAGED, LOADS, WO_LOADS = 5 * 16, 4 * 16, 2 * GRP * 16
        x_in = sig("x_in", 1, step=16)
        xn_done = sig("xn_done", TT)
        xnT_ps = sig("xnT_ps", KC, credit=1)
        xnT_sb = sig("xnT_sb", KC)
        proj_ps = sig("proj_ps", NB)
        rot_mul = sig("rot_mul", NB)
        rot_half = sig("rot_half", NB)
        rot_sum = sig("rot_sum", NB, credit=2)
        hi_done = sig("hi_done", NB)
        lo_done = sig("lo_done", NB, credit=2)
        v_done = sig("v_done", TT)
        kT_ps = sig("kT_ps", 2 * KV)
        kA_done = sig("kA_done", KV)
        kB_done = sig("kB_done", KV)
        qAT_ps = sig("qAT_ps", H)
        qA_done = sig("qA_done", H)
        max_ps = sig("max_ps", QUADS * MQ)
        max_done = sig("max_done", QUADS * MQ, credit=2)
        neg_done = sig("neg_done", H)
        qBT_ps = sig("qBT_ps", H)
        qB_done = sig("qB_done", H)
        score_ps = sig("score_ps", QUADS * UQ)
        exp_done = sig("exp_done", QUADS * UQ, credit=3)
        pv_done = sig("pv_done", QUADS * TT, credit=TT)
        added = sig("added", ADDED * (TT - 1) * GRP)
        sums_ps = sig("sums_ps", QUADS, credit=1)
        den_taken = sig("den_taken", QUADS, credit=1)
        o_taken = sig("o_taken", QUADS, credit=1)
        rden_done = sig("rden_done", QUADS, credit=1)
        norm_done = sig("norm_done", QUADS, credit=1)
        out_ps = sig("out_ps", 2)
        acc_done = sig("acc_done", 2, credit=1)
        res_in = sig("res_in", 1, step=16)
        rows_known = sig("rows_known", 1)
        fed_in = sig("fed_in", TT, step=16)
        fed_added = sig("fed_added", 1, credit=1)
        stored = sig("stored", 1, credit=1, step=16)

        def rotated(n):
            return (n, None, KV * HD) if n < TT else (n % TT, n // TT - 1, 512)

        rows = x.rearrange("b (t p) d -> b p t d", p=P)
        out_rows = result.rearrange("b (t p) d -> b p t d", p=P)
        def passes(engine, batch):
            with engine.Fori(0, B - 1) as b:
                batch(b, True)
            batch(B - 1, False)

        block = ctx.enter_context(nc.Block())

        @block.sync
        def _(sp):
            stored.grant(sp)
            sp.dma_start(xn[:, :, :], rows[0]).then_inc(x_in.sem, 16)
            sp.dma_start(idn[:, :], ident).then_inc(staged, 16)
            sp.dma_start(positions, key_rows[1].partition_broadcast(P)).then_inc(staged, 16)
            sp.dma_start(slope_cols, slopes.partition_broadcast(P)).then_inc(staged, 16)
            sp.dma_start(part_cols, slope_parts.partition_broadcast(P)).then_inc(staged, 16)
            sp.dma_start(const_rows, key_rows).then_inc(staged, 16)
            sp.dma_start(wkv[:, :, 0:KV * HD], Wk.rearrange("(c p) n -> p c n", p=P)).then_inc(loads, 16)
            sp.dma_start(wkv[:, :, KV * HD:], Wv.rearrange("(c p) n -> p c n", p=P)).then_inc(loads, 16)
            sp.dma_start(rope_t[:, :, :, :].rearrange("p k t n -> p (k t) n"),
                         rope.rearrange("k (t p) n -> p (k t) n", p=P)).then_inc(loads, 16)
            sp.dma_start(wq[:, :, :], Wq.rearrange("(c p) n -> p c n", p=P)).then_inc(loads, 16)
            heads = Wo.rearrange("(q e a d) n -> e a d q n", e=GRP, a=2, d=HALF)
            for e in range(GRP):
                for a in range(2):
                    sp.dma_start(wo[e * HALF:(e + 1) * HALF, :, a, :], heads[e, a]).then_inc(wo_in, 16)

            def batch(b, more):
                if more:
                    sp.wait_ge(xnT_ps.sem, xnT_ps.at(b, KC - 1))
                    sp.dma_start(xn[:, :, :], rows[b + 1]).then_inc(x_in.sem, 16)
                sp.wait_ge(stored.sem, stored.at(b, -1))
                sp.dma_start(acc[:, :, :], rows[b]).then_inc(res_in.sem, 16)
                sp.wait_ge(acc_done.sem, acc_done.at(b, 1))
                sp.dma_start(out_rows[b], acc[:, :, :]).then_inc(stored.sem, 16)

            passes(sp, batch)
            sp.wait_ge(stored.sem, stored.at(B - 1, 0))

        @block.gpsimd
        def _(pool):
            rot_sum.grant(pool)
            norm_done.grant(pool)
            fed_added.grant(pool)
            nc.gpsimd.memset(ones[:, :], 1.0).then_inc(ones_made, 1)
            nc.gpsimd.memset(minus[:, :], -1.0).then_inc(ones_made, 1)
            pool.wait_ge(ones_made, 2)
            norm.set_power(pool)
            norm.raise_variance(pool, 0)
            pool.wait_ge(staged, STAGED)
            for t in range(TT):
                nc.gpsimd.tensor_copy(q_tok[:, t, :, 2 * HD + 1:HD + XR], part_cols).then_inc(slopes_set, 1)
            pool.wait_ge(slopes_set, TT)

            def rotate(b, n):
                t, i, w = rotated(n)
                pool.wait_ge(rot_half.sem, rot_half.at(b, n))
                pool.wait_ge(lo_done.sem, lo_done.at(b, n - 2))
                nc.gpsimd.tensor_tensor(rot[:, n % 2, 0:w], rot_c[:, n % 2, 0:w], rot_s[:, n % 2, 0:w],
                                        ALU.add).then_inc(rot_sum.sem, 1)

            def gather_fed(b):
                pool.wait_ge(fed_added.sem, fed_added.at(b, -1))
                pool.sem_inc(passed, 1)
                nc.gpsimd.tensor_copy(rows_of[:, :], place[:, bass.ds(b * TT, TT)]).then_inc(rows_known.sem, 1)
                pool.wait_ge(rows_known.sem, rows_known.at(b, 0))
                pool.sem_inc(passed, 1)
                for t in range(TT):
                    nc.gpsimd.indirect_dma_start(
                        out=fed[:, t, :], out_offset=None, in_=sorted_z,
                        in_offset=bass.IndirectOffsetOnAxis(ap=rows_of[:, t:t + 1], axis=0))\
                        .then_inc(fed_in.sem, 16)

            def add_fed(b):
                pool.wait_ge(fed_in.sem, fed_in.at(b, TT - 1))
                pool.wait_ge(res_in.sem, res_in.at(b, 0))
                nc.gpsimd.tensor_tensor(acc[:, :, :], acc[:, :, :], fed[:, :, :], ALU.add).then_inc(fed_added.sem, 1)

            def negate(b, h):
                pool.wait_ge(max_done.sem, max_done.at(b, TT * h + TT - 1))
                nc.gpsimd.tensor_tensor(q_tok[:, :, h, 2 * HD], maxes[:, h, :], minus[:, :],
                                        ALU.mult).then_inc(neg_done.sem, 1)

            def normalize(b, quad):
                pool.wait_ge(rden_done.sem, rden_done.at(b, quad))
                nc.gpsimd.tensor_tensor(oT[:, quad, :, :], oT[:, quad, :, :],
                                        rden[:, :].unsqueeze(1).to_broadcast([P, 2, S]),
                                        ALU.mult).then_inc(norm_done.sem, 1)

            def add_tiles(b, quad, j, heads):
                for e in heads:
                    pool.wait_ge(pv_done.sem, pv_done.at(b, TT * quad + j))
                    if j > 1:
                        pool.wait_ge(added.sem, added.at(b, (quad * (TT - 1) + j - 2) * GRP + e))
                    slot = probs[:, GRP * j + e, :]
                    nc.gpsimd.tensor_tensor(slot, slot, probs[:, GRP * (j - 1) + e, :],
                                            ALU.add).then_inc(added.sem, 1)

            def prepare(b, before=None):
                for n in range(NB):
                    if n == 1 and before is not None:
                        normalize(before, QUADS - 1)
                    rotate(b, n)
                for h in range(GRP):
                    negate(b, h)

            def batch(b, more):
                gather_fed(b)
                for quad in range(QUADS):
                    if quad > 0:
                        add_tiles(b, quad - 1, 2, range(GRP))
                    for h in range(GRP):
                        if quad + 1 < QUADS:
                            negate(b, GRP * (quad + 1) + h)
                        if quad > 0 and h < 2:
                            add_tiles(b, quad - 1, 3, (2 * h, 2 * h + 1))
                    if quad > 1:
                        normalize(b, quad - 2)
                    if quad < ADDED:
                        add_tiles(b, quad, 1, range(GRP))
                    if quad == NORM_AT:
                        if more:
                            norm.raise_variance(pool, b + 1)
                        add_fed(b)
                normalize(b, QUADS - 2)
                if more:
                    prepare(b + 1, b)
                else:
                    normalize(b, QUADS - 1)

            prepare(0)
            passes(pool, batch)

        @block.scalar
        def _(act):
            exp_done.grant(act)
            o_taken.grant(act)
            den_taken.grant(act)
            act.wait_ge(staged, STAGED)
            for g in range(KV):
                nc.scalar.copy(kB[HD:XR, g, :], const_rows).then_inc(rows_made, 1)
            act.wait_ge(rows_made, KV)

            def take_xnT(b):
                for c in range(KC):
                    act.wait_ge(xnT_ps.sem, xnT_ps.at(b, c))
                    nc.scalar.copy(xnT[:, c, :], psR[:, c, :]).then_inc(xnT_sb.sem, 1)

            def high_part(b, n):
                t, i, w = rotated(n)
                if i is None:
                    act.wait_ge(rot_half.sem, rot_half.at(b, n))
                    nc.scalar.copy(v[:, t, :], psS[:, n % 3, KV * HD:]).then_inc(v_done.sem, 1)
                act.wait_ge(rot_sum.sem, rot_sum.at(b, n))
                src = rot[:, n % 2, 0:w].rearrange("p (h d) -> p h d", d=HD)
                if i is None:
                    high = k_tok[:, t, :, 1:3, :]
                    src = src.unsqueeze(2).to_broadcast([P, KV, 2, HD])
                else:
                    high = q_tok[:, t, i * 8:i * 8 + 8, HD:2 * HD]
                nc.scalar.copy(high.bitcast(F32R), src).then_inc(hi_done.sem, 1)

            def take(b, kind, n):
                if kind == "K":
                    act.wait_ge(kT_ps.sem, kT_ps.at(b, 2 * n))
                    nc.scalar.copy(kA[:, n, :], psR[:, bank_of(kind, n), :]).then_inc(kA_done.sem, 1)
                elif kind == "L":
                    act.wait_ge(kT_ps.sem, kT_ps.at(b, 2 * n + 1))
                    nc.scalar.copy(kB[0:HD, n, :], psR[0:HD, bank_of(kind, n), :]).then_inc(kB_done.sem, 1)
                elif kind == "A":
                    act.wait_ge(qAT_ps.sem, qAT_ps.at(b, n))
                    nc.scalar.copy(qA[:, n % RG, :], psR[:, bank_of(kind, n), :]).then_inc(qA_done.sem, 1)
                elif kind == "B":
                    act.wait_ge(qBT_ps.sem, qBT_ps.at(b, n))
                    nc.scalar.copy(qB[:, n % RG, :], psR[0:XR, bank_of(kind, n), :]).then_inc(qB_done.sem, 1)

            def take_output(b, quad):
                act.wait_ge(pv_done.sem, pv_done.at(b, TT * quad + TT - 1))
                nc.scalar.copy(oT[:, quad, :, :], psO[:, :, :]).then_inc(o_taken.sem, 1)

            def take_sums(b, quad):
                act.wait_ge(sums_ps.sem, sums_ps.at(b, quad))
                act.wait_ge(rden_done.sem, rden_done.at(b, quad - 1))
                nc.scalar.copy(den[:, :], psD[:, :]).then_inc(den_taken.sem, 1)

            def prepare(b):
                take_xnT(b)
                for n in range(NB):
                    for item in SIDE_AFTER.get(n, ()):
                        take(b, *item)
                    high_part(b, n)
                for item in SIDE_BEFORE:
                    take(b, *item)

            def batch(b, more):
                for quad in range(QUADS):
                    for slot in range(UQ):
                        act.wait_ge(score_ps.sem, score_ps.at(b, UQ * quad + slot))
                        j, e = divmod(slot, GRP)
                        if e == 0 and quad > 0 and j + 1 < TT:
                            act.wait_ge(added.sem, added.at(b, ((quad - 1) * (TT - 1) + j) * GRP + GRP - 1))
                        elif e == 0:
                            act.wait_ge(sums_ps.sem, sums_ps.at(b, quad - 1))
                        nc.scalar.activation(probs[:, slot, :], psS[:, (UQ * quad + slot) % 3, :],
                                             ACT.Exp).then_inc(exp_done.sem, 1)
                        for item in side(quad, slot):
                            take(b, *item)
                        if slot == 3 and quad > 0:
                            take_output(b, quad - 1)
                        if slot == SUM_AT + 1 and quad > 0:
                            take_sums(b, quad - 1)
                take_output(b, QUADS - 1)
                take_sums(b, QUADS - 1)
                if more:
                    prepare(b + 1)

            prepare(0)
            act.wait_ge(alibi_made, H)
            act.wait_ge(slopes_set, TT)
            passes(act, batch)

        @block.vector
        def _(dve):
            max_done.grant(dve)
            lo_done.grant(dve)
            rden_done.grant(dve)
            acc_done.grant(dve)
            def rotate(b, n):
                t, i, w = rotated(n)
                k, hw = (3 if i is None else 0), w // (HD // 2)
                dve.wait_ge(proj_ps.sem, proj_ps.at(b, n))
                dve.wait_ge(rot_sum.sem, rot_sum.at(b, n - 2))
                halves = psS[:, n % 3, 0:w].rearrange("p (h d) -> p h d", d=HD // 2)
                cos = rope_t[:, k, t, :].unsqueeze(1).to_broadcast([P, hw, HD // 2])
                nc.vector.tensor_tensor(rot_c[:, n % 2, 0:w].rearrange("p (h d) -> p h d", d=HD // 2),
                                        halves, cos, ALU.mult).then_inc(rot_mul.sem, 1)
                pairs = psS[:, n % 3, 0:w].rearrange("p (h a d) -> p h a d", a=2, d=HD // 2)
                out = rot_s[:, n % 2, 0:w].rearrange("p (h a d) -> p h a d", a=2, d=HD // 2)
                for a in range(2):
                    sin = rope_t[:, k + 1 + a, t, :].unsqueeze(1).to_broadcast([P, hw // 2, HD // 2])
                    last = nc.vector.tensor_tensor(out[:, :, a, :], pairs[:, :, 1 - a, :], sin, ALU.mult)
                last.then_inc(rot_half.sem, 1)

            def low_part(b, n):
                t, i, w = rotated(n)
                dve.wait_ge(hi_done.sem, hi_done.at(b, n))
                src = rot[:, n % 2, 0:w].rearrange("p (h d) -> p h d", d=HD)
                if i is None:
                    low, high = k_tok[:, t, :, 0, :], k_tok[:, t, :, 1, :]
                else:
                    hs = slice(i * 8, i * 8 + 8)
                    low, high = q_tok[:, t, hs, 0:HD], q_tok[:, t, hs, HD:2 * HD]
                nc.vector.tensor_tensor(low, src, high, ALU.subtract).then_inc(lo_done.sem, 1)

            def take_max(b, m):
                h, c = divmod(m, TT)
                dve.wait_ge(max_ps.sem, max_ps.at(b, m))
                dve.wait_ge(max_done.sem, max_done.at(b, m - 2))
                dve.sem_inc(passed, 1)
                nc.vector.tensor_tensor_reduce(
                    out=junk[:, m % 2, :], in0=psR[:, bank_of("max", m), :], in1=alibi[:, h, :], scale=1.0,
                    scalar=-3.0e38, op0=ALU.add, op1=ALU.max,
                    accum_out=maxes[:, h, c:c + 1]).then_inc(max_done.sem, 1)

            def invert_sums(b, quad):
                dve.wait_ge(den_taken.sem, den_taken.at(b, quad))
                dve.wait_ge(norm_done.sem, norm_done.at(b, quad - 1))
                nc.vector.reciprocal(rden[:, :], den[:, :]).then_inc(rden_done.sem, 1)

            dve.wait_ge(x_in.sem, x_in.at(0, 0))
            norm.statistics(dve, 0, xn)
            norm.apply(dve, 0, xn, xn, xn_done)
            dve.wait_ge(staged, STAGED)
            for h in range(H):
                nc.vector.tensor_scalar(alibi[:, h, :], positions, slope_cols[:, h:h + 1], None,
                                        ALU.mult).then_inc(alibi_made, 1)
            dve.wait_ge(alibi_made, H)
            dve.wait_ge(loads, LOADS)
            def add_output(b, k):
                if k == 0:
                    dve.wait_ge(fed_added.sem, fed_added.at(b, 0))
                dve.wait_ge(out_ps.sem, out_ps.at(b, k))
                nc.vector.tensor_tensor(acc[:, 2 * k:2 * k + 2, :], acc[:, 2 * k:2 * k + 2, :],
                                        psO[:, k, :].rearrange("p (t d) -> p t d", d=D),
                                        ALU.add).then_inc(acc_done.sem, 1)

            def prepare(b, before=None):
                def take_maxima(items):
                    for kind, m in items:
                        if kind == "max":
                            take_max(b, m)
                            if m % (MQ // 2) == MQ // 2 - 1 and before is not None:
                                add_output(before, m // (MQ // 2))

                for n in range(NB):
                    rotate(b, n)
                    if n >= 2:
                        low_part(b, n - 2)
                    take_maxima(SIDE_AFTER.get(n, ()))
                low_part(b, NB - 2)
                low_part(b, NB - 1)
                take_maxima(SIDE_BEFORE)

            def batch(b, more):
                for quad in range(QUADS):
                    if quad + 1 < QUADS:
                        for m in range(MQ):
                            take_max(b, (quad + 1) * MQ + m)
                    if quad == NORM_AT and more:
                        dve.wait_ge(x_in.sem, x_in.at(b + 1, 0))
                        norm.statistics(dve, b + 1, xn)
                        norm.apply(dve, b + 1, xn, xn, xn_done)
                    if quad > 0:
                        invert_sums(b, quad - 1)
                invert_sums(b, QUADS - 1)
                if more:
                    prepare(b + 1, b)
                else:
                    for k in range(2):
                        add_output(b, k)

            prepare(0)
            passes(dve, batch)

        @block.tensor
        def _(pe):
            xnT_ps.grant(pe)
            pv_done.grant(pe)
            sums_ps.grant(pe)
            pe.wait_ge(staged, STAGED)
            pe.wait_ge(ones_made, 1)
            pe.wait_ge(rows_made, KV)
            def transpose_rows(b):
                for t in range(TT):
                    pe.wait_ge(xn_done.sem, xn_done.at(b, t))
                    for c in range(KC):
                        last = nc.tensor.transpose(psR[:, c, t * P:(t + 1) * P], xn[:, t, c * P:(c + 1) * P],
                                                   idn[:, :])
                        if t == TT - 1:
                            last.then_inc(xnT_ps.sem, 1)

            def project(b, n):
                t, i, w = rotated(n)
                if n == 0:
                    pe.wait_ge(xnT_sb.sem, xnT_sb.at(b, KC - 1))
                if n >= 3:
                    pe.wait_ge(rot_half.sem, rot_half.at(b, n - 3))
                    if n - 3 < TT:
                        pe.wait_ge(v_done.sem, v_done.at(b, n - 3))
                for c in range(KC):
                    rhs = wkv[:, c, :] if i is None else wq[:, c, i * 512:(i + 1) * 512]
                    last = nc.tensor.matmul(psS[:, n % 3, :], xnT[:, c, t * P:(t + 1) * P], rhs,
                                            start=(c == 0), stop=(c == KC - 1))
                last.then_inc(proj_ps.sem, 1)

            reader = {"K": kA_done, "L": kB_done, "A": qA_done, "B": qB_done, "max": max_done}

            def do(b, kind, n):
                use = ring.index((kind, n))
                if use >= 2:
                    before, i = ring[use - 2]
                    pe.wait_ge(reader[before].sem, reader[before].at(b, i))
                bank = bank_of(kind, n)
                if kind in "KL":
                    if n == 0:
                        pe.wait_ge(lo_done.sem, lo_done.at(b, TT - 1))
                    first = 1 if kind == "K" else 0
                    for t in range(TT):
                        src = k_tok[:, t, n, first:first + 2, :].rearrange("p a d -> p (a d)")
                        last = nc.tensor.transpose(psR[:, bank, t * P:(t + 1) * P], src, idn[:, :])
                    last.then_inc(kT_ps.sem, 1)
                elif kind == "A":
                    if n in (0, H // 2):
                        pe.wait_ge(lo_done.sem, lo_done.at(b, (2 if n == 0 else 3) * TT - 1))
                    for t in range(TT):
                        last = nc.tensor.transpose(psR[:, bank, t * P:(t + 1) * P],
                                                   q_tok[:, t, n, 0:2 * HD], idn[:, :])
                    last.then_inc(qAT_ps.sem, 1)
                elif kind == "B":
                    pe.wait_ge(neg_done.sem, neg_done.at(b, n))
                    for t in range(TT):
                        last = nc.tensor.transpose(psR[0:XR, bank, t * P:(t + 1) * P],
                                                   q_tok[:, t, n, HD:HD + XR], idn[:, :])
                    last.then_inc(qBT_ps.sem, 1)
                else:
                    h, c = divmod(n, TT)
                    if n % MQ == 0:
                        pe.wait_ge(kA_done.sem, kA_done.at(b, h // GRP))
                    if c == 0:
                        pe.wait_ge(qA_done.sem, qA_done.at(b, h))
                    nc.tensor.matmul(psR[:, bank, :], qA[:, h % RG, c * P:(c + 1) * P], kA[:, h // GRP, :],
                                     start=True, stop=True).then_inc(max_ps.sem, 1)

            def scores(b, quad, slot):
                i, (j, e) = UQ * quad + slot, divmod(slot, GRP)
                h, keys, bank = GRP * quad + e, slice(j * P, (j + 1) * P), psS[:, i % 3, :]
                pe.wait_ge(exp_done.sem, exp_done.at(b, i - 3))
                if slot == 0:
                    pe.wait_ge(kB_done.sem, kB_done.at(b, quad))
                if j == 0:
                    pe.wait_ge(qB_done.sem, qB_done.at(b, h))
                nc.tensor.matmul(bank, kA[:, quad, keys], qA[:, h % RG, :], start=True, stop=False)
                nc.tensor.matmul(bank, kB[:, quad, keys], qB[:, h % RG, :], start=False,
                                 stop=True).then_inc(score_ps.sem, 1)

            def weigh(b, quad, j, part):
                if part == 0:
                    pe.wait_ge(exp_done.sem, exp_done.at(b, UQ * quad + GRP * j + GRP - 1))
                    if j == 0:
                        pe.wait_ge(o_taken.sem, o_taken.at(b, quad - 1))
                        if quad == 0:
                            pe.wait_ge(acc_done.sem, acc_done.at(b, -1))
                first = quad * HD + part * HALF
                for e in range(GRP):
                    last = nc.tensor.matmul(psO[e * HALF:(e + 1) * HALF, part, :], v[:, j, first:first + HALF],
                                            probs[:, GRP * j + e, :], start=(j == 0), stop=(j == TT - 1),
                                            tile_position=(0, e * HALF))
                if part == 1:
                    last.then_inc(pv_done.sem, 1)

            def sum_weights(b, quad):
                pe.wait_ge(den_taken.sem, den_taken.at(b, quad - 1))
                if quad < ADDED:
                    pe.wait_ge(added.sem, added.at(b, (quad + 1) * (TT - 1) * GRP - 1))
                tiles = [TT - 1] if quad < ADDED else range(TT)
                for j in tiles:
                    for e in range(GRP):
                        last = nc.tensor.matmul(psD[e * HALF:(e + 1) * HALF, :], ones[:, :], probs[:, GRP * j + e, :],
                                                start=(j == tiles[0]), stop=(j == TT - 1),
                                                tile_position=(0, e * HALF))
                last.then_inc(sums_ps.sem, 1)

            def project_output(b, n):
                t, k = divmod(n, 2 * QUADS)
                if n == 0:
                    pe.wait_ge(norm_done.sem, norm_done.at(b, QUADS - 1))
                last = nc.tensor.matmul(psO[:, t // 2, (t % 2) * D:(t % 2 + 1) * D],
                                        oT[:, k // 2, k % 2, t * P:(t + 1) * P], wo[:, k // 2, k % 2, :],
                                        start=(k == 0), stop=(k == 2 * QUADS - 1))
                if t % 2 and k == 2 * QUADS - 1:
                    last.then_inc(out_ps.sem, 1)

            def prepare(b, before=None):
                def do_all(items):
                    for kind, m in items:
                        do(b, kind, m)
                        if kind == "max" and before is not None:
                            for n in (2 * m, 2 * m + 1):
                                project_output(before, n)

                transpose_rows(b)
                if before is None:
                    pe.wait_ge(loads, LOADS)
                for n in range(NB):
                    project(b, n)
                    do_all(SIDE_AFTER.get(n, ()))
                do_all(SIDE_BEFORE)
                pe.wait_ge(lo_done.sem, lo_done.at(b, NB - 1))

            def batch(b, more):
                for quad in range(QUADS):
                    for slot in range(UQ):
                        scores(b, quad, slot)
                        j, e = divmod(slot, GRP)
                        items = side(quad, slot)
                        for item in items[:1]:
                            do(b, *item)
                        if e in (1, 3) and (quad or j):
                            weigh(b, *divmod(TT * quad + j - 1, TT), e // 2)
                        if slot == SUM_AT and quad > 0:
                            sum_weights(b, quad - 1)
                        for item in items[1:]:
                            do(b, *item)
                for part in range(2):
                    weigh(b, QUADS - 1, TT - 1, part)
                sum_weights(b, QUADS - 1)
                if more:
                    prepare(b + 1, b)
                else:
                    for n in range(2 * QUADS * TT):
                        project_output(b, n)

            prepare(0)
            pe.wait_ge(wo_in, WO_LOADS)
            passes(pe, batch)


def plain_attention_phase(nc, x, w, ident, x1, sorted_x, preloads, preloaded):
    NB = TT + TT // 2
    QUADS = H // 4
    MP = 2 * TT
    MQ = 2 * MP
    UQ = 8
    NEG = 3 * FH
    RING = 3
    SHIFT_AFTER = MP + 2
    with ExitStack() as ctx:
        def sb(name, shape, dt=F32):
            return ctx.enter_context(nc.sbuf_tensor("f_" + name, shape, dt))

        def ps(name, shape):
            return ctx.enter_context(nc.psum_tensor("f_" + name, shape, F32))

        def sig(name, per, credit=0, step=1):
            return Signal(ctx, nc, "f_" + name, per, credit, step)

        wqk = sb("wqk", [P, KC, 2 * D])
        wv = sb("wv", [P, KC, D])
        wo = sb("wo", [P, QUADS, D])
        bqk = sb("bqk", [P, 2 * D])
        bv, bo, g1, b1 = (sb(n, [P, D]) for n in ("bv", "bo", "g1", "b1"))
        idn = sb("idn", [P, P])
        zeros = sb("zeros", [P, D])
        norm0, norm1 = LayerNorm(nc, ctx, "f_norm0"), LayerNorm(nc, ctx, "f_norm1")
        xn = sb("xn", [P, TT, D])
        xnb = sb("xnb", [P, TT, D])
        xnT = sb("xnT", [P, KC, S])
        qk = sb("qk", [P, 2, 2 * D])
        q_tok = sb("q_tok", [P, TT, H, FB])
        k_tok = sb("k_tok", [P, TT, H, FB])
        v = sb("v", [P, TT, H, 2 * FH])
        kZ = sb("kZ", [P, 8, S], F32R)
        qM = sb("qM", [P, 2, S], F32R)
        qS = sb("qS", [P, 4, S], F32R)
        probs = sb("probs", [P, 8, 2, S])
        sums = sb("sums", [P, S])
        rsum = sb("rsum", [P, S])
        oT = sb("oT", [P, QUADS, S])
        r1 = sb("r1", [P, TT, D])

        psS = ps("psS", [P, 4, S])
        psR = ps("psR", [P, RING, S])
        psO = ps("psO", [P, S])

        loads = ctx.enter_context(nc.semaphore("f_loads"))
        wo_in = ctx.enter_context(nc.semaphore("f_wo_in"))
        zeroed = ctx.enter_context(nc.semaphore("f_zeroed"))
        cleared = ctx.enter_context(nc.semaphore("f_cleared"))
        passed = ctx.enter_context(nc.semaphore("f_passed"))
        scaled = ctx.enter_context(nc.semaphore("f_scaled"))
        LOADS = 10 * 16
        ZEROED = 7
        x_in = sig("x_in", 1, step=16)
        xn_done = sig("xn_done", TT)
        xnb_done = sig("xnb_done", 1, credit=1)
        xnT_ps = sig("xnT_ps", KC, credit=1)
        xnT_sb = sig("xnT_sb", KC)
        proj_ps = sig("proj_ps", NB)
        bias_done = sig("bias_done", NB)
        hi_done = sig("hi_done", TT)
        lo_done = sig("lo_done", TT, credit=2)
        neg_reset = sig("neg_reset", 1)
        kT_ps = sig("kT_ps", 2 * QUADS)
        kZ_done = sig("kZ_done", 2 * QUADS)
        qM_ps = sig("qM_ps", 2 * QUADS)
        qM_done = sig("qM_done", 2 * QUADS)
        max_ps = sig("max_ps", QUADS * MQ)
        max_done = sig("max_done", QUADS * MQ)
        qS_ps = sig("qS_ps", 2 * QUADS, credit=1)
        qS_done = sig("qS_done", 2 * QUADS)
        score_ps = sig("score_ps", QUADS * UQ)
        exp_done = sig("exp_done", QUADS * UQ, credit=2)
        pv_done = sig("pv_done", 2 * QUADS, credit=2)
        o_taken = sig("o_taken", QUADS, credit=1)
        sum_done = sig("sum_done", QUADS)
        rsum_done = sig("rsum_done", QUADS)
        norm_done = sig("norm_done", QUADS, credit=1)
        out_ps = sig("out_ps", 2)
        r1_done = sig("r1_done", 2, credit=1)
        n1_done = sig("n1_done", TT)
        gain_done = sig("gain_done", 1)
        x1_done = sig("x1_done", 1, credit=1)

        rows = x.rearrange("b (t p) d -> b p t d", p=P)
        def extras(quad, u):
            items = []
            if 2 * u + 2 == SHIFT_AFTER:
                items.append(("shifted", 2 * quad + 2))
            if quad + 2 < QUADS:
                items += {5: [("queries", 2 * quad + 4)], 6: [("keys", 2 * quad + 4)],
                          7: [("keys", 2 * quad + 5), ("queries", 2 * quad + 5)]}.get(u, [])
            return items

        ring = [(kind, p) for kind in ("keys", "queries") for p in (0, 1)]
        ring += [("max", m) for m in range(MQ)]
        ring.insert(4 + SHIFT_AFTER, ("shifted", 0))
        ring += [(kind, p) for kind in ("keys", "queries") for p in (2, 3)]
        for quad in range(QUADS):
            ring += [("shifted", 2 * quad + 1)]
            if quad + 1 < QUADS:
                for u in range(UQ):
                    ring += [("max", (quad + 1) * MQ + 2 * u + k) for k in (0, 1)] + extras(quad, u)
        reader = {"keys": kZ_done, "queries": qM_done, "max": max_done, "shifted": qS_done}

        def bank_of(kind, n):
            return ring.index((kind, n)) % RING

        def passes(engine, batch):
            with engine.Fori(0, B - 1) as b:
                batch(b, True)
            batch(B - 1, False)

        block = ctx.enter_context(nc.Block())

        @block.sync
        def _(sp):
            sp.dma_start(xn[:, :, :], rows[0]).then_inc(x_in.sem, 16)
            sp.dma_start(idn[:, :], ident).then_inc(loads, 16)
            sp.dma_start(wqk[:, :, 0:D], w["Wq"].rearrange("(c p) n -> p c n", p=P)).then_inc(loads, 16)
            sp.dma_start(wqk[:, :, D:], w["Wk"].rearrange("(c p) n -> p c n", p=P)).then_inc(loads, 16)
            sp.dma_start(wv[:, :, :], w["Wv"].rearrange("(c p) n -> p c n", p=P)).then_inc(loads, 16)
            sp.dma_start(bqk[:, 0:D], w["bq"].partition_broadcast(P)).then_inc(loads, 16)
            sp.dma_start(bqk[:, D:], w["bk"].partition_broadcast(P)).then_inc(loads, 16)
            for tile, name in ((bv, "bv"), (bo, "bo"), (g1, "ln1_g"), (b1, "ln1_b")):
                sp.dma_start(tile[:, :], w[name].partition_broadcast(P)).then_inc(loads, 16)
            sp.wait_ge(zeroed, ZEROED)
            heads = w["Wo"].rearrange("(q i d) n -> i d q n", i=4, d=FH)
            for i in range(4):
                sp.dma_start(wo[32 * i:32 * i + FH, :, :], heads[i]).then_inc(wo_in, 16)
            sp.dma_start(sorted_x.rearrange("(n p) d -> p n d", p=P),
                         zeros[:, :].unsqueeze(1).to_broadcast([P, TILES * TOK // P, D])).then_inc(cleared, 16)

            for tile, source in preloads:
                sp.dma_start(tile, source).then_inc(preloaded, 16)

            def batch(b, more):
                if more:
                    sp.wait_ge(xnT_ps.sem, xnT_ps.at(b, KC - 1))
                    sp.sem_inc(passed, 1)
                    sp.wait_ge(xnb_done.sem, xnb_done.at(b, 0))
                    sp.dma_start(xn[:, :, :], rows[b + 1]).then_inc(x_in.sem, 16)

            passes(sp, batch)
            sp.wait_ge(cleared, 16)

        @block.gpsimd
        def _(pool):
            lo_done.grant(pool)
            norm_done.grant(pool)
            xnb_done.grant(pool)
            x1_done.grant(pool)
            norm0.set_power(pool)
            norm1.set_power(pool)
            nc.gpsimd.memset(wo[:, :, :], 0.0).then_inc(zeroed, 1)
            nc.gpsimd.memset(zeros[:, :], 0.0).then_inc(zeroed, 1)
            nc.gpsimd.memset(q_tok[:, :, :, NEG + 1:], 0.0).then_inc(zeroed, 1)
            nc.gpsimd.memset(k_tok[:, :, :, NEG + 1:], 0.0).then_inc(zeroed, 1)
            nc.gpsimd.memset(k_tok[:, :, :, NEG], 1.0).then_inc(zeroed, 1)
            nc.gpsimd.memset(v[:, :, :, FH:], 1.0).then_inc(zeroed, 1)

            def xnb_sum(b):
                pool.wait_ge(r1_done.sem, r1_done.at(b, -1))
                pool.wait_ge(xn_done.sem, xn_done.at(b, TT - 1))
                bias = bo[:, :].unsqueeze(1).to_broadcast([P, TT, D])
                nc.gpsimd.tensor_tensor(xnb[:, :, :], xn[:, :, :], bias, ALU.add).then_inc(xnb_done.sem, 1)

            def low_parts(b, t):
                pool.wait_ge(hi_done.sem, hi_done.at(b, t))
                src = qk[:, t % 2, :].rearrange("p (a h d) -> p a h d", a=2, d=FH)
                nc.gpsimd.tensor_tensor(q_tok[:, t, :, FH:2 * FH], src[:, 0], q_tok[:, t, :, 0:FH], ALU.subtract)
                nc.gpsimd.tensor_tensor(k_tok[:, t, :, 2 * FH:NEG], src[:, 1], k_tok[:, t, :, 0:FH],
                                        ALU.subtract).then_inc(lo_done.sem, 1)

            def normalize(b, quad):
                pool.wait_ge(rsum_done.sem, rsum_done.at(b, quad))
                nc.gpsimd.tensor_tensor(oT[:, quad, :], oT[:, quad, :], rsum[:, :], ALU.mult)\
                    .then_inc(norm_done.sem, 1)

            def reset_maxima(b):
                pool.wait_ge(qS_ps.sem, qS_ps.at(b, -1))
                pool.sem_inc(passed, 1)
                nc.gpsimd.memset(q_tok[:, :, :, NEG], 0.0).then_inc(neg_reset.sem, 1)

            norm0.raise_variance(pool, 0)
            reset_maxima(0)
            pool.wait_ge(loads, LOADS)
            xnb_sum(0)
            for t in range(TT):
                low_parts(0, t)

            def batch(b, more):
                for quad in range(1, QUADS):
                    normalize(b, quad - 1)
                if more:
                    norm0.raise_variance(pool, b + 1)
                    reset_maxima(b + 1)
                    low_parts(b + 1, 0)
                normalize(b, QUADS - 1)
                if more:
                    for t in range(1, TT):
                        low_parts(b + 1, t)
                norm1.raise_variance(pool, b)
                if more:
                    xnb_sum(b + 1)
                pool.wait_ge(n1_done.sem, n1_done.at(b, TT - 1))
                x1_b = x1[:, bass.ds(b * TT, TT), :]
                gain, offset = (g[:, :].unsqueeze(1).to_broadcast([P, TT, D]) for g in (g1, b1))
                pool.sem_inc(passed, 1)
                nc.gpsimd.tensor_tensor(x1_b, r1[:, :, :], gain, ALU.mult).then_inc(gain_done.sem, 1)
                pool.wait_ge(gain_done.sem, gain_done.at(b, 0))
                pool.sem_inc(passed, 1)
                nc.gpsimd.tensor_tensor(x1_b, x1_b, offset, ALU.add).then_inc(x1_done.sem, 1)

            passes(pool, batch)

        @block.scalar
        def _(act):
            exp_done.grant(act)
            o_taken.grant(act)
            act.wait_ge(loads, LOADS)
            act.wait_ge(zeroed, ZEROED)
            nc.scalar.mul(wqk[:, :, 0:D], wqk[:, :, 0:D], FH ** -0.5).then_inc(scaled, 1)
            nc.scalar.mul(bqk[:, 0:D], bqk[:, 0:D], FH ** -0.5).then_inc(scaled, 1)

            def take_xnT(b):
                for c in range(KC):
                    act.wait_ge(xnT_ps.sem, xnT_ps.at(b, c))
                    nc.scalar.copy(xnT[:, c, :], psR[:, c, :]).then_inc(xnT_sb.sem, 1)

            def high_parts(b, t):
                act.wait_ge(bias_done.sem, bias_done.at(b, t))
                src = qk[:, t % 2, :].rearrange("p (a h d) -> p a h d", a=2, d=FH)
                q_high = q_tok[:, t, :, :].rearrange("p h (a c) -> p h a c", a=2)[:, :, :, 0:FH]
                k_high = k_tok[:, t, :, 0:2 * FH].rearrange("p h (a c) -> p h a c", a=2)
                nc.scalar.copy(q_high.bitcast(F32R), src[:, 0].unsqueeze(2).to_broadcast([P, H, 2, FH]))
                nc.scalar.copy(k_high.bitcast(F32R),
                               src[:, 1].unsqueeze(2).to_broadcast([P, H, 2, FH])).then_inc(hi_done.sem, 1)

            def take_keys(b, p):
                act.wait_ge(kT_ps.sem, kT_ps.at(b, p))
                nc.scalar.copy(kZ[0:FB, 2 * p % 8, :], psR[0:FB, bank_of("keys", p), :])
                nc.scalar.copy(kZ[FB:, (2 * p + 1) % 8, :], psR[FB:, bank_of("keys", p), :]).then_inc(kZ_done.sem, 1)

            def take_queries(b, p):
                act.wait_ge(qM_ps.sem, qM_ps.at(b, p))
                nc.scalar.copy(qM[:, p % 2, :], psR[:, bank_of("queries", p), :]).then_inc(qM_done.sem, 1)

            def take_shifted(b, p):
                act.wait_ge(qS_ps.sem, qS_ps.at(b, p))
                nc.scalar.copy(qS[:, p % 4, :], psR[:, bank_of("shifted", p), :]).then_inc(qS_done.sem, 1)

            take = {"keys": take_keys, "queries": take_queries, "shifted": take_shifted}

            def take_output(b, quad):
                act.wait_ge(pv_done.sem, pv_done.at(b, 2 * quad + 1))
                nc.scalar.copy(oT[:, quad, :], psO[:, :]).then_inc(o_taken.sem, 1)

            def prepare(b):
                take_xnT(b)
                for t in range(TT):
                    high_parts(b, t)
                for quad in (0, 1):
                    for p in (2 * quad, 2 * quad + 1):
                        take_keys(b, p)
                    for p in (2 * quad, 2 * quad + 1):
                        take_queries(b, p)
                    if quad == 0:
                        take_shifted(b, 0)

            def batch(b, more):
                for quad in range(QUADS):
                    nxt = quad + 1 < QUADS
                    for u in range(UQ):
                        i = UQ * quad + u
                        act.wait_ge(score_ps.sem, score_ps.at(b, i))
                        act.wait_ge(pv_done.sem, pv_done.at(b, 2 * (quad - 1) + u // 4))
                        nc.scalar.activation(probs[:, u, :, :], psS[:, 2 * (u % 2):2 * (u % 2) + 2, :],
                                             ACT.Exp).then_inc(exp_done.sem, 1)
                        if u == 0:
                            take_shifted(b, 2 * quad + 1)
                        if u == 3 and quad:
                            take_output(b, quad - 1)
                        if nxt:
                            for kind, p in extras(quad, u):
                                take[kind](b, p)
                take_output(b, QUADS - 1)
                if more:
                    prepare(b + 1)

            prepare(0)
            passes(act, batch)

        @block.vector
        def _(dve):
            r1_done.grant(dve)
            nc.vector.memset(kZ[:, :, :].bitcast(F32), 0.0).then_inc(zeroed, 1)

            def add_bias(b, n):
                dve.wait_ge(proj_ps.sem, proj_ps.at(b, n))
                if n < TT:
                    dve.wait_ge(lo_done.sem, lo_done.at(b, n - 2))
                    nc.vector.tensor_tensor(qk[:, n % 2, :], psS[:, n, :], bqk[:, :],
                                            ALU.add).then_inc(bias_done.sem, 1)
                    return
                for k in range(2):
                    last = nc.vector.tensor_tensor(
                        v[:, 2 * (n - TT) + k, :, 0:FH],
                        psS[:, n - TT, k * D:(k + 1) * D].rearrange("p (h d) -> p h d", d=FH),
                        bv[:, :].rearrange("p (h d) -> p h d", d=FH), ALU.add)
                last.then_inc(bias_done.sem, 1)

            def take_max(b, m):
                h, c = divmod(m, TT)
                dve.wait_ge(max_ps.sem, max_ps.at(b, m))
                nc.vector.tensor_reduce(q_tok[:, c, h, NEG:NEG + 1], psR[:, bank_of("max", m), :], AX.X, ALU.max,
                                        negate=True).then_inc(max_done.sem, 1)

            def invert_sums(b, quad):
                dve.wait_ge(o_taken.sem, o_taken.at(b, quad))
                dve.wait_ge(norm_done.sem, norm_done.at(b, quad - 1))
                dve.sem_inc(passed, 1)
                nc.vector.stream_shuffle(sums[:, :], oT[:, quad, :], [FH + i % FH for i in range(32)])\
                    .then_inc(sum_done.sem, 1)
                dve.wait_ge(sum_done.sem, sum_done.at(b, quad))
                nc.vector.reciprocal(rsum[:, :], sums[:, :]).then_inc(rsum_done.sem, 1)

            dve.wait_ge(x_in.sem, x_in.at(0, 0))
            norm0.statistics(dve, 0, xn)
            norm0.apply(dve, 0, xn, xn, xn_done)
            dve.wait_ge(loads, LOADS)
            dve.wait_ge(scaled, 2)
            for n in range(NB):
                add_bias(0, n)
            for m in range(MQ):
                take_max(0, m)

            def batch(b, more):
                for quad in range(QUADS):
                    if quad + 1 < QUADS:
                        for m in range(MQ):
                            take_max(b, (quad + 1) * MQ + m)
                    if quad:
                        invert_sums(b, quad - 1)
                if more:
                    dve.wait_ge(x_in.sem, x_in.at(b + 1, 0))
                    norm0.statistics(dve, b + 1, xn)
                    norm0.apply(dve, b + 1, xn, xn, xn_done)
                invert_sums(b, QUADS - 1)
                if more:
                    for n in range(NB):
                        add_bias(b + 1, n)
                dve.wait_ge(xnb_done.sem, xnb_done.at(b, 0))
                dve.wait_ge(x1_done.sem, x1_done.at(b, -1))
                for k in range(2):
                    if more:
                        for m in range(MP):
                            take_max(b + 1, k * MP + m)
                    dve.wait_ge(out_ps.sem, out_ps.at(b, k))
                    nc.vector.tensor_tensor(r1[:, 2 * k:2 * k + 2, :], xnb[:, 2 * k:2 * k + 2, :],
                                            (psO[:, :], psS[:, 2, :])[k].rearrange("p (t d) -> p t d", d=D),
                                            ALU.add).then_inc(r1_done.sem, 1)
                dve.wait_ge(r1_done.sem, r1_done.at(b, 1))
                norm1.statistics(dve, b, r1)
                norm1.apply(dve, b, r1, r1, n1_done)

            passes(dve, batch)

        @block.tensor
        def _(pe):
            xnT_ps.grant(pe)
            qS_ps.grant(pe)
            pv_done.grant(pe)
            pe.wait_ge(loads, LOADS)
            pe.wait_ge(scaled, 2)
            pe.wait_ge(zeroed, ZEROED)

            def transpose_rows(b):
                for t in range(TT):
                    pe.wait_ge(xn_done.sem, xn_done.at(b, t))
                    for c in range(KC):
                        last = nc.tensor.transpose(psR[:, c, t * P:(t + 1) * P], xn[:, t, c * P:(c + 1) * P],
                                                   idn[:, :])
                        if t == TT - 1:
                            last.then_inc(xnT_ps.sem, 1)

            def project(b, n):
                if n == 0:
                    pe.wait_ge(xnT_sb.sem, xnT_sb.at(b, KC - 1))
                if n >= TT:
                    pe.wait_ge(bias_done.sem, bias_done.at(b, n - TT))
                    for k in range(2):
                        t = 2 * (n - TT) + k
                        for c in range(KC):
                            last = nc.tensor.matmul(psS[:, n - TT, k * D:(k + 1) * D], xnT[:, c, t * P:(t + 1) * P],
                                                    wv[:, c, :], start=(c == 0), stop=(c == KC - 1))
                else:
                    for c in range(KC):
                        last = nc.tensor.matmul(psS[:, n, :], xnT[:, c, n * P:(n + 1) * P], wqk[:, c, :],
                                                start=(c == 0), stop=(c == KC - 1))
                last.then_inc(proj_ps.sem, 1)

            def transpose_pair(bank, src, p):
                for t in range(TT):
                    heads = src[:, t, 2 * p:2 * p + 2, :].rearrange("p h d -> p (h d)")
                    last = nc.tensor.transpose(psR[:, bank, t * P:(t + 1) * P], heads, idn[:, :])
                return last

            def bank_read(b, kind, n):
                use = ring.index((kind, n))
                if use >= RING:
                    before, i = ring[use - RING]
                    pe.wait_ge(reader[before].sem, reader[before].at(b, i))

            def keys(b, p):
                bank_read(b, "keys", p)
                transpose_pair(bank_of("keys", p), k_tok, p).then_inc(kT_ps.sem, 1)

            def queries(b, p):
                bank_read(b, "queries", p)
                transpose_pair(bank_of("queries", p), q_tok, p).then_inc(qM_ps.sem, 1)

            def scores_for_max(b, m):
                h, c = divmod(m, TT)
                if c == 0:
                    pe.wait_ge(qM_done.sem, qM_done.at(b, h // 2))
                bank_read(b, "max", m)
                nc.tensor.matmul(psR[:, bank_of("max", m), :], qM[:, h // 2 % 2, c * P:(c + 1) * P],
                                 kZ[:, h % 8, :], start=True, stop=True).then_inc(max_ps.sem, 1)

            def shifted(b, p):
                bank_read(b, "shifted", p)
                pe.wait_ge(max_done.sem, max_done.at(b, (p + 1) * MP - 1))
                transpose_pair(bank_of("shifted", p), q_tok, p).then_inc(qS_ps.sem, 1)

            def scores(b, quad, u):
                h, half = 4 * quad + u % 4, u // 4
                if quad == 0 and u < 2:
                    pe.wait_ge(bias_done.sem, bias_done.at(b, NB - 1))
                    pe.wait_ge(r1_done.sem, r1_done.at(b, -1))
                pe.wait_ge(exp_done.sem, exp_done.at(b, UQ * quad + u - 2))
                pe.wait_ge(qS_done.sem, qS_done.at(b, h // 2))
                for a in range(2):
                    j = 2 * half + a
                    last = nc.tensor.matmul(psS[:, 2 * (u % 2) + a, :], kZ[:, h % 8, j * P:(j + 1) * P],
                                            qS[:, h // 2 % 4, :], start=True, stop=True)
                last.then_inc(score_ps.sem, 1)

            def weigh(b, quad, j):
                if j % 2 == 0:
                    pe.wait_ge(exp_done.sem, exp_done.at(b, UQ * quad + 2 * j + 3))
                if j == 0:
                    pe.wait_ge(o_taken.sem, o_taken.at(b, quad - 1))
                    if quad == 0:
                        pe.wait_ge(r1_done.sem, r1_done.at(b, -1))
                for e in range(4):
                    last = nc.tensor.matmul(psO[32 * e:32 * e + 32, :], v[:, j, 4 * quad + e, :],
                                            probs[:, 4 * (j // 2) + e, j % 2, :],
                                            start=(j == 0), stop=(j == TT - 1), tile_position=(0, 32 * e))
                if j % 2:
                    last.then_inc(pv_done.sem, 1)

            def project_output(b, n, more):
                t, quad = divmod(n, QUADS)
                if n == 0:
                    pe.wait_ge(norm_done.sem, norm_done.at(b, QUADS - 1))
                if n == 2 * QUADS and more:
                    pe.wait_ge(bias_done.sem, bias_done.at(b + 1, 2))
                bank = (psO[:, :], psS[:, 2, :])[t // 2]
                last = nc.tensor.matmul(bank[:, (t % 2) * D:(t % 2 + 1) * D], oT[:, quad, t * P:(t + 1) * P],
                                        wo[:, quad, :], start=(quad == 0), stop=(quad == QUADS - 1))
                if t % 2 and quad == QUADS - 1:
                    last.then_inc(out_ps.sem, 1)

            def prepare(b, before=None):
                transpose_rows(b)
                for n in range(NB):
                    project(b, n)
                pe.wait_ge(neg_reset.sem, neg_reset.at(b, 0))
                pe.wait_ge(lo_done.sem, lo_done.at(b, TT - 1))
                for p in (0, 1):
                    keys(b, p)
                for p in (0, 1):
                    queries(b, p)
                for m in range(MQ):
                    if m == SHIFT_AFTER:
                        shifted(b, 0)
                    scores_for_max(b, m)
                    if before is not None:
                        project_output(before, m, True)
                for p in (2, 3):
                    keys(b, p)
                for p in (2, 3):
                    queries(b, p)

            transposes = {"keys": keys, "queries": queries, "shifted": shifted}

            def batch(b, more):
                for quad in range(QUADS):
                    nxt = quad + 1 < QUADS
                    for u in range(UQ):
                        scores(b, quad, u)
                        if u == 0:
                            shifted(b, 2 * quad + 1)
                        if nxt:
                            scores_for_max(b, (quad + 1) * MQ + 2 * u)
                        if u in (1, 2) and quad:
                            weigh(b, quad - 1, u + 1)
                        if u in (5, 6):
                            weigh(b, quad, u - 5)
                        if nxt:
                            scores_for_max(b, (quad + 1) * MQ + 2 * u + 1)
                            for kind, p in extras(quad, u):
                                transposes[kind](b, p)
                for j in (2, 3):
                    weigh(b, QUADS - 1, j)
                if more:
                    prepare(b + 1, b)
                else:
                    for n in range(TT * QUADS):
                        project_output(b, n, False)

            prepare(0)
            pe.wait_ge(wo_in, 4 * 16)
            passes(pe, batch)


class ExpertWeights:

    def __init__(self, nc, ctx, W1, b1, W2, b2, tile_expert):
        def sb(name, shape):
            return ctx.enter_context(nc.sbuf_tensor("w_" + name, shape, F32))

        self.nc, self.sources, self.tile_expert = nc, (W1, b1, W2, b2), tile_expert
        self.w1, self.w2 = sb("w1", [P, 2, KC, FF]), sb("w2", [P, 2, FF // P, D])
        self.o1_rows, self.o2 = sb("o1_rows", [FF // P, 2, P]), sb("o2", [P, 2, D])
        self.w_in = [Signal(ctx, nc, f"w_in{k}", 1, step=64) for k in range(2)]

    def load(self, sp, tile, k):
        W1, b1, W2, b2 = self.sources
        e = sp.value_load(self.tile_expert[0:1, bass.ds(tile, 1)], min_val=0, max_val=NE - 1)
        sp.dma_start(self.w1[:, k, :, :], W1[e].rearrange("(c p) n -> p c n", p=P)).then_inc(self.w_in[k].sem, 16)
        sp.dma_start(self.w2[:, k, :, :], W2[e].rearrange("(m p) n -> p m n", p=P)).then_inc(self.w_in[k].sem, 16)
        sp.dma_start(self.o1_rows[:, k, :], b1[e].rearrange("(m p) -> m p", p=P)).then_inc(self.w_in[k].sem, 16)
        sp.dma_start(self.o2[:, k, :], b2[e].partition_broadcast(P)).then_inc(self.w_in[k].sem, 16)


def routing_phase(nc, x1, tri, starts, rw, rb, preloaded, place, tile_expert, sorted_x, weights):
    CT = B * TT
    with ExitStack() as ctx:
        def sb(name, shape, dt=F32):
            return ctx.enter_context(nc.sbuf_tensor("r_" + name, shape, dt))

        ones = sb("ones", [P, P])
        weighed = sb("weighed", [P, 2, D])
        dots = sb("dots", [P, CT])
        key = sb("key", [P, CT])
        nearest_i = sb("nearest_i", [P, CT], I32)
        nearest = sb("nearest", [P, CT])
        above = sb("above", [P, CT])
        floor_i = sb("floor_i", [P, CT], I32)
        expert_i = sb("expert_i", [P, CT], I32)
        expert = sb("expert", [P, CT])
        hot = sb("hot", [P, NE, CT])
        total = sb("total", [P, NE * CT])
        upto = sb("upto", [P, NE * CT])
        ahead = sb("ahead", [P, NE * CT])
        count = sb("count", [P, NE])
        count_i = sb("count_i", [P, NE], I32)
        padded_i = sb("padded_i", [P, NE], I32)
        padded = sb("padded", [P, NE])
        end = sb("end", [P, NE])
        shift = sb("shift", [P, NE])
        row = sb("row", [P, NE, CT])
        row_f = sb("row_f", [P, CT])
        tile_f = sb("tile_f", [P, 2, TILES])
        psP = ctx.enter_context(nc.psum_tensor("r_psP", [P, NE * CT], F32))
        psT = ctx.enter_context(nc.psum_tensor("r_psT", [P, 512], F32))

        consts, dot_done, hot_done, sums_ps, chain, placed, scattered = (
            ctx.enter_context(nc.semaphore("r_" + n)) for n in
            ("consts", "dot_done", "hot_done", "sums_ps", "chain", "placed", "scattered"))
        block = ctx.enter_context(nc.Block())

        @block.sync
        def _(sp):
            sp.wait_ge(placed, 1)
            for k in range(2):
                weights.load(sp, k, k)

        @block.gpsimd
        def _(pool):
            nc.gpsimd.memset(ones[:, :], 1.0).then_inc(consts, 1)
            nc.gpsimd.memset(shift[:, :], 0.0).then_inc(consts, 1)
            pool.wait_ge(placed, 1)
            for c in range(CT):
                nc.gpsimd.indirect_dma_start(
                    out=sorted_x, out_offset=bass.IndirectOffsetOnAxis(ap=place[:, c:c + 1], axis=0),
                    in_=x1[:, c, :], in_offset=None).then_inc(scattered, 16)
            pool.wait_ge(scattered, 16 * CT)

        @block.tensor
        def _(pe):
            pe.wait_ge(preloaded, 64)
            pe.wait_ge(consts, 2)
            pe.wait_ge(hot_done, NE)
            tokens = hot[:, :, :].rearrange("p e c -> p (e c)")
            nc.tensor.matmul(psP[:, :], tri[:, :], tokens, start=True, stop=True)
            nc.tensor.matmul(psT[:, 0:NE * CT], ones[:, :], tokens, start=True, stop=True).then_inc(sums_ps, 1)

        @block.vector
        def _(dve):
            steps = [0]

            def link(instruction):
                steps[0] += 1
                instruction.then_inc(chain, 1)
                dve.wait_ge(chain, steps[0])

            dve.wait_ge(preloaded, 64)
            for c in range(CT):
                if c >= 2:
                    dve.wait_ge(dot_done, c - 1)
                nc.vector.tensor_tensor_reduce(out=weighed[:, c % 2, :], in0=x1[:, c, :], in1=rw[:, :], scale=1.0,
                                               scalar=0.0, op0=ALU.mult, op1=ALU.add,
                                               accum_out=dots[:, c:c + 1]).then_inc(dot_done, 1)
            dve.wait_ge(dot_done, CT)
            link(nc.vector.tensor_scalar(key[:, :], dots[:, :], rb[:, 0:1], None, ALU.add))
            link(nc.vector.tensor_copy(nearest_i[:, :], key[:, :]))
            link(nc.vector.tensor_copy(nearest[:, :], nearest_i[:, :]))
            link(nc.vector.tensor_tensor(above[:, :], nearest[:, :], key[:, :], ALU.is_gt))
            link(nc.vector.tensor_tensor(floor_i[:, :], nearest[:, :], above[:, :], ALU.subtract))
            link(nc.vector.tensor_scalar(expert_i[:, :], floor_i[:, :], NE - 1, None, ALU.bitwise_and))
            link(nc.vector.tensor_copy(expert[:, :], expert_i[:, :]))
            for e in range(NE):
                nc.vector.tensor_scalar(hot[:, e, :], expert[:, :], float(e), None, ALU.is_equal).then_inc(hot_done, 1)
            dve.wait_ge(sums_ps, 1)
            dve.wait_ge(consts, 2)
            link(nc.vector.tensor_copy(total[:, :], psT[:, 0:NE * CT]))
            link(nc.vector.tensor_tensor_scan(upto[:, :], ones[:, :], total[:, :], 0.0, ALU.mult, ALU.add))
            link(nc.vector.tensor_tensor(ahead[:, :], upto[:, :], total[:, :], ALU.subtract))
            ends = upto[:, :].rearrange("p (e c) -> p e c", c=CT)[:, :, CT - 1]
            link(nc.vector.tensor_copy(count[:, 0:1], ends[:, 0:1]))
            link(nc.vector.tensor_tensor(count[:, 1:NE], ends[:, 1:NE], ends[:, 0:NE - 1], ALU.subtract))
            link(nc.vector.tensor_scalar(count_i[:, :], count[:, :], float(TOK - 1), None, ALU.add))
            bits = TOK.bit_length() - 1
            link(nc.vector.tensor_scalar(padded_i[:, :], count_i[:, :], bits, bits,
                                         ALU.logical_shift_right, ALU.logical_shift_left))
            link(nc.vector.tensor_copy(padded[:, :], padded_i[:, :]))
            link(nc.vector.tensor_tensor_scan(end[:, :], ones[:, 0:NE], padded[:, :], 0.0, ALU.mult, ALU.add))
            link(nc.vector.tensor_tensor(shift[:, 1:NE], end[:, 0:NE - 1], ends[:, 0:NE - 1], ALU.subtract))
            flat = row[:, :, :].rearrange("p e c -> p (e c)")
            link(nc.vector.tensor_tensor(flat, psP[:, :], ahead[:, :], ALU.add))
            link(nc.vector.tensor_tensor(row[:, :, :], row[:, :, :],
                                         shift[:, :].unsqueeze(2).to_broadcast([P, NE, CT]), ALU.add))
            link(nc.vector.tensor_tensor(row[:, :, :], row[:, :, :], hot[:, :, :], ALU.mult))
            link(nc.vector.tensor_reduce(row_f[:, :], row[:, :, :].rearrange("p e c -> p c e"), AX.X, ALU.add))
            link(nc.vector.tensor_copy(place[:, :], row_f[:, :]))
            link(nc.vector.tensor_scalar(tile_f[:, 0, :], starts[:, :], end[:, 0:1], None, ALU.is_ge))
            link(nc.vector.scalar_tensor_tensor(tile_f[:, 1, :], starts[:, :], end[:, 1:2], tile_f[:, 0, :],
                                                ALU.is_ge, ALU.add))
            link(nc.vector.scalar_tensor_tensor(tile_f[:, 0, :], starts[:, :], end[:, 2:3], tile_f[:, 1, :],
                                                ALU.is_ge, ALU.add))
            nc.vector.tensor_copy(tile_expert[:, :], tile_f[:, 0, :]).then_inc(placed, 1)


def experts_phase(nc, weights, gain, offset, ident, sorted_x, sorted_z):
    MC = FF // P
    TC = TOK // P
    NG = MC // 2
    NW = KC * FF // 512
    LOOPED = (TILES - 3) // 2
    with ExitStack() as ctx:
        def sb(name, shape, dt=F32):
            return ctx.enter_context(nc.sbuf_tensor("e_" + name, shape, dt))

        def sig(name, per, credit=0, step=1):
            return Signal(ctx, nc, "e_" + name, per, credit, step)

        w1, w2, o1_rows, o2, w_in = weights.w1, weights.w2, weights.o1_rows, weights.o2, weights.w_in
        idn = sb("idn", [P, P])
        o1 = sb("o1", [P, 2, MC])
        xs = sb("xs", [P, 2, TC, D])
        h = sb("h", [P, MC, TOK])
        w1_high, w1_low = (sb(n, [P, 2, KC, FF], F32R) for n in ("w1_high", "w1_low"))
        w2_high, w2_low = (sb(n, [P, 2, MC, D], F32R) for n in ("w2_high", "w2_low"))
        xT_high, xT_low = (sb(n, [P, 2, KC, TOK], F32R) for n in ("xT_high", "xT_low"))
        h_high, h_low = (sb(n, [P, MC, TOK], F32R) for n in ("h_high", "h_low"))
        xo = sb("xo", [P, 2, TC, D])
        r2 = sb("r2", [P, 2, TC, D])
        z = sb("z", [P, 2, TC, D])
        g2, b2_norm = sb("g2", [P, D]), sb("b2_norm", [P, D])
        norm = LayerNorm(nc, ctx, "e_norm", TC, turns=2)
        psX = ctx.enter_context(nc.psum_tensor("e_psX", [P, 2, 512], F32))
        psH = ctx.enter_context(nc.psum_tensor("e_psH", [P, 4, 512], F32))
        psY = ctx.enter_context(nc.psum_tensor("e_psY", [P, 2, 512], F32))

        passed = ctx.enter_context(nc.semaphore("e_passed"))
        passed_sp = ctx.enter_context(nc.semaphore("e_passed_sp"))
        consts_in = ctx.enter_context(nc.semaphore("e_consts_in"))
        x_in = [sig(f"x_in{k}", 1, step=16) for k in range(2)]
        xT_ps = sig("xT_ps", 2)
        xT_sb = sig("xT_sb", 2)
        o1_ps = sig("o1_ps", 2)
        o1_sb = sig("o1_sb", 2)
        h_ps = sig("h_ps", MC)
        h_sb = sig("h_sb", MC, credit=4)
        h_split = sig("h_split", MC)
        h_rest = sig("h_rest", MC, credit=4)
        w_split = sig("w_split", 4 * NW)
        w1_rest = sig("w1_rest", 2 * NW)
        w2_rest = sig("w2_rest", 2 * NW)
        xT_split = sig("xT_split", 2)
        y_ps = sig("y_ps", 2)
        xo_done = sig("xo_done", 2)
        r2_done = sig("r2_done", 2, credit=2)
        normed = sig("normed", 2 * TC)
        gain_done = sig("gain_done", 2, credit=2)
        z_done = sig("z_done", 2)
        stored = [sig(f"stored{k}", 1, credit=1, step=16) for k in range(2)]
        x_tiles = sorted_x.rearrange("(i c p) d -> i p c d", p=P, c=TC)
        z_tiles = sorted_z.rearrange("(i c p) d -> i p c d", p=P, c=TC)
        block = ctx.enter_context(nc.Block())

        def at_place(i, k):
            return (i, k) if k < 2 else (i + 1, 0)

        def chunk(weights, place, q):
            return weights[:, place, :, :].rearrange("p a n -> p (a n)")[:, q * 512:(q + 1) * 512]

        def bank(tile, g):
            return tile[:, 2 * g:2 * g + 2, :].rearrange("p a n -> p (a n)")

        def tiles(engine, step):
            with engine.Fori(0, LOOPED) as i:
                for k in range(2):
                    step(i, k, 2)
            for t in range(2 * LOOPED, TILES):
                step(t // 2, t % 2, min(2, TILES - 1 - t))

        @block.sync
        def _(sp):
            for s in stored:
                s.grant(sp)
            sp.dma_start(idn[:, :], ident).then_inc(consts_in, 16)
            sp.dma_start(g2[:, :], gain.partition_broadcast(P)).then_inc(consts_in, 16)
            sp.dma_start(b2_norm[:, :], offset.partition_broadcast(P)).then_inc(consts_in, 16)

            def load_rows(i, k):
                sp.dma_start(xs[:, k, :, :], x_tiles[2 * i + k]).then_inc(x_in[k].sem, 16)

            def step(i, k, follow):
                if follow == 2:
                    for done, n in ((h_ps, NG * k), (w2_rest, NW * k + NW - 1), (xo_done, k)):
                        sp.wait_ge(done.sem, done.at(i, n))
                        sp.sem_inc(passed_sp, 1)
                    load_rows(i + 1, k)
                    weights.load(sp, 2 * (i + 1) + k, k)
                sp.wait_ge(z_done.sem, z_done.at(i, k))
                sp.dma_start(z_tiles[2 * i + k], z[:, k, :, :]).then_inc(stored[k].sem, 16)

            load_rows(0, 0)
            load_rows(0, 1)
            tiles(sp, step)
            last = divmod(TILES - 1, 2)
            sp.wait_ge(stored[last[1]].sem, stored[last[1]].at(last[0], 0))
            sp.wait_ge(stored[1 - last[1]].sem, stored[1 - last[1]].at((TILES - 2) // 2, 0))

        @block.scalar
        def _(act):
            h_sb.grant(act)

            def split_weights(i, k):
                i, place = at_place(i, k)
                act.wait_ge(w_in[place].sem, w_in[place].at(i, 0))
                for high, whole in ((w1_high, w1), (w2_high, w2)):
                    for q in range(NW):
                        nc.scalar.copy(chunk(high, place, q), chunk(whole, place, q)).then_inc(w_split.sem, 1)

            def step(i, k, follow):
                act.wait_ge(o1_ps.sem, o1_ps.at(i, k))
                nc.scalar.copy(o1[:, k, :], psY[:, k, 0:MC]).then_inc(o1_sb.sem, 1)
                act.wait_ge(o1_sb.sem, o1_sb.at(i, k))
                for g in range(NG):
                    n = NG * k + g
                    act.wait_ge(h_ps.sem, h_ps.at(i, n))
                    act.wait_ge(h_rest.sem, h_rest.at(i, n - NG))
                    for m in (2 * g, 2 * g + 1):
                        last = nc.scalar.activation(h[:, m, :], psH[:, g, m % 2 * TOK:(m % 2 + 1) * TOK],
                                                    ACT.Relu, bias=o1[:, k, m:m + 1])
                    last.then_inc(h_sb.sem, 1)
                    act.wait_ge(h_sb.sem, h_sb.at(i, n))
                    nc.scalar.copy(bank(h_high, g), bank(h, g)).then_inc(h_split.sem, 1)
                if follow:
                    split_weights(i, k + 1)

            split_weights(0, 0)
            tiles(act, step)

        @block.gpsimd
        def _(pool):
            gain_done.grant(pool)
            norm.set_power(pool)
            pool.wait_ge(consts_in, 48)
            wide = [P, TC, D]

            def residual(i, k):
                pool.wait_ge(x_in[k].sem, x_in[k].at(i, 0))
                pool.wait_ge(w_in[k].sem, w_in[k].at(i, 0))
                pool.wait_ge(r2_done.sem, r2_done.at(i, k - 2))
                nc.gpsimd.tensor_tensor(xo[:, k, :, :], xs[:, k, :, :], o2[:, k, :].unsqueeze(1).to_broadcast(wide),
                                        ALU.add).then_inc(xo_done.sem, 1)

            def split_rest(i, k):
                i, place = at_place(i, k)
                for q in range(NW):
                    pool.wait_ge(w_split.sem, w_split.at(i, 2 * NW * place + NW + q))
                    nc.gpsimd.tensor_tensor(chunk(w2_low, place, q), chunk(w2, place, q), chunk(w2_high, place, q),
                                            ALU.subtract).then_inc(w2_rest.sem, 1)

            def step(i, k, follow):
                residual(i, k)
                if follow:
                    split_rest(i, k + 1)
                norm.raise_variance(pool, i, k)
                pool.wait_ge(normed.sem, normed.at(i, TC * k + TC - 1))
                pool.wait_ge(stored[k].sem, stored[k].at(i, -1))
                nc.gpsimd.tensor_tensor(z[:, k, :, :], r2[:, k, :, :], g2[:, :].unsqueeze(1).to_broadcast(wide),
                                        ALU.mult).then_inc(gain_done.sem, 1)
                pool.wait_ge(gain_done.sem, gain_done.at(i, k))
                nc.gpsimd.tensor_tensor(z[:, k, :, :], z[:, k, :, :], b2_norm[:, :].unsqueeze(1).to_broadcast(wide),
                                        ALU.add).then_inc(z_done.sem, 1)

            split_rest(0, 0)
            tiles(pool, step)

        @block.vector
        def _(dve):
            r2_done.grant(dve)
            h_rest.grant(dve)

            def take_rows(i, k):
                i, place = at_place(i, k)
                dve.wait_ge(xT_ps.sem, xT_ps.at(i, place))
                high, low = (x[:, place, :, :].rearrange("p c n -> p (c n)") for x in (xT_high, xT_low))
                nc.vector.tensor_copy(high, psX[:, place, :]).then_inc(xT_split.sem, 1)
                dve.wait_ge(xT_split.sem, xT_split.at(i, place))
                nc.vector.tensor_tensor(low, psX[:, place, :], high, ALU.subtract).then_inc(xT_sb.sem, 1)

            def split_rest(i, k):
                i, place = at_place(i, k)
                for q in range(NW):
                    dve.wait_ge(w_split.sem, w_split.at(i, 2 * NW * place + q))
                    nc.vector.tensor_tensor(chunk(w1_low, place, q), chunk(w1, place, q), chunk(w1_high, place, q),
                                            ALU.subtract).then_inc(w1_rest.sem, 1)

            def step(i, k, follow):
                for g in range(NG):
                    dve.wait_ge(h_split.sem, h_split.at(i, NG * k + g))
                    nc.vector.tensor_tensor(bank(h_low, g), bank(h, g), bank(h_high, g),
                                            ALU.subtract).then_inc(h_rest.sem, 1)
                if follow:
                    take_rows(i, k + 1)
                    split_rest(i, k + 1)
                dve.wait_ge(y_ps.sem, y_ps.at(i, k))
                dve.wait_ge(xo_done.sem, xo_done.at(i, k))
                dve.wait_ge(gain_done.sem, gain_done.at(i, k - 2))
                nc.vector.tensor_tensor(r2[:, k, :, :], psY[:, k, :].rearrange("p (c n) -> p c n", c=TC),
                                        xo[:, k, :, :], ALU.add).then_inc(r2_done.sem, 1)
                dve.wait_ge(r2_done.sem, r2_done.at(i, k))
                norm.statistics(dve, i, r2[:, k, :, :], k)
                norm.apply(dve, i, r2[:, k, :, :], r2[:, k, :, :], normed, k)

            take_rows(0, 0)
            split_rest(0, 0)
            tiles(dve, step)

        @block.tensor
        def _(pe):
            pe.wait_ge(consts_in, 48)

            def transpose_tile(i, k):
                i, place = at_place(i, k)
                pe.wait_ge(x_in[place].sem, x_in[place].at(i, 0))
                for c in range(KC):
                    for t in range(TC):
                        last = nc.tensor.transpose(psX[:, place, c * TOK + t * P:c * TOK + (t + 1) * P],
                                                   xs[:, place, t, c * P:(c + 1) * P], idn[:, :])
                last.then_inc(xT_ps.sem, 1)

            def transpose_offsets(i, k):
                i, place = at_place(i, k)
                pe.wait_ge(w_in[place].sem, w_in[place].at(i, 0))
                pe.wait_ge(r2_done.sem, r2_done.at(i, place - 2))
                pe.sem_inc(passed, 1)
                nc.tensor.transpose(psY[:, place, 0:MC], o1_rows[:, place, :], idn[0:MC, 0:MC]).then_inc(o1_ps.sem, 1)

            def step(i, k, follow):
                pe.wait_ge(xT_sb.sem, xT_sb.at(i, k))
                pe.wait_ge(w1_rest.sem, w1_rest.at(i, NW * k + NW - 1))
                for m in range(MC):
                    if m % 2 == 0:
                        pe.wait_ge(h_sb.sem, h_sb.at(i, 4 * k + m // 2 - 4))
                    parts = [(c, w, x) for c in range(KC)
                             for w, x in ((w1_high, xT_high), (w1_high, xT_low), (w1_low, xT_high))]
                    for n, (c, w, x) in enumerate(parts):
                        last = nc.tensor.matmul(psH[:, m // 2, m % 2 * TOK:(m % 2 + 1) * TOK],
                                                w[:, k, c, m * P:(m + 1) * P], x[:, k, c, :],
                                                start=(n == 0), stop=(n == len(parts) - 1))
                    if m % 2:
                        last.then_inc(h_ps.sem, 1)
                if follow:
                    transpose_tile(i, k + 1)
                pe.wait_ge(w2_rest.sem, w2_rest.at(i, NW * k + NW - 1))
                parts = [(m, h_high, w) for m in range(MC) for w in (w2_high, w2_low)]
                parts += [(m, h_low, w2_high) for m in range(MC)]
                for t in range(TC):
                    for n, (m, rows, w) in enumerate(parts):
                        if t == 0 and n < 2 * MC and n % 4 == 0:
                            pe.wait_ge(h_split.sem, h_split.at(i, 4 * k + n // 4))
                        if t == 0 and n == 2 * MC:
                            pe.wait_ge(h_rest.sem, h_rest.at(i, 4 * k + 3))
                        last = nc.tensor.matmul(psY[:, k, t * D:(t + 1) * D], rows[:, m, t * P:(t + 1) * P],
                                                w[:, k, m, :], start=(n == 0), stop=(n == len(parts) - 1))
                last.then_inc(y_ps.sem, 1)
                if follow:
                    transpose_offsets(i, k + 1)

            transpose_tile(0, 0)
            transpose_offsets(0, 0)
            tiles(pe, step)
def shape_constants():
    import numpy as np

    inv_freq = 1.0 / np.float32(10000.0) ** (np.arange(0, HD, 2, dtype=np.float32) / np.float32(HD))
    angle = (np.arange(S, dtype=np.float32)[:, None] * inv_freq.astype(np.float32)[None, :]).astype(np.float32)
    cos, sin = np.cos(angle).astype(np.float32), np.sin(angle).astype(np.float32)
    scale = np.float32(HD ** -0.5)
    start = 2.0 ** (-2.0 ** (-(np.log2(H) - 3)))
    slopes = np.array([start * start ** i for i in range(H)], np.float32)
    high = (slopes.view(np.uint32) & np.uint32(0xFFFFF000)).view(np.float32)
    pos = np.arange(S, dtype=np.float32)
    return {
        "rope": np.stack([cos * scale, -sin * scale, sin * scale, cos, -sin, sin]),
        "slopes": slopes,
        "slope_parts": np.stack([high, slopes - high], 1),
        "key_rows": np.stack([np.ones_like(pos), pos, pos]),
        "before": np.triu(np.ones((P, P), np.float32), 1),
        "tile_starts": np.arange(TILES, dtype=np.float32) * TOK,
        "ident": np.eye(P, dtype=np.float32),
    }


_INS = ["L0_attn_x", "L0_attn_Wq", "L0_attn_Wk", "L0_attn_Wv", "L0_attn_Wo", "L0_ffn_Wq", "L0_ffn_bq", "L0_ffn_Wk",
        "L0_ffn_bk", "L0_ffn_Wv", "L0_ffn_bv", "L0_ffn_Wo", "L0_ffn_bo", "L0_ffn_router_w", "L0_ffn_router_b",
        "L0_ffn_W1", "L0_ffn_b1", "L0_ffn_W2", "L0_ffn_b2", "L0_ffn_ln1_g", "L0_ffn_ln1_b", "L0_ffn_ln2_g",
        "L0_ffn_ln2_b"]


def block_program(nc, ins, consts, out):
    x = ins["L0_attn_x"]
    w = {n[len("L0_ffn_"):]: ap for n, ap in ins.items() if n.startswith("L0_ffn_")}
    sorted_x = nc.dram_tensor("sorted_x", (TILES * TOK, D), F32, kind="Internal").ap()
    sorted_z = nc.dram_tensor("sorted_z", (TILES * TOK, D), F32, kind="Internal").ap()
    with ExitStack() as ctx:
        place = ctx.enter_context(nc.sbuf_tensor("place", [P, B * TT], I32))
        tile_expert = ctx.enter_context(nc.sbuf_tensor("tile_expert", [P, TILES], I32))
        with ExitStack() as routed:
            def sb(name, shape):
                return routed.enter_context(nc.sbuf_tensor(name, shape, F32))

            x1 = sb("x1", [P, B * TT, D])
            tri, starts, rw, rb = sb("tri", [P, P]), sb("starts", [P, TILES]), sb("rw", [P, D]), sb("rb", [P, 1])
            preloaded = routed.enter_context(nc.semaphore("preloaded"))
            preloads = [(tri[:, :], consts["before"]),
                        (starts[:, :], consts["tile_starts"].partition_broadcast(P)),
                        (rw[:, :], w["router_w"].rearrange("d a -> (d a)").partition_broadcast(P)),
                        (rb[:, :], w["router_b"].partition_broadcast(P))]
            plain_attention_phase(nc, x, w, consts["ident"], x1, sorted_x, preloads, preloaded)
            weights = ExpertWeights(nc, routed, w["W1"], w["b1"], w["W2"], w["b2"], tile_expert)
            routing_phase(nc, x1, tri, starts, rw, rb, preloaded, place, tile_expert, sorted_x, weights)
            experts_phase(nc, weights, w["ln2_g"], w["ln2_b"], consts["ident"], sorted_x, sorted_z)
        rotary_attention_phase(nc, x, *(ins["L0_attn_" + n] for n in ("Wq", "Wk", "Wv", "Wo")), consts["rope"],
                               consts["slopes"], consts["slope_parts"], consts["key_rows"], consts["ident"],
                               place, sorted_z, out)


def kernel(**inputs):
    import numpy as np
    import concourse.bacc as bacc
    from concourse.bass_utils import run_bass_kernel_spmd

    nc = bacc.Bacc("TRN2", target_bir_lowering=False, num_devices=1)
    arrays = {}

    def argument(name, a):
        a = np.ascontiguousarray(a)
        arrays[f"in_{name}"] = a
        return nc.dram_tensor(f"in_{name}", a.shape, mybir.dt.from_np(a.dtype), kind="ExternalInput").ap()

    ins = {name: argument(name, inputs[name]) for name in _INS}
    consts = {name: argument(name, a) for name, a in shape_constants().items()}
    out = nc.dram_tensor("out_0", (B, S, D), F32, kind="ExternalOutput").ap()
    block_program(nc, ins, consts, out)
    result = run_bass_kernel_spmd(nc, [arrays], core_ids=[0])
    return np.array(result.results[0]["out_0"])
```
